# Optimizing a Trainium2 kernel written in Bass

```python
import numpy as np
import jax
import jax.numpy as jnp

def _softmax(x, axis=-1):
    return jax.nn.softmax(x, axis=axis)

def _gelu(x):
    return jax.nn.gelu(x, approximate=True)

def _silu(x):
    return jax.nn.silu(x)

def _sigmoid(x):
    return jax.nn.sigmoid(x)

def _layernorm(x, axis=-1, eps=1e-05):
    m = jnp.mean(x, axis=axis, keepdims=True)
    v = jnp.var(x, axis=axis, keepdims=True)
    return (x - m) / jnp.sqrt(v + eps)

def _scatter_add(tgt, idx, src, axis=0):
    return tgt.at[idx].add(src)

def _segment_sum(src, seg, n):
    return jax.ops.segment_sum(src, seg, n)
kernel_name = 'mk_gnn_ffn_d2_gnn_r32_3b1503'

def setup_inputs(seed: int=0):
    np.random.seed(seed)
    _w = jnp.asarray

    def _rec_inputs():
        import jax
        import jax.numpy as jnp
        _gk = jax.random.key(seed)
        x = -0.0003713 + 1 * jax.random.normal(jax.random.fold_in(_gk, 1), (3125, 256), jnp.float32)
        _s = jax.random.randint(jax.random.fold_in(_gk, 2), (25000,), 0, 3125, jnp.int32)
        _d = jax.random.randint(jax.random.fold_in(_gk, 3), (25000,), 0, 3125, jnp.int32)
        _loop = jnp.arange(3125, dtype=jnp.int32)
        src = jnp.concatenate([_s, _d, _loop])
        dst = jnp.concatenate([_d, _s, _loop])
        _o = jnp.argsort(dst, stable=True)
        src = src[_o]
        dst = dst[_o]
        return (x, src, dst)
    x, src, dst = _rec_inputs()

    def _L0_gnn_setup():
        import jax, jax.numpy as jnp
        import numpy as np
        N = 50000
        E_RAND = 25000
        IN, HID, H, OUT = (256, 64, 4, 256)
        NEG_SLOPE = 0.2

        def gat_layer(h, W, a_src, a_dst, src, dst, concat):
            n = h.shape[0]
            nh, nf = a_src.shape
            hp = (h @ W.T).reshape(n, nh, nf)
            e = (hp[src] * a_src).sum(-1) + (hp[dst] * a_dst).sum(-1)
            e = jnp.where(e > 0, e, NEG_SLOPE * e)
            e_max = jax.ops.segment_max(e, dst, num_segments=n)
            ex = jnp.exp(e - e_max[dst])
            e_sum = jax.ops.segment_sum(ex, dst, num_segments=n)
            alpha = ex / (e_sum[dst] + 1e-16)
            out = jax.ops.segment_sum(hp[src] * alpha[..., None], dst, num_segments=n)
            return out.reshape(n, nh * nf) if concat else out.mean(axis=1)
        key = jax.random.key(seed)
        ks = jax.random.split(key, 8)
        x = jax.random.normal(ks[0], (N, IN), dtype=jnp.float32)
        er = jax.random.randint(ks[1], (2, E_RAND), 0, N, dtype=jnp.int32)
        loops = jnp.arange(N, dtype=jnp.int32)
        edge_index = jnp.concatenate([er, jnp.stack([loops, loops])], axis=1)
        W1 = jax.random.normal(ks[2], (H * HID, IN), jnp.float32) * (2.0 / (IN + H * HID)) ** 0.5
        a1_src = jax.random.normal(ks[3], (H, HID), jnp.float32) * 0.1
        a1_dst = jax.random.normal(ks[4], (H, HID), jnp.float32) * 0.1
        W2 = jax.random.normal(ks[5], (OUT, H * HID), jnp.float32) * (2.0 / (H * HID + OUT)) ** 0.5
        a2_src = jax.random.normal(ks[6], (1, OUT), jnp.float32) * 0.1
        a2_dst = jax.random.normal(ks[7], (1, OUT), jnp.float32) * 0.1
        return {'x': x, 'edge_index': edge_index, 'W1': W1, 'a1_src': a1_src, 'a1_dst': a1_dst, 'W2': W2, 'a2_src': a2_src, 'a2_dst': a2_dst}
    _L0_gnn_all = _L0_gnn_setup()
    _L0_gnn_in = {k: v for k, v in _L0_gnn_all.items() if k in ('W1', 'a1_src', 'a1_dst', 'W2', 'a2_src', 'a2_dst')}
    del _L0_gnn_all

    def _L0_ffn_setup():
        import jax, jax.numpy as jnp
        import numpy as np
        B, S, H, F, E, K = (8, 128, 256, 512, 16, 2)
        EPS = 1e-05
        key = jax.random.key(seed)
        ks = jax.random.split(key, 9)
        sc = 0.02
        return {'x': jax.random.normal(ks[0], (B, S, H), dtype=jnp.float32), 'gate_w': jax.random.normal(ks[1], (H, E), dtype=jnp.float32) * sc, 'gate_b': jnp.zeros((E,), dtype=jnp.float32), 'w1': jax.random.normal(ks[2], (E, H, F), dtype=jnp.float32) * sc, 'b1': jnp.zeros((E, F), dtype=jnp.float32), 'w2': jax.random.normal(ks[3], (E, F, H), dtype=jnp.float32) * sc, 'b2': jnp.zeros((E, H), dtype=jnp.float32), 'gamma': jnp.ones((H,), dtype=jnp.float32), 'beta': jnp.zeros((H,), dtype=jnp.float32)}
    _L0_ffn_all = _L0_ffn_setup()
    _L0_ffn_in = {k: v for k, v in _L0_ffn_all.items() if k in ('gate_w', 'gate_b', 'w1', 'b1', 'w2', 'b2', 'gamma', 'beta')}
    del _L0_ffn_all

    def _L1_gnn_setup():
        import jax, jax.numpy as jnp
        import numpy as np
        N = 50000
        E = 25000
        DIM = 256
        H = 8
        DH = DIM // H
        SCALE = DH ** (-0.5)
        key = jax.random.key(seed)
        ks = jax.random.split(key, 7)
        h = jax.random.normal(ks[0], (N, DIM), dtype=jnp.float32)
        src = jax.random.randint(ks[1], (E,), 0, N, dtype=jnp.int32)
        dst = jax.random.randint(ks[2], (E,), 0, N, dtype=jnp.int32)
        W_qkv = jax.random.normal(ks[3], (DIM, 3 * DIM), dtype=jnp.float32) * DIM ** (-0.5)
        b_qkv = jnp.zeros((3 * DIM,), dtype=jnp.float32)
        W_out = jax.random.normal(ks[4], (DIM, DIM), dtype=jnp.float32) * DIM ** (-0.5)
        b_out = jnp.zeros((DIM,), dtype=jnp.float32)
        return {'h': h, 'src': src, 'dst': dst, 'W_qkv': W_qkv, 'b_qkv': b_qkv, 'W_out': W_out, 'b_out': b_out}
    _L1_gnn_all = _L1_gnn_setup()
    _L1_gnn_in = {k: v for k, v in _L1_gnn_all.items() if k in ('W_qkv', 'b_qkv', 'W_out', 'b_out')}
    del _L1_gnn_all

    def _L1_ffn_setup():
        import jax, jax.numpy as jnp
        import numpy as np
        TOP_K = 2
        LN_EPS = 1e-05
        key = jax.random.key(seed)
        ks = jax.random.split(key, 8)
        B, S, D, E, H = (16, 1024, 256, 8, 1024)
        x = jax.random.normal(ks[0], (B, S, D), dtype=jnp.float32)
        Wr = jax.random.normal(ks[1], (D, E), dtype=jnp.float32) * 0.1
        br = jnp.zeros((E,), dtype=jnp.float32)
        ln_g = jnp.ones((E, D), dtype=jnp.float32)
        ln_b = jnp.zeros((E, D), dtype=jnp.float32)
        W1 = jax.random.normal(ks[2], (E, D, H), dtype=jnp.float32) * (1.0 / np.sqrt(D))
        b1 = jnp.zeros((E, H), dtype=jnp.float32)
        W2 = jax.random.normal(ks[3], (E, H, D), dtype=jnp.float32) * (1.0 / np.sqrt(H))
        b2 = jnp.zeros((E, D), dtype=jnp.float32)
        return {'x': x, 'Wr': Wr, 'br': br, 'ln_g': ln_g, 'ln_b': ln_b, 'W1': W1, 'b1': b1, 'W2': W2, 'b2': b2}
    _L1_ffn_all = _L1_ffn_setup()
    _L1_ffn_in = {k: v for k, v in _L1_ffn_all.items() if k in ('Wr', 'br', 'ln_g', 'ln_b', 'W1', 'b1', 'W2', 'b2')}
    del _L1_ffn_all
    return {'x': x, 'src': src, 'dst': dst, 'L0_gnn_W1': _L0_gnn_in['W1'], 'L0_gnn_a1_src': _L0_gnn_in['a1_src'], 'L0_gnn_a1_dst': _L0_gnn_in['a1_dst'], 'L0_gnn_W2': _L0_gnn_in['W2'], 'L0_gnn_a2_src': _L0_gnn_in['a2_src'], 'L0_gnn_a2_dst': _L0_gnn_in['a2_dst'], 'L0_ffn_gate_w': _L0_ffn_in['gate_w'], 'L0_ffn_gate_b': _L0_ffn_in['gate_b'], 'L0_ffn_w1': _L0_ffn_in['w1'], 'L0_ffn_b1': _L0_ffn_in['b1'], 'L0_ffn_w2': _L0_ffn_in['w2'], 'L0_ffn_b2': _L0_ffn_in['b2'], 'L0_ffn_gamma': _L0_ffn_in['gamma'], 'L0_ffn_beta': _L0_ffn_in['beta'], 'L1_gnn_W_qkv': _L1_gnn_in['W_qkv'], 'L1_gnn_b_qkv': _L1_gnn_in['b_qkv'], 'L1_gnn_W_out': _L1_gnn_in['W_out'], 'L1_gnn_b_out': _L1_gnn_in['b_out'], 'L1_ffn_Wr': _L1_ffn_in['Wr'], 'L1_ffn_br': _L1_ffn_in['br'], 'L1_ffn_ln_g': _L1_ffn_in['ln_g'], 'L1_ffn_ln_b': _L1_ffn_in['ln_b'], 'L1_ffn_W1': _L1_ffn_in['W1'], 'L1_ffn_b1': _L1_ffn_in['b1'], 'L1_ffn_W2': _L1_ffn_in['W2'], 'L1_ffn_b2': _L1_ffn_in['b2']}

def reference(x, src, dst, L0_gnn_W1, L0_gnn_a1_src, L0_gnn_a1_dst, L0_gnn_W2, L0_gnn_a2_src, L0_gnn_a2_dst, L0_ffn_gate_w, L0_ffn_gate_b, L0_ffn_w1, L0_ffn_b1, L0_ffn_w2, L0_ffn_b2, L0_ffn_gamma, L0_ffn_beta, L1_gnn_W_qkv, L1_gnn_b_qkv, L1_gnn_W_out, L1_gnn_b_out, L1_ffn_Wr, L1_ffn_br, L1_ffn_ln_g, L1_ffn_ln_b, L1_ffn_W1, L1_ffn_b1, L1_ffn_W2, L1_ffn_b2):
    import jax
    import jax.numpy as jnp

    def _L0_gnn_ref(x, edge_index, W1, a1_src, a1_dst, W2, a2_src, a2_dst):
        import jax, jax.numpy as jnp
        import numpy as np
        N = 50000
        E_RAND = 25000
        IN, HID, H, OUT = (256, 64, 4, 256)
        NEG_SLOPE = 0.2

        def gat_layer(h, W, a_src, a_dst, src, dst, concat):
            n = h.shape[0]
            nh, nf = a_src.shape
            hp = (h @ W.T).reshape(n, nh, nf)
            e = (hp[src] * a_src).sum(-1) + (hp[dst] * a_dst).sum(-1)
            e = jnp.where(e > 0, e, NEG_SLOPE * e)
            e_max = jax.ops.segment_max(e, dst, num_segments=n)
            ex = jnp.exp(e - e_max[dst])
            e_sum = jax.ops.segment_sum(ex, dst, num_segments=n)
            alpha = ex / (e_sum[dst] + 1e-16)
            out = jax.ops.segment_sum(hp[src] * alpha[..., None], dst, num_segments=n)
            return out.reshape(n, nh * nf) if concat else out.mean(axis=1)
        src, dst = (edge_index[0], edge_index[1])
        h = jax.nn.relu(gat_layer(x, W1, a1_src, a1_dst, src, dst, True))
        return gat_layer(h, W2, a2_src, a2_dst, src, dst, False)

    def _L0_ffn_ref(x, gate_w, gate_b, w1, b1, w2, b2, gamma, beta):
        import jax, jax.numpy as jnp
        import numpy as np
        B, S, H, F, E, K = (8, 128, 256, 512, 16, 2)
        EPS = 1e-05
        gate_logits = x @ gate_w + gate_b
        topk_vals, topk_idx = jax.lax.top_k(gate_logits, K)
        topk_w = jax.nn.softmax(topk_vals, axis=-1)
        h = jax.nn.relu(jnp.einsum('bsh,ehf->bsef', x, w1) + b1)
        expert_out = jnp.einsum('bsef,efh->bseh', h, w2) + b2
        sel = jnp.take_along_axis(expert_out, topk_idx[:, :, :, None], axis=2)
        moe = jnp.sum(topk_w[..., None] * sel, axis=2)
        y = x + moe
        mu = jnp.mean(y, axis=-1, keepdims=True)
        var = jnp.var(y, axis=-1, keepdims=True)
        return (y - mu) / jnp.sqrt(var + EPS) * gamma + beta

    def _L1_gnn_ref(h, src, dst, W_qkv, b_qkv, W_out, b_out):
        import jax, jax.numpy as jnp
        import numpy as np
        N = 50000
        E = 25000
        DIM = 256
        H = 8
        DH = DIM // H
        SCALE = DH ** (-0.5)
        n = h.shape[0]
        qkv = (h @ W_qkv + b_qkv).reshape(n, 3, H, DH)
        q, k, v = (qkv[:, 0], qkv[:, 1], qkv[:, 2])
        score = jnp.einsum('ehd,ehd->eh', q[dst], k[src]) * SCALE
        mx = jax.ops.segment_max(score, dst, num_segments=n)
        ex = jnp.exp(score - mx[dst])
        denom = jax.ops.segment_sum(ex, dst, num_segments=n)
        attn = ex / denom[dst]
        msg = attn[:, :, None] * v[src]
        h_new = jax.ops.segment_sum(msg, dst, num_segments=n)
        h_out = jnp.transpose(h_new, (0, 2, 1)).reshape(n, DIM)
        return (h_out + h) @ W_out + b_out

    def _L1_ffn_ref(x, Wr, br, ln_g, ln_b, W1, b1, W2, b2):
        import jax, jax.numpy as jnp
        import numpy as np
        TOP_K = 2
        LN_EPS = 1e-05
        B, S, D = x.shape
        N = B * S
        xt = x.reshape(N, D)
        logits = xt @ Wr + br
        probs = jax.nn.softmax(logits, axis=-1)
        top_p, top_idx = jax.lax.top_k(probs, TOP_K)
        weights = top_p / top_p.sum(axis=-1, keepdims=True)
        mu = xt.mean(axis=-1, keepdims=True)
        var = ((xt - mu) ** 2).mean(axis=-1, keepdims=True)
        xn = (xt - mu) * jax.lax.rsqrt(var + LN_EPS)
        xe = xn[None, :, :] * ln_g[:, None, :] + ln_b[:, None, :]
        h = jax.nn.gelu(jnp.einsum('end,edh->enh', xe, W1) + b1[:, None, :], approximate=False)
        y = jnp.einsum('enh,ehd->end', h, W2) + b2[:, None, :]
        y_tok = jnp.transpose(y, (1, 0, 2))
        sel = jnp.take_along_axis(y_tok, top_idx[:, :, None], axis=1)
        out = (weights[:, :, None] * sel).sum(axis=1)
        return out.reshape(B, S, D)
    edge_index = jnp.stack([src, dst])
    x = x + _L0_gnn_ref(_layernorm(x, axis=-1), edge_index, L0_gnn_W1, L0_gnn_a1_src, L0_gnn_a1_dst, L0_gnn_W2, L0_gnn_a2_src, L0_gnn_a2_dst)
    x = x + _L0_ffn_ref(_layernorm(x, axis=-1)[None], L0_ffn_gate_w, L0_ffn_gate_b, L0_ffn_w1, L0_ffn_b1, L0_ffn_w2, L0_ffn_b2, L0_ffn_gamma, L0_ffn_beta)[0]
    x = x + _L1_gnn_ref(_layernorm(x, axis=-1), src, dst, L1_gnn_W_qkv, L1_gnn_b_qkv, L1_gnn_W_out, L1_gnn_b_out)
    x = x + _L1_ffn_ref(_layernorm(x, axis=-1)[None], L1_ffn_Wr, L1_ffn_br, L1_ffn_ln_g, L1_ffn_ln_b, L1_ffn_W1, L1_ffn_b1, L1_ffn_W2, L1_ffn_b2)[0]
    return x

_drawn_inputs = setup_inputs


def setup_inputs(seed=0):
    import zlib

    import numpy as np

    out = dict(_drawn_inputs(seed))
    spreads = {'L0_ffn_gate_b': (0.0, 0.1),
     'L0_ffn_b1': (0.0, 0.385),
     'L0_ffn_b2': (0.0, 0.1),
     'L0_ffn_gamma': (1.0, 0.2),
     'L0_ffn_beta': (0.0, 0.1),
     'L1_gnn_b_qkv': (0.0, 0.1),
     'L1_gnn_b_out': (0.0, 0.1),
     'L1_ffn_br': (0.0, 0.1),
     'L1_ffn_ln_g': (1.0, 0.2),
     'L1_ffn_ln_b': (0.0, 0.339),
     'L1_ffn_b1': (0.0, 0.352),
     'L1_ffn_b2': (0.0, 0.1)}
    factors = {'L0_gnn_a1_dst': 3.319, 'L0_gnn_a2_src': 7.377, 'L0_gnn_a2_dst': 7.522}
    for name, (base, spread) in spreads.items():
        noise = np.random.default_rng([zlib.crc32(name.encode()), seed]).standard_normal(out[name].shape)
        drawn = base * np.exp(spread * noise) if base else spread * noise
        out[name] = jnp.asarray(drawn.astype(out[name].dtype))
    for name, factor in factors.items():
        out[name] = (out[name] * factor).astype(out[name].dtype)
    return out
```

```python
from contextlib import ExitStack, contextmanager

import numpy as np

import concourse.bass as bass
from concourse import mybir

F32 = mybir.dt.float32
I32 = mybir.dt.int32
ALU = mybir.AluOpType
ACT = mybir.ActivationFunctionType
AX = mybir.AxisListType.X

N, D, E = 3125, 256, 53125
W = 125
NW = N // W
NV = NW + 1
NT = E // W
G = 10
NB = 46
NP = NB * G
PC = 4
PQ = NP // PC
HEAD = W
FAR = -3.0e38
MAGIC = 12582912.0
EPS = 1e-5
KC = D // 128
assert NP >= NT + NW - 1 and NB % 2 == 0 and NP % PC == 0 and NV % 2 == 0

FFN = [dict(E=16, F=512), dict(E=8, F=1024)]
for _f in FFN:
    _f["NBLK"] = (2 * N - _f["E"]) // 128 + _f["E"]
    _f["FC"] = _f["F"] // 128
    _f["ob"] = KC * _f["F"]
    _f["og"] = _f["ob"] + _f["FC"]
    _f["PK"] = _f["og"] + 2 * KC
SLOTS = 128 * max(f["NBLK"] for f in FFN)
ATT = [dict(H=4, ROW=260), dict(H=1, ROW=257), dict(H=8, ROW=512)]


def build(nc, t):
    with ExitStack() as top:
        def sb(name, shape, dt=F32, stack=top):
            return stack.enter_context(nc.sbuf_tensor(name, shape, dt))

        sems = [[]]

        def sem(name):
            sems[-1].append(nc.alloc_semaphore(name=name))
            return sems[-1][-1]

        def gather_sem(name):
            return top.enter_context(nc.semaphore(name))

        @contextmanager
        def phase():
            sems.append([])
            with ExitStack() as ph:
                yield ph
            mine = sems.pop()
            if mine:
                with nc.Block() as clear:
                    @clear.gpsimd
                    def _(pool):
                        for s in mine:
                            pool.sem_clear(s)
            for s in mine:
                nc.release_semaphore(s)

        v, a, g = nc.vector, nc.scalar, nc.gpsimd

        gate_tab = nc.dram_tensor("gate_tab", (NP, W + 1), F32).ap()
        code_tab = nc.dram_tensor("code_tab", (NP, W), F32).ap()
        srcs_tab = nc.dram_tensor("srcs_tab", (NB, W, G), I32).ap()
        row_tab = [nc.dram_tensor(f"row_tab{l}", (NV * W, ATT[l]["ROW"]), F32).ap() for l in range(3)]
        head_tab = [nc.dram_tensor(f"head_tab{l}", (NP, D + 2 * ATT[l]["H"]), F32).ap() for l in range(3)]
        xs_tab = nc.dram_tensor("xs_tab", (SLOTS, D), F32).ap()
        ys_tab = nc.dram_tensor("ys_tab", (SLOTS, D), F32).ap()

        xcur = sb("xcur", [W, NV, D])
        z = sb("z", [W, NV, D])
        ident = sb("ident", [128, 128])
        ones = sb("ones", [128, 128])
        iota_row = sb("iota_row", [128, 128])
        iota_col = sb("iota_col", [128, 1])
        mcode = sb("mcode", [W, NP])
        first = sb("first", [W, NP])
        wtab = sb("wtab", [1, NP], I32)
        hdst = sb("hdst", [PQ, PC])
        hfirst = sb("hfirst", [PQ, PC])
        hgate = sb("hgate", [8, NP + 1])
        stats = sb("stats", [W, NV, 6])
        mean = sb("mean", [W, NV])
        rstd = sb("rstd", [W, NV])
        lt = [sb(f"lt{k}", [W, NV]) for k in range(3)]
        dwin = sb("dwin", [W, NV, 4])

        def vd(_):
            v.drain()

        def mm(*args, **kw):
            return nc.tensor.matmul(*args, **kw)

        with phase() as ph:
            def ps(name, shape):
                return ph.enter_context(nc.psum_tensor(name, shape, F32))

            ends_i = sb("ends_i", [1, 2, NT], I32, ph)
            ends = sb("ends", [1, 2, NT], F32, ph)
            low = sb("low", [1, 2, NT], F32, ph)
            span = sb("span", [1, NT], F32, ph)
            zrow = sb("zrow", [1, NT], F32, ph)
            stair = sb("stair", [1, 2, NT], F32, ph)
            tnum = sb("tnum", [1, NT], F32, ph)
            bnum = sb("bnum", [PQ, PC], F32, ph)
            mask = sb("mask", [PQ, NT], F32, ph)
            tmpn = sb("tmpn", [PQ, NT], F32, ph)
            cnt = sb("cnt", [PQ, PC], F32, ph)
            bfirst = sb("bfirst", [PQ, PC], F32, ph)
            wlow = sb("wlow", [PQ, PC], F32, ph)
            wb = sb("wb", [PQ, PC], F32, ph)
            w125 = sb("w125", [PQ, PC], F32, ph)
            tb_i = sb("tb_i", [PQ, PC], I32, ph)
            er_i = sb("er_i", [PQ, PC, 256], I32, ph)
            er = sb("er", [PQ, PC, 256], F32, ph)
            gate = sb("gate", [PQ, PC, W + 1], F32, ph)
            st = sb("st", [PQ, PC, W], F32, ph)
            hd = sb("hd", [PQ, PC, W], F32, ph)
            dl = sb("dl", [PQ, PC, W], F32, ph)
            inw = sb("inw", [PQ, PC, W], F32, ph)
            dco = sb("dco", [PQ, PC, W], F32, ph)
            mco = sb("mco", [PQ, PC, W], F32, ph)
            u = sb("u", [PQ, PC, W], F32, ph)
            hv = sb("hv", [PQ, PC], F32, ph)
            hrow = sb("hrow", [8, NP + 1], F32, ph)
            hr2 = sb("hr2", [8, NP + 1], F32, ph)
            srcp = sb("srcp", [W, NP], I32, ph)
            zero = sb("zero", [128, 4096], F32, ph)
            p_b = ps("p_b", [PQ, 2, 512])
            p_t = [ps(f"p_t{k}", [W, 512]) for k in range(3)]
            p_w = ps("p_w", [1, 512])
            p_h = ps("p_h", [8, 512])
            s_in = sem("a_in")
            s_const = sem("a_const")
            s_stair = sem("a_stair")
            s_bc = sem("a_bc")
            s_tb = sem("a_tb")
            s_er = gather_sem("a_er")
            s_rows = sem("a_rows")
            s_tr = sem("a_tr")
            s_trd = sem("a_trd")
            s_cols = sem("a_cols")
            s_out = sem("a_out")
            s_hf = sem("a_hf")
            s_zero = sem("a_zero")
            block = ph.enter_context(nc.Block())

            @block.sync
            def _(sp):
                for k in range(2):
                    sp.dma_start(ends_i[0:1, k, :], t["ends"][k:k + 1, :]).then_inc(s_in, 16)
                sp.dma_start(xcur[:, 0:NW, :], t["x"].rearrange("(w p) d -> p w d", p=W)).then_inc(s_in, 16)
                sp.wait_ge(s_zero, 1)
                for k in range(SLOTS * D // (128 * 4096)):
                    sp.dma_start(xs_tab.rearrange("(k p r) d -> k p (r d)", p=128, r=4096 // D)[k],
                                 zero[:]).then_inc(s_out, 16)
                sp.wait_ge(s_rows, 1)
                sp.dma_start(gate_tab.rearrange("(c p) e -> p c e", p=PQ), gate[:]).then_inc(s_out, 16)
                sp.dma_start(code_tab.rearrange("(c p) e -> p c e", p=PQ), dco[:]).then_inc(s_out, 16)
                sp.wait_ge(s_cols, 1)
                sp.dma_start(srcs_tab.rearrange("n p g -> p n g"),
                             srcp[:].rearrange("p (n g) -> p n g", g=G)).then_inc(s_out, 16)
                sp.wait_ge(s_out, 16 * (3 + SLOTS * D // (128 * 4096)))

            @block.gpsimd
            def _(pool):
                g.memset(ones[:], 1.0).then_inc(s_const, 1)
                pool.wait_ge(s_const, 1)
                g.affine_select(out=ident[:], in_=ones[:], compare_op=ALU.is_equal, fill=0.0, base=0,
                                pattern=[[-1, 128]], channel_multiplier=1).then_inc(s_const, 1)
                g.iota(iota_row[:], pattern=[[1, 128]], base=0, channel_multiplier=0,
                       allow_small_or_imprecise_dtypes=True).then_inc(s_const, 1)
                g.iota(iota_col[:], pattern=[[1, 1]], base=0, channel_multiplier=1,
                       allow_small_or_imprecise_dtypes=True).then_inc(s_const, 1)
                g.iota(tnum[:], pattern=[[1, NT]], base=0, channel_multiplier=0,
                       allow_small_or_imprecise_dtypes=True).then_inc(s_const, 1)
                g.iota(bnum[:], pattern=[[PQ, PC]], base=0, channel_multiplier=1,
                       allow_small_or_imprecise_dtypes=True).then_inc(s_const, 1)
                pool.wait_ge(s_tb, 1)
                for c in range(PC):
                    g.indirect_dma_start(out=er_i[:, c, :], out_offset=None, in_=t["edges"],
                                         in_offset=bass.IndirectOffsetOnAxis(ap=tb_i[:, c:c + 1], axis=0)
                                         ).then_inc(s_er, 16)
                pool.wait_ge(s_er, 16 * PC)

            @block.tensor
            def _(pe):
                pe.wait_ge(s_const, 6)
                pe.wait_ge(s_stair, 1)
                for k in range(2):
                    last = mm(p_b[:, k, 0:NT], ones[0:1, 0:PQ], stair[0:1, k, :], start=True, stop=True)
                last.then_inc(s_bc, 1)
                pe.wait_ge(s_rows, 1)
                for c in range(PC):
                    for k, (out, src) in enumerate(((p_t[0], mco[:, c, :]), (p_t[1], st[:, c, :]),
                                                    (p_t[2], er[:, c, W + 2:2 * W + 2]))):
                        nc.tensor.transpose(out[:, c * PQ:(c + 1) * PQ], src, ident[0:PQ, 0:PQ])
                    nc.tensor.transpose(p_w[:, c * PQ:(c + 1) * PQ], wb[:, c:c + 1], ident[0:PQ, 0:PQ])
                    last = mm(p_h[:, c * PQ:(c + 1) * PQ], hdst[:, c:c + 1].to_broadcast([PQ, 8]),
                              ident[0:PQ, 0:PQ], start=True, stop=True)
                last.then_inc(s_tr, 1)
                pe.wait_ge(s_hf, 1)
                for c in range(PC):
                    last = nc.tensor.transpose(p_b[:, 0, c:c + 1], hr2[0:1, c * PQ:(c + 1) * PQ],
                                               ident[0:1, 0:1])
                last.then_inc(s_trd, 1)

            @block.vector
            def _(dve):
                v.memset(zero[:], 0.0)
                v.drain().then_inc(s_zero, 1)
                v.memset(xcur[:, NW, :], 0.0)
                vd(v.memset(zrow[:], 0.0))
                dve.wait_ge(s_in, 48)
                dve.wait_ge(s_const, 6)
                vd(v.tensor_copy(ends[:], ends_i[:]))
                vd(v.tensor_scalar(low[:], ends[:], -(W // 2) * 1.0, 1.0 / W, ALU.add, ALU.mult))
                vd(v.tensor_scalar(ends[:], low[:], MAGIC, None, ALU.add))
                vd(v.tensor_scalar(low[:], ends[:], MAGIC, None, ALU.subtract))
                vd(v.tensor_tensor(span[:], low[0:1, 1, :], low[0:1, 0, :], ALU.subtract))
                vd(v.tensor_tensor_scan(out=stair[0:1, 0, :], data0=span[:], data1=zrow[:], initial=0.0,
                                        op0=ALU.add, op1=ALU.add))
                vd(v.tensor_tensor(stair[0:1, 0, :], stair[0:1, 0, :], span[:], ALU.subtract))
                vd(v.tensor_tensor(stair[0:1, 0, :], stair[0:1, 0, :], tnum[:], ALU.add))
                v.tensor_copy(stair[0:1, 1, :], low[0:1, 0, :])
                v.drain().then_inc(s_stair, 1)
                dve.wait_ge(s_bc, 1)
                for c in range(PC):
                    vd(v.tensor_scalar(mask[:], p_b[:, 0, 0:NT], bnum[:, c:c + 1], None, ALU.is_le))
                    v.tensor_reduce(cnt[:, c:c + 1], mask[:], AX, ALU.add)
                    vd(v.tensor_tensor(tmpn[:], mask[:], p_b[:, 0, 0:NT], ALU.mult))
                    vd(v.tensor_reduce(bfirst[:, c:c + 1], tmpn[:], AX, ALU.max))
                    vd(v.tensor_tensor(tmpn[:], mask[:], p_b[:, 1, 0:NT], ALU.mult))
                    vd(v.tensor_reduce(wlow[:, c:c + 1], tmpn[:], AX, ALU.max))
                v.tensor_scalar(tb_i[:], cnt[:], -1.0, None, ALU.add)
                v.drain().then_inc(s_tb, 1)
                vd(v.tensor_tensor(wb[:], wlow[:], bnum[:], ALU.add))
                vd(v.tensor_tensor(wb[:], wb[:], bfirst[:], ALU.subtract))
                vd(v.tensor_scalar(wb[:], wb[:], float(NW), None, ALU.min))
                vd(v.tensor_scalar(w125[:], wb[:], float(W), None, ALU.mult))
                dve.wait_ge(s_er, 16 * PC)
                vd(v.tensor_copy(er[:], er_i[:]))
                v.memset(gate[:], FAR)
                dst = er[:, :, 1:W + 1]
                vd(v.tensor_tensor(st[:], dst, er[:, :, 0:W], ALU.not_equal))
                vd(v.tensor_scalar(gate[:, :, 0:W], st[:], FAR, None, ALU.mult))
                v.memset(st[:, :, 0:1], 1.0)
                vd(v.tensor_tensor(hd[:], dst, er[:, :, 0:1].to_broadcast([PQ, PC, W]), ALU.is_equal))
                vd(v.tensor_tensor(dl[:], dst, w125[:].unsqueeze(2).to_broadcast([PQ, PC, W]), ALU.subtract))
                vd(v.tensor_scalar(u[:], dl[:], 0.0, None, ALU.is_ge))
                vd(v.tensor_scalar(inw[:], dl[:], W - 1.0, None, ALU.is_le))
                vd(v.tensor_tensor(inw[:], inw[:], u[:], ALU.mult))
                vd(v.tensor_scalar(dco[:], dl[:], 1.0, None, ALU.add))
                vd(v.tensor_tensor(dco[:], dco[:], inw[:], ALU.mult))
                vd(v.tensor_scalar(dco[:], dco[:], -1.0, None, ALU.add))
                vd(v.tensor_scalar(u[:], dl[:], -1.0, float(HEAD), ALU.mult, ALU.add))
                vd(v.tensor_tensor(u[:], u[:], hd[:], ALU.mult))
                vd(v.tensor_tensor(u[:], u[:], inw[:], ALU.mult))
                vd(v.tensor_tensor(mco[:], dco[:], u[:], ALU.add))
                vd(v.tensor_tensor(hv[:], hd[:, :, 0], inw[:, :, 0], ALU.mult))
                vd(v.tensor_scalar(hdst[:], er[:, :, 0], 1.0, None, ALU.add))
                vd(v.tensor_tensor(hdst[:], hdst[:], hv[:], ALU.mult))
                v.tensor_scalar(hdst[:], hdst[:], -1.0, None, ALU.add)
                v.drain().then_inc(s_rows, 1)
                v.memset(hrow[:], -2.0)
                vd(v.memset(hr2[:], 1.0))
                dve.wait_ge(s_tr, 1)
                v.tensor_copy(mcode[:], p_t[0][:, 0:NP])
                v.tensor_copy(first[:], p_t[1][:, 0:NP])
                v.tensor_copy(srcp[:], p_t[2][:, 0:NP])
                v.tensor_copy(wtab[:], p_w[:, 0:NP])
                v.tensor_copy(hrow[:, 1:NP + 1], p_h[:, 0:NP])
                v.drain().then_inc(s_cols, 1)
                vd(v.tensor_tensor(hr2[:, 0:NP], hrow[:, 1:NP + 1], hrow[:, 0:NP], ALU.not_equal))
                v.tensor_scalar(hgate[:], hr2[:], FAR, None, ALU.mult)
                v.drain().then_inc(s_hf, 1)
                dve.wait_ge(s_trd, 1)
                v.tensor_copy(hfirst[:], p_b[:, 0, 0:PC])

        def norm_stats(dve, src, s_var, s_std):
            with dve.Fori(0, NV) as w:
                v.bn_stats(stats[:, bass.ds(w, 1), :].rearrange("p a b -> p (a b)"),
                           src[:, bass.ds(w, 1), :].rearrange("p a b -> p (a b)"))
            v.drain()
            v.tensor_tensor(mean[:], stats[:, :, 1], stats[:, :, 4], ALU.add)
            v.tensor_tensor(lt[0][:], stats[:, :, 1], stats[:, :, 4], ALU.subtract)
            vd(v.tensor_tensor(lt[1][:], stats[:, :, 2], stats[:, :, 5], ALU.add))
            v.tensor_scalar(mean[:], mean[:], 0.5, None, ALU.mult)
            vd(v.tensor_scalar(lt[2][:], lt[0][:], 0.25, None, ALU.mult))
            vd(v.tensor_tensor(lt[0][:], lt[0][:], lt[2][:], ALU.mult))
            vd(v.tensor_scalar(lt[1][:], lt[1][:], 1.0 / D, EPS, ALU.mult, ALU.add))
            v.tensor_tensor(lt[0][:], lt[0][:], lt[1][:], ALU.add)
            v.drain().then_inc(s_var, 1)
            dve.wait_ge(s_std, 1)
            vd(v.reciprocal(rstd[:], lt[2][:]))

        def norm_apply(dve, src, dst):
            with dve.Fori(0, NV) as w:
                v.tensor_scalar(dst[:, bass.ds(w, 1), :].rearrange("p a b -> p (a b)"),
                                src[:, bass.ds(w, 1), :].rearrange("p a b -> p (a b)"),
                                mean[:, bass.ds(w, 1)], rstd[:, bass.ds(w, 1)],
                                ALU.subtract, ALU.mult)
            v.drain()

        def norm_sqrt(act, s_var, s_std):
            act.wait_ge(s_var, 1)
            a.activation(lt[2][:], lt[0][:], ACT.Sqrt).then_inc(s_std, 1)

        def sem2(name):
            return [sem(f"{name}{k}") for k in range(2)]

        def project(name, src, cols, loads, wt, emit, norm=False, dve_first=None, pe_first=None,
                    rows=None, row_dram=None, frees=None):
            nb = (cols + 511) // 512
            with phase() as ph:
                slot = sb(name + "slot", [W, 2, D], F32, ph)
                tr = sb(name + "tr", [128, 2, KC, 128], F32, ph)
                p_tr = [ph.enter_context(nc.psum_tensor(f"{name}p_tr{k}", [128, 512], F32)) for k in range(2)]
                p_o = [ph.enter_context(nc.psum_tensor(f"{name}p_o{k}", [128, 512 * nb], F32)) for k in range(2)]
                s_load, s_wts, s_var, s_std = sem(name + "load"), sem(name + "wts"), sem(name + "var"), sem(name + "std")
                s_slot = sem(name + "slot")
                s_turn = sem(name + "turn")
                s_feat = sem(name + "feat")
                s_prod = sem(name + "prod")
                s_emit = sem(name + "emit")
                s_row = sem2(name + "row")
                block = ph.enter_context(nc.Block())

                @block.sync
                def _(sp):
                    for dst, dram in loads:
                        sp.dma_start(dst, dram, allow_slow_non_contiguous=True).then_inc(s_load, 16)
                    if rows is not None:
                        for k in range(2):
                            sp.sem_inc(s_row[k], 16)
                        with sp.Fori(0, NV // 2) as i:
                            for k in range(2):
                                sp.wait_ge(s_emit, i * 2 + k + 3)
                                sp.dma_start(row_dram[bass.ds(i * (2 * W) + k * W, W), :],
                                             rows[k][:]).then_inc(s_row[k], 16)
                        for k in range(2):
                            sp.wait_ge(s_row[k], 16 * (NV // 2 + 1))
                    sp.wait_ge(s_load, 16 * len(loads))

                @block.scalar
                def _(act):
                    act.sem_inc(s_feat, 2)
                    if norm:
                        norm_sqrt(act, s_var, s_std)
                    with act.Fori(0, NV // 2) as i:
                        for k in range(2):
                            act.wait_ge(s_turn, i * 2 + k + 3)
                            act.wait_ge(s_prod, i * 2 + k + 1)
                            a.activation(tr[:, k, :, 0:W],
                                         p_tr[k][:, 0:256].rearrange("p (c w) -> p c w", c=KC)[:, :, 0:W],
                                         ACT.Copy).then_inc(s_feat, 1)

                @block.vector
                def _(dve):
                    dve.sem_inc(s_emit, 2)
                    if dve_first is not None:
                        dve_first(dve, s_load, s_wts, frees)
                    if norm:
                        norm_stats(dve, xcur, s_var, s_std)
                        norm_apply(dve, xcur, z)

                    def fill(j, k):
                        dve.wait_ge(s_turn, j + 1)
                        v.tensor_copy(slot[:, k, :], src[:, bass.ds(j, 1), :].rearrange("p a b -> p (a b)")
                                      ).then_inc(s_slot, 1)

                    def take(j, k):
                        if rows is not None:
                            dve.wait_ge(s_row[k], j * 8 + (16 - 8 * k))
                        dve.wait_ge(s_prod, j + 3)
                        emit(j, k, p_o[k]).then_inc(s_emit, 1)

                    fill(0, 0)
                    fill(1, 1)
                    with dve.Fori(0, NV // 2 - 1) as i:
                        for k in range(2):
                            fill(i * 2 + k + 2, k)
                            take(i * 2 + k, k)
                    take(NV - 2, 0)
                    take(NV - 1, 1)

                @block.tensor
                def _(pe):
                    pe.sem_inc(s_turn, 2)
                    pe.sem_inc(s_prod, 2)
                    pe.wait_ge(s_load, 16 * len(loads))
                    if pe_first is not None:
                        pe_first(pe, frees)
                        pe.wait_ge(s_wts, 1)

                    def turn(j, k):
                        pe.wait_ge(s_slot, j + 1)
                        pe.wait_ge(s_feat, j + 1)
                        for c in range(KC):
                            last = nc.tensor.transpose(p_tr[k][:, c * 128:c * 128 + W],
                                                       slot[:, k, c * 128:(c + 1) * 128], ident[0:W, 0:W])
                        last.then_inc(s_turn, 1)

                    def product(j, k):
                        pe.wait_ge(s_feat, j + 3)
                        pe.wait_ge(s_emit, j + 1)
                        for b in range(nb):
                            c0, c1 = b * 512, min(cols, b * 512 + 512)
                            for c in range(KC):
                                last = mm(p_o[k][0:W, c0:c1], tr[:, k, c, 0:W], wt[:, c, c0:c1],
                                          start=c == 0, stop=c == KC - 1)
                        last.then_inc(s_prod, 1)

                    turn(0, 0)
                    with pe.Fori(0, NV // 2 - 1) as i:
                        for k in range(2):
                            turn(i * 2 + k + 1, 1 - k)
                            product(i * 2 + k, k)
                    turn(NV - 1, 1)
                    product(NV - 2, 0)
                    product(NV - 1, 1)

        def edges(l, acc, scale):
            H, RW, dots = ATT[l]["H"], D + 2 * ATT[l]["H"], l == 2
            V0 = D if dots else 0
            GW = V0 + RW
            GH = G * H
            name = f"e{l}_"
            with phase() as ph:
                rowbuf = [sb(f"{name}rowbuf{k}", [W, G, GW], F32, ph) for k in range(2)]
                idx = [sb(f"{name}idx{k}", [W, G], I32, ph) for k in range(2)]
                codet = [sb(f"{name}codet{k}", [W, G * W], F32, ph) for k in range(2)]
                gates = [sb(f"{name}gates{k}", [GH, W + 1], F32, ph) for k in range(2)]
                hot = [sb(f"{name}hot{k}", [W, G, W + 1], F32, ph) for k in range(2)]
                zb = [sb(f"{name}zb{k}", [W + 1, G, RW], F32, ph) for k in range(2)]
                prod = sb(f"{name}prod", [W, 3, 2 * D], F32, ph) if dots else sb(f"{name}prod", [W, GH], F32, ph)
                sc = sb(f"{name}sc", [W, GH], F32, ph)
                df = sb(f"{name}df", [W, GH], F32, ph)
                fw = sb(f"{name}fw", [GH, W], F32, ph)
                mx = sb(f"{name}mx", [GH, W], F32, ph)
                NG = G // 2
                p_q = [ph.enter_context(nc.psum_tensor(f"{name}p_q{k}", [W, 512], F32))
                       for k in range(NG if dots else 2)]
                NZ = 2 if dots else 5
                p_z = [ph.enter_context(nc.psum_tensor(f"{name}p_z{k}", [W + 1, 512], F32)) for k in range(NZ)]
                p_turn = ph.enter_context(nc.psum_tensor(f"{name}p_turn", [128, 512], F32))
                p_sc, p_m = p_turn[0:GH, 0:W], p_turn[0:W, W:W + GH]
                s_ld = sem2(name + "ld")
                s_go = sem(name + "go")
                s_seen = sem(name + "seen")
                s_rows = [gather_sem(f"{name}rows{k}") for k in range(2)]
                s_codet = sem(name + "codet")
                s_hot = sem(name + "hot")
                s_q = sem(name + "q")
                s_mul = sem(name + "mul")
                s_red = sem(name + "red")
                s_sc = sem(name + "sc")
                s_tsc = sem(name + "tsc")
                s_fw = sem(name + "fw")
                s_mx = sem(name + "mx")
                s_tm = sem(name + "tm")
                s_df = sem(name + "df")
                s_w = sem(name + "w")
                s_wv = sem(name + "wv")
                s_z = sem(name + "z")
                s_zb = sem(name + "zb")
                s_acc = sem(name + "acc")
                s_hs = sem2(name + "hs")
                block = ph.enter_context(nc.Block())

                def windows_of(engine, n):
                    return nc.values_load_multi_w_load_instructions(
                        wtab[0:1, bass.ds(n * G, G)], engines=[engine], min_val=0, max_val=NW,
                        skip_runtime_bounds_check_because="the table was made with min(., NW) of values >= 0")[1]

                def dmas(n, par, each):
                    return n * (each // 2) + (each - par * (each // 2))

                @block.sync
                def _(sp):
                    with sp.Fori(0, NB // 2) as i:
                        for par in range(2):
                            n = i * 2 + par
                            sp.wait_ge(s_mx, n + 1)
                            sp.dma_start(idx[par][:], srcs_tab[bass.ds(n, 1)].rearrange("a p g -> (a p) g")
                                         ).then_inc(s_ld[par], 16)
                            sp.dma_start(codet[par][:],
                                         code_tab[bass.ds(n * G, G), :].rearrange("(o g) e -> o (g e)", o=1)
                                         .to_broadcast([W, G * W])).then_inc(s_ld[par], 16)
                            sp.dma_start(gates[par][:],
                                         gate_tab[bass.ds(n * G, G), :].unsqueeze(1)
                                         .to_broadcast([G, H, W + 1])).then_inc(s_ld[par], 16)
                    for par in range(2):
                        sp.wait_ge(s_ld[par], 48 * (NB // 2))

                @block.gpsimd
                def _(pool):
                    with pool.Fori(0, NB // 2) as i:
                        for par in range(2):
                            n = i * 2 + par
                            pool.wait_ge(s_ld[par], dmas(n, par, 48))
                            for q in range(G):
                                pool.wait_ge(s_z, n * G + (q + 1))
                                pool.sem_inc(s_go, 1)
                                g.indirect_dma_start(
                                    out=rowbuf[par][:, q, 0:ATT[l]["ROW"]], out_offset=None, in_=row_tab[l],
                                    in_offset=bass.IndirectOffsetOnAxis(ap=idx[par][:, q:q + 1], axis=0)
                                ).then_inc(s_rows[par], 16)

                @block.scalar
                def _(act):
                    act.sem_inc(s_zb, NZ)
                    for k in range(2):
                        act.sem_inc(s_hs[k], 16)
                    with act.Fori(0, NB // 2) as i:
                        for par in range(2):
                            n = i * 2 + par
                            act.wait_ge(s_df, n + 1)
                            a.activation(rowbuf[par][:, :, V0 + D:V0 + D + H],
                                         df[:].rearrange("p (g h) -> p g h", h=H),
                                         ACT.Exp, scale=scale).then_inc(s_w, 1)
                            act.wait_ge(s_hs[par], dmas(n, par, 16))
                            for q in range(G):
                                act.wait_ge(s_z, n * G + (q + 1 + 2 * G))
                                act.wait_ge(s_acc, n * G + (q + 1))
                                a.activation(zb[par][:, q, :], p_z[q % NZ][:, 0:RW], ACT.Copy).then_inc(s_zb, 1)
                            act.wait_ge(s_zb, n * G + (G + NZ))
                            act.dma_start(head_tab[l][bass.ds(n * G, G), :].rearrange("(o g) r -> o g r", o=1),
                                          zb[par][HEAD:HEAD + 1, :, :]).then_inc(s_hs[par], 16)
                    for k in range(2):
                        act.wait_ge(s_hs[k], 16 * (NB // 2 + 1))

                @block.tensor
                def _(pe):
                    pe.sem_inc(s_z, 2 * G)

                    def spread(n, par):
                        wins = windows_of(mybir.EngineType.PE, n)
                        pe.wait_ge(s_codet, n + 1)
                        if dots:
                            for q in range(NG):
                                pe.wait_ge(s_mul, n * NG + (q + 1))
                                for r in range(2):
                                    last = mm(p_q[q][:, r * D:(r + 1) * D],
                                              codet[par][:, (2 * q + r) * W:(2 * q + r + 1) * W],
                                              z[:, bass.ds(wins[2 * q + r], 1), :].rearrange("p a b -> p (a b)"),
                                              start=True, stop=True)
                                last.then_inc(s_q, 1)
                        else:
                            pe.wait_ge(s_sc, n + 1)
                            for q in range(G):
                                last = mm(p_q[par][:, q * H:(q + 1) * H], codet[par][:, q * W:(q + 1) * W],
                                          dwin[:, bass.ds(wins[q], 1), 0:H].rearrange("p a b -> p (a b)"),
                                          start=True, stop=True)
                            last.then_inc(s_q, 1)

                    def turn_scores(n):
                        pe.wait_ge(s_sc, n + 3)
                        pe.sem_inc(s_seen, 1)
                        nc.tensor.transpose(p_sc, sc[:], ident[0:W, 0:W]).then_inc(s_tsc, 1)

                    def turn_maxima(n):
                        pe.wait_ge(s_mx, n + 3)
                        pe.sem_inc(s_seen, 1)
                        nc.tensor.transpose(p_m, mx[:], ident[0:GH, 0:GH]).then_inc(s_tm, 1)

                    def batch(n, par, ahead=True):
                        if ahead:
                            spread(n + 1, 1 - par)
                        pe.wait_ge(s_hot, n * G + G)
                        pe.wait_ge(s_wv, n + 1)
                        for q in range(G):
                            if ahead and q == 4:
                                turn_scores(n + 1)
                            if ahead and q == 8:
                                turn_maxima(n + 1)
                            pe.wait_ge(s_zb, n * G + (q + 1))
                            mm(p_z[q % NZ][:, 0:RW], hot[par][:, q, :], rowbuf[par][:, q, V0:V0 + RW],
                               start=True, stop=True).then_inc(s_z, 1)

                    spread(0, 0)
                    turn_scores(0)
                    turn_maxima(0)
                    batch(0, 0)
                    with pe.Fori(0, NB // 2 - 1) as i:
                        for par in range(2):
                            batch(i * 2 + par + 1, 1 - par)
                    batch(NB - 1, 1, ahead=False)

                @block.vector
                def _(dve):
                    v.memset(acc[:], 0.0).then_inc(s_acc, 2 * G)
                    dve.sem_inc(s_mul, NG)
                    dve.sem_inc(s_sc, 2)
                    dve.sem_inc(s_mx, 2)

                    def add_up(n, par, pairs, wins, ahead=False):
                        for q in pairs:
                            into = acc[:, bass.ds(wins[q], 1), :].rearrange("p a b -> p (a b)")
                            dve.wait_ge(s_zb, n * G + (q + 1 + NZ))
                            dve.wait_ge(s_acc, n * G + (q + 2 * G))
                            v.tensor_tensor(into, into, zb[par][:, q, :], ALU.add).then_inc(s_acc, 1)
                            if ahead:
                                one_hot(n + 2, par, q)

                    def code_t(n, par):
                        dve.wait_ge(s_ld[par], dmas(n, par, 48))
                        v.tensor_scalar(codet[par][:], codet[par][:], iota_col[0:W, :], None,
                                        ALU.is_equal).then_inc(s_codet, 1)

                    def one_hot(n, par, q):
                        v.tensor_scalar(hot[par][:, q, :], iota_row[0:W, 0:W + 1], mcode[:, bass.ds(n * G + q, 1)],
                                        None, ALU.is_equal).then_inc(s_hot, 1)

                    def scores(n, par):
                        dve.wait_ge(s_rows[par], dmas(n, par, 16 * G))
                        if dots:
                            def multiply(q):
                                if q >= 3:
                                    dve.wait_ge(s_red, n * NG + (q - 2))
                                dve.wait_ge(s_q, n * NG + (q + 1))
                                v.tensor_tensor(prod[:, q % 3, :].rearrange("p (r d) -> p r d", r=2),
                                                rowbuf[par][:, 2 * q:2 * q + 2, 0:D],
                                                p_q[q][:].rearrange("p (r d) -> p r d", r=2),
                                                ALU.mult).then_inc(s_mul, 1)
                            multiply(0)
                            for q in range(NG):
                                if q + 1 < NG:
                                    multiply(q + 1)
                                dve.wait_ge(s_mul, n * NG + (q + 1 + NG))
                                v.tensor_reduce(sc[:, 2 * H * q:2 * H * (q + 1)],
                                                       prod[:, q % 3, :].rearrange("p (h d) -> p h d", d=D // H),
                                                       AX, ALU.add).then_inc(s_red, 1)
                            dve.wait_ge(s_red, n * NG + NG)
                            dve.sem_inc(s_sc, 1)
                        else:
                            dve.wait_ge(s_q, n + 1)
                            v.tensor_tensor(prod[:].rearrange("p (g h) -> p g h", h=H),
                                            rowbuf[par][:, :, D:D + H],
                                            p_q[par][:, 0:GH].rearrange("p (g h) -> p g h", h=H),
                                            ALU.add).then_inc(s_mul, 1)
                            dve.wait_ge(s_mul, n + (1 + NG))
                            v.scalar_tensor_tensor(out=sc[:], in0=prod[:], scalar=0.2, in1=prod[:],
                                                   op0=ALU.mult, op1=ALU.max).then_inc(s_sc, 1)

                    def weights(n, par, before=True, ahead=True):
                        if before:
                            wins = windows_of(mybir.EngineType.DVE, n - 1)
                            add_up(n - 1, 1 - par, range(0, 3), wins, ahead)
                        dve.wait_ge(s_tsc, n + 1)
                        v.tensor_tensor_scan(out=fw[:], data0=gates[par][:, 0:W], data1=p_sc, initial=FAR,
                                             op0=ALU.add, op1=ALU.max).then_inc(s_fw, 1)
                        if before:
                            add_up(n - 1, 1 - par, range(3, 4), wins, ahead)
                        dve.wait_ge(s_fw, n + 1)
                        v.tensor_tensor_scan(out=mx[:, ::-1], data0=gates[par][:, 1:W + 1][:, ::-1],
                                             data1=fw[:, ::-1], initial=FAR,
                                             op0=ALU.add, op1=ALU.max).then_inc(s_mx, 1)
                        if before:
                            add_up(n - 1, 1 - par, range(4, G), wins, ahead)
                        if ahead:
                            code_t(n + 1, 1 - par)
                        dve.wait_ge(s_tm, n + 1)
                        v.tensor_tensor(df[:], sc[:], p_m, ALU.subtract).then_inc(s_df, 1)
                        v.tensor_tensor(rowbuf[par][:, :, V0 + D + H:V0 + RW],
                                        p_m.rearrange("p (g h) -> p g h", h=H),
                                        first[:, bass.ds(n * G, G)].unsqueeze(2).to_broadcast([W, G, H]), ALU.mult)
                        dve.wait_ge(s_w, n + 1)
                        rows = rowbuf[par][:, :, V0:V0 + D].rearrange("p g (h d) -> p g h d", h=H)
                        v.tensor_tensor(rows, rows, rowbuf[par][:, :, V0 + D:V0 + D + H].unsqueeze(3)
                                        .to_broadcast([W, G, H, D // H]), ALU.mult).then_inc(s_wv, 1)

                    code_t(0, 0)
                    for par in range(2):
                        for q in range(G):
                            one_hot(par, par, q)
                    scores(0, 0)
                    weights(0, 0, before=False)
                    with dve.Fori(0, NB // 2 - 1) as i:
                        for par in range(2):
                            scores(i * 2 + par + 1, 1 - par)
                            weights(i * 2 + par + 1, 1 - par)
                    scores(NB - 1, 1)
                    weights(NB - 1, 1, ahead=False)
                    add_up(NB - 1, 1, range(G), windows_of(mybir.EngineType.DVE, NB - 1))

        def merge(l, acc, scale, finish):
            H, RW = ATT[l]["H"], D + 2 * ATT[l]["H"]
            name = f"m{l}_"
            with phase() as ph:
                hrows = sb(name + "hrows", [PQ, PC, RW], F32, ph)
                hm = sb(name + "hm", [8, NP], F32, ph)
                hf = sb(name + "hf", [8, NP], F32, ph)
                hr = sb(name + "hr", [PQ, PC, H], F32, ph)
                hx = sb(name + "hx", [PQ, PC, H], F32, ph)
                winof = sb(name + "winof", [PQ, NV], F32, ph)
                oh = sb(name + "oh", [PQ, 2, PC, W], F32, ph)
                acc2 = sb(name + "acc2", [W, NV, RW], F32, ph)
                sm = [sb(f"{name}sm{k}", [W, NW, H], F32, ph) for k in range(5)]
                part = [sb(f"{name}part{k}", [W, 5, D], F32, ph) for k in range(2)]
                p_r = ph.enter_context(nc.psum_tensor(name + "p_r", [8, 512], F32))
                p_c = ph.enter_context(nc.psum_tensor(name + "p_c", [PQ, 512], F32))
                p_w = [ph.enter_context(nc.psum_tensor(f"{name}p_w{k}", [W, 512], F32)) for k in range(2)]
                s_in, s_iota, s_r, s_hm, s_c, s_hx, s_hr, s_hv = [
                    sem(name + n) for n in ("in", "iota", "r", "hm", "c", "hx", "hr", "hv")]
                s_oh = sem(name + "oh")
                s_p = sem(name + "p")
                s_ev = sem(name + "ev")
                s_sh, s_ex = sem(name + "sh"), sem(name + "ex")
                block = ph.enter_context(nc.Block())

                @block.sync
                def _(sp):
                    sp.dma_start(hrows[:], head_tab[l].rearrange("(c p) r -> p c r", p=PQ)).then_inc(s_in, 16)
                    sp.wait_ge(s_in, 16)

                @block.gpsimd
                def _(pool):
                    g.iota(winof[:], pattern=[[W, NV]], base=0, channel_multiplier=0,
                           allow_small_or_imprecise_dtypes=True).then_inc(s_iota, 1)

                @block.tensor
                def _(pe):
                    pe.sem_inc(s_p, 2)
                    pe.wait_ge(s_in, 16)
                    for c in range(PC):
                        last = nc.tensor.transpose(p_r[0:H, c * PQ:(c + 1) * PQ], hrows[:, c, D + H:RW],
                                                   ident[0:PQ, 0:PQ])
                    last.then_inc(s_r, 1)
                    pe.wait_ge(s_hm, 1)
                    for c in range(PC):
                        last = nc.tensor.transpose(p_c[:, c * H:(c + 1) * H], hm[0:H, c * PQ:(c + 1) * PQ],
                                                   ident[0:H, 0:H])
                    last.then_inc(s_c, 1)
                    pe.wait_ge(s_hv, 1)
                    with pe.Fori(0, NV // 2) as i:
                        for k in range(2):
                            pe.wait_ge(s_oh, i * 2 + k + 1)
                            pe.wait_ge(s_ev, i * 2 + k + 1)
                            for c in range(PC):
                                last = mm(p_w[k][:, 0:RW], oh[:, k, c, :], hrows[:, c, :],
                                          start=c == 0, stop=c == PC - 1)
                            last.then_inc(s_p, 1)

                @block.scalar
                def _(act):
                    act.sem_inc(s_ev, 2)
                    act.wait_ge(s_hx, 1)
                    a.activation(hr[:], hx[:], ACT.Exp, scale=scale).then_inc(s_hr, 1)
                    with act.Fori(0, NV // 2) as i:
                        for k in range(2):
                            act.wait_ge(s_p, i * 2 + k + 3)
                            a.activation(acc2[:, bass.ds(i * 2 + k, 1), :].rearrange("p a b -> p (a b)"),
                                         p_w[k][:, 0:RW], ACT.Copy).then_inc(s_ev, 1)
                    act.wait_ge(s_sh, 1)
                    a.activation(sm[0][:], sm[0][:], ACT.Exp, scale=scale)
                    a.activation(sm[1][:], sm[1][:], ACT.Exp, scale=scale).then_inc(s_ex, 1)

                @block.vector
                def _(dve):
                    dve.wait_ge(s_r, 1)
                    vd(v.tensor_copy(hm[0:H, :], p_r[0:H, 0:NP]))
                    vd(v.tensor_tensor_scan(out=hf[0:H, :], data0=hgate[0:H, 0:NP], data1=hm[0:H, :], initial=FAR,
                                            op0=ALU.add, op1=ALU.max))
                    v.tensor_tensor_scan(out=hm[0:H, ::-1], data0=hgate[0:H, 1:NP + 1][:, ::-1],
                                         data1=hf[0:H, ::-1], initial=FAR,
                                         op0=ALU.add, op1=ALU.max).then_inc(s_hm, 1)
                    dve.wait_ge(s_c, 1)
                    dve.wait_ge(s_in, 16)
                    top_m = p_c[:, 0:PC * H].rearrange("p (c h) -> p c h", h=H)
                    v.tensor_tensor(hx[:], hrows[:, :, D + H:RW], top_m, ALU.subtract).then_inc(s_hx, 1)
                    dve.wait_ge(s_hr, 1)
                    v.tensor_tensor(hrows[:, :, D + H:RW], top_m, hfirst[:].unsqueeze(2).to_broadcast([PQ, PC, H]),
                                    ALU.mult)
                    v.tensor_tensor(hrows[:, :, D:D + H], hrows[:, :, D:D + H], hr[:], ALU.mult)
                    body = hrows[:, :, 0:D].rearrange("p c (h d) -> p c h d", h=H)
                    v.tensor_tensor(body, body, hr[:].unsqueeze(3).to_broadcast([PQ, PC, H, D // H]),
                                    ALU.mult).then_inc(s_hv, 1)
                    dve.wait_ge(s_iota, 1)
                    with dve.Fori(0, NV // 2) as i:
                        for k in range(2):
                            dve.wait_ge(s_p, i * 2 + k + 1)
                            for c in range(PC):
                                last = v.tensor_scalar(oh[:, k, c, :], iota_row[0:PQ, 0:W],
                                                       winof[:, bass.ds(i * 2 + k, 1)], hdst[:, c:c + 1],
                                                       ALU.add, ALU.is_equal)
                            last.then_inc(s_oh, 1)
                    dve.wait_ge(s_ev, NV + 2)
                    acc1, ac2 = acc[0:W, 0:NW, :], acc2[:, 0:NW, :]
                    den1, max1 = acc1[:, :, D:D + H], acc1[:, :, D + H:RW]
                    den2, max2 = ac2[:, :, D:D + H], ac2[:, :, D + H:RW]
                    v.tensor_scalar(sm[0][:], den1, 0.0, FAR, ALU.is_equal, ALU.mult)
                    vd(v.tensor_scalar(sm[1][:], den2, 0.0, FAR, ALU.is_equal, ALU.mult))
                    v.tensor_tensor(sm[0][:], sm[0][:], max1, ALU.add)
                    vd(v.tensor_tensor(sm[1][:], sm[1][:], max2, ALU.add))
                    vd(v.tensor_tensor(sm[2][:], sm[0][:], sm[1][:], ALU.max))
                    v.tensor_tensor(sm[0][:], sm[0][:], sm[2][:], ALU.subtract)
                    v.tensor_tensor(sm[1][:], sm[1][:], sm[2][:], ALU.subtract)
                    v.drain().then_inc(s_sh, 1)
                    dve.wait_ge(s_ex, 1)
                    v.tensor_tensor(sm[2][:], sm[0][:], den1, ALU.mult)
                    vd(v.tensor_tensor(sm[3][:], sm[1][:], den2, ALU.mult))
                    vd(v.tensor_tensor(sm[2][:], sm[2][:], sm[3][:], ALU.add))
                    if l < 2:
                        vd(v.tensor_scalar(sm[2][:], sm[2][:], 1e-16, None, ALU.add))
                    else:
                        vd(v.tensor_scalar(sm[2][:], sm[2][:], 1e-30, None, ALU.max))
                    vd(v.reciprocal(sm[4][:], sm[2][:]))
                    v.tensor_tensor(sm[0][:], sm[0][:], sm[4][:], ALU.mult)
                    vd(v.tensor_tensor(sm[1][:], sm[1][:], sm[4][:], ALU.mult))
                    for c in range(0, NW, 5):
                        for k, ac in enumerate((acc1, ac2)):
                            v.tensor_tensor(part[k][:].rearrange("p w (h d) -> p w h d", h=H),
                                            ac[:, c:c + 5, 0:D].rearrange("p w (h d) -> p w h d", h=H),
                                            sm[k][:, c:c + 5, :].unsqueeze(3).to_broadcast([W, 5, H, D // H]),
                                            ALU.mult)
                        v.drain()
                        finish(c, part)
                        v.drain()

        def experts(f, last_layer):
            cf = FFN[f]
            NE, FC, NBLK = cf["E"], cf["FC"], cf["NBLK"]
            name = f"x{f}_"
            with ExitStack() as keep:
                logit = sb(name + "logit", [W, NV, NE], F32, keep)
                wt2 = [sb(f"{name}wt{k}", [W, NW], F32, keep) for k in range(2)]
                pos = [sb(f"{name}pos{k}", [W, NW], I32, keep) for k in range(2)]
                bexp = sb(name + "bexp", [1, NBLK], I32, keep)
                with phase() as ph:
                    gw = sb(name + "gw", [128, KC, NE], F32, ph)
                    gb = sb(name + "gb", [W, NE], F32, ph)
                    project(name + "g_", z, NE,
                            [(gw[:], t[f"gate_w{f}"].rearrange("(c p) e -> p c e", p=128)),
                             (gb[:], t[f"gate_b{f}"].to_broadcast([W, NE]))], gw,
                            lambda j, k, p: v.tensor_tensor(logit[:, bass.ds(j, 1), :].rearrange("p a b -> p (a b)"),
                                                            p[0:W, 0:NE], gb[:], ALU.add), norm=True)
                with phase() as ph:
                    def arr(n, shape=(W, NW, NE)):
                        return sb(name + n, list(shape), F32, ph)
                    lg = logit[:, 0:NW, :]
                    order = arr("order", (W, NE))
                    eq, key, lg2, both, base, rank = [arr(n) for n in ("eq", "key", "lg2", "both", "base", "rank")]
                    oh = [arr("oh0"), arr("oh1")]
                    top1, top2, kmax, dd, ee = [arr(n, (W, NW)) for n in ("top1", "top2", "kmax", "dd", "ee")]
                    colt, reset, run = [arr(n, (W, NE, NW)) for n in ("colt", "reset", "run")]
                    steps = arr("steps", (W, NW))
                    nblk, cend, zer = [arr(n, (W, NE)) for n in ("nblk", "cend", "zer")]
                    lower = arr("lower", (W, W))
                    bnum = arr("bnum", (1, NBLK))
                    bcmp = arr("bcmp", (1, NBLK, NE))
                    bsum = arr("bsum", (1, NBLK))
                    p_rank = ph.enter_context(nc.psum_tensor(name + "p_rank", [W, 512], F32))
                    p_col = ph.enter_context(nc.psum_tensor(name + "p_col", [W, 512], F32))
                    s_const, s_both, s_ranks, s_dd, s_ee, s_pos, s_var, s_std = [
                        sem(name + n) for n in ("const", "both", "ranks", "dd", "ee", "pos", "var", "std")]
                    s_sent = gather_sem(name + "sent")
                    block = ph.enter_context(nc.Block())

                    @block.gpsimd
                    def _(pool):
                        g.iota(order[:], pattern=[[-1, NE]], base=NE, channel_multiplier=0,
                               allow_small_or_imprecise_dtypes=True).then_inc(s_const, 1)
                        g.iota(steps[:], pattern=[[128, NW]], base=0, channel_multiplier=0,
                               allow_small_or_imprecise_dtypes=True).then_inc(s_const, 1)
                        g.iota(bnum[:], pattern=[[1, NBLK]], base=0, channel_multiplier=0,
                               allow_small_or_imprecise_dtypes=True).then_inc(s_const, 1)
                        g.affine_select(out=lower[:], in_=ones[0:W, 0:W], compare_op=ALU.is_ge, fill=0.0, base=-1,
                                        pattern=[[1, W]], channel_multiplier=-1).then_inc(s_const, 1)
                        pool.wait_ge(s_pos, 1)
                        for w in range(NW):
                            for k in range(2):
                                g.indirect_dma_start(out=xs_tab, in_=z[:, w, :], in_offset=None,
                                                     out_offset=bass.IndirectOffsetOnAxis(ap=pos[k][:, w:w + 1], axis=0)
                                                     ).then_inc(s_sent, 16)
                        pool.wait_ge(s_sent, 16 * 2 * NW)

                    @block.tensor
                    def _(pe):
                        pe.wait_ge(s_both, 1)
                        flat = both[:].rearrange("p w e -> p (w e)")
                        mm(p_rank[:, 0:NW * NE], lower[:], flat, start=True, stop=True)
                        mm(p_col[:, 0:NW * NE], ones[0:W, 0:W], flat, start=True, stop=True).then_inc(s_ranks, 1)

                    @block.scalar
                    def _(act):
                        act.wait_ge(s_dd, 1)
                        a.activation(ee[:], dd[:], ACT.Exp).then_inc(s_ee, 1)
                        if f == 1:
                            norm_sqrt(act, s_var, s_std)

                    @block.vector
                    def _(dve):
                        def wide(ap):
                            return ap.unsqueeze(2).to_broadcast([W, NW, NE])

                        def each(ap):
                            return ap.unsqueeze(1).to_broadcast([W, NW, NE])

                        dve.wait_ge(s_const, 4)

                        def pick(src, best, hot):
                            vd(v.tensor_reduce(best[:], src, AX, ALU.max))
                            vd(v.tensor_tensor(eq[:], src, wide(best[:]), ALU.is_equal))
                            vd(v.tensor_tensor(key[:], eq[:], each(order[:]), ALU.mult))
                            vd(v.tensor_reduce(kmax[:], key[:], AX, ALU.max))
                            vd(v.tensor_tensor(hot[:], key[:], wide(kmax[:]), ALU.is_equal))

                        pick(lg, top1, oh[0])
                        vd(v.tensor_scalar(lg2[:], oh[0][:], FAR, None, ALU.mult))
                        vd(v.tensor_tensor(lg2[:], lg2[:], lg, ALU.add))
                        pick(lg2[:], top2, oh[1])
                        vd(v.tensor_tensor(both[:], oh[0][:], oh[1][:], ALU.add))
                        v.tensor_tensor(dd[:], top2[:], top1[:], ALU.subtract)
                        v.drain().then_inc(s_both, 1)
                        dve.sem_inc(s_dd, 1)
                        dve.wait_ge(s_ee, 1)
                        vd(v.tensor_scalar(dd[:], ee[:], 1.0, None, ALU.add))
                        vd(v.reciprocal(wt2[0][:], dd[:]))
                        v.tensor_tensor(wt2[1][:], ee[:], wt2[0][:], ALU.mult)
                        v.memset(reset[:], 1.0)
                        dve.wait_ge(s_ranks, 1)
                        v.tensor_copy(colt[:], p_col[:, 0:NW * NE].rearrange("p (w e) -> p e w", e=NE))
                        v.memset(zer[:], 0.0)
                        v.drain()
                        vd(v.memset(reset[:, :, 0:1], 0.0))
                        vd(v.tensor_tensor_scan(out=run[:].rearrange("p e w -> p (e w)"),
                                                data0=reset[:].rearrange("p e w -> p (e w)"),
                                                data1=colt[:].rearrange("p e w -> p (e w)"), initial=0.0,
                                                op0=ALU.mult, op1=ALU.add))
                        cmp3 = reset[:]
                        vd(v.tensor_tensor(cmp3, run[:, :, NW - 1:NW].to_broadcast([W, NE, NW]),
                                           steps[:].unsqueeze(1).to_broadcast([W, NE, NW]), ALU.is_gt))
                        vd(v.tensor_reduce(nblk[:], cmp3, AX, ALU.add))
                        vd(v.tensor_tensor_scan(out=cend[:], data0=nblk[:], data1=zer[:], initial=0.0,
                                                op0=ALU.add, op1=ALU.add))
                        vd(v.tensor_tensor(zer[:], cend[:], nblk[:], ALU.subtract))
                        vd(v.tensor_scalar(zer[:], zer[:], 128.0, None, ALU.mult))
                        v.tensor_tensor(run[:], run[:], colt[:], ALU.subtract)
                        v.drain()
                        vd(v.tensor_tensor(base[:], run[:].rearrange("p e w -> p w e"), each(zer[:]), ALU.add))
                        vd(v.tensor_tensor(rank[:], base[:],
                                           p_rank[:, 0:NW * NE].rearrange("p (w e) -> p w e", e=NE), ALU.add))
                        for k in range(2):
                            vd(v.tensor_tensor(key[:], rank[:], oh[k][:], ALU.mult))
                            vd(v.tensor_reduce(top1[:], key[:], AX, ALU.add))
                            vd(v.tensor_copy(pos[k][:], top1[:]))
                        vd(v.tensor_tensor(bcmp[:], cend[0:1, :].unsqueeze(1).to_broadcast([1, NBLK, NE]),
                                           bnum[:].unsqueeze(2).to_broadcast([1, NBLK, NE]), ALU.is_le))
                        vd(v.tensor_reduce(bsum[:], bcmp[:], AX, ALU.add))
                        vd(v.tensor_scalar(bexp[:], bsum[:], NE - 1.0, None, ALU.min))
                        if f == 1:
                            norm_stats(dve, z, s_var, s_std)
                            norm_apply(dve, z, z)
                        v.drain().then_inc(s_pos, 1)
                with phase() as ph:
                    pack = [sb(f"{name}pack{k}", [128, cf["PK"]], F32, ph) for k in range(2)]
                    w2 = [sb(f"{name}w2{k}", [128, FC * D], F32, ph) for k in range(2)]
                    b2 = [sb(f"{name}b2{k}", [1, D], F32, ph) for k in range(2)]
                    xb = [sb(f"{name}xb{k}", [128, D], F32, ph) for k in range(2)]
                    xt = [sb(f"{name}xt{k}", [128, KC, 128], F32, ph) for k in range(2)]
                    ht = [sb(f"{name}ht{k}", [128, FC, 128], F32, ph) for k in range(2)]
                    yb = [sb(f"{name}yb{k}", [128, D], F32, ph) for k in range(2)]
                    p_x = [ph.enter_context(nc.psum_tensor(f"{name}p_x{k}", [128, 512], F32)) for k in range(2)]
                    p_h = [ph.enter_context(nc.psum_tensor(f"{name}p_h{k}", [128, max(4, FC), 128], F32)) for k in range(2)]
                    p_y = [ph.enter_context(nc.psum_tensor(f"{name}p_y{k}", [128, 512], F32))
                           for k in range(2)] if FC == 4 else None
                    if p_y is None:
                        p_y = [ph.enter_context(nc.psum_tensor(f"{name}p_y{k}", [128, 512], F32)) for k in range(2)]
                    s_w = sem2(name + "w")
                    s_w2 = sem2(name + "w2")
                    s_xt = sem(name + "xtp")
                    s_xs = sem(name + "xs")
                    s_h = sem(name + "h")
                    s_hs = sem(name + "hs")
                    s_y = sem(name + "y")
                    s_ys = sem(name + "ys")
                    s_st = sem2(name + "st")
                    block = ph.enter_context(nc.Block())

                    @block.sync
                    def _(sp):
                        for k in range(2):
                            sp.sem_inc(s_st[k], 16)

                        def load(b, k):
                            e = sp.value_load(bexp[0:1, bass.ds(b, 1)], min_val=0, max_val=NE - 1)
                            sp.wait_ge(s_h, b * FC + FC)
                            sp.wait_ge(s_hs, b * FC + FC)
                            sp.dma_start(xb[k][:], xs_tab[bass.ds(b * 128, 128), :]).then_inc(s_w[k], 16)
                            sp.dma_start(pack[k][:], t[f"pack{f}"][bass.ds(e, 1)].rearrange("a p c -> (a p) c")
                                         ).then_inc(s_w[k], 16)
                            return e

                        def load2(b, k):
                            e = sp.value_load(bexp[0:1, bass.ds(b, 1)], min_val=0, max_val=NE - 1)
                            sp.wait_ge(s_y, b + 1)
                            sp.dma_start(w2[k][:], t[f"w2_{f}"][bass.ds(e, 1)].rearrange("a p c -> (a p) c")
                                         ).then_inc(s_w2[k], 16)
                            sp.dma_start(b2[k][:], t[f"b2_{f}"][bass.ds(e, 1), :]).then_inc(s_w2[k], 16)

                        def store(b, k):
                            sp.wait_ge(s_ys, b + 3)
                            sp.dma_start(ys_tab[bass.ds(b * 128, 128), :], yb[k][:]).then_inc(s_st[k], 16)

                        for k in range(2):
                            load(k, k)
                            load2(k, k)
                        with sp.Fori(0, NBLK // 2 - 1) as i:
                            for k in range(2):
                                load(i * 2 + k + 2, k)
                                load2(i * 2 + k + 2, k)
                                store(i * 2 + k, k)
                        for k in range(2):
                            store(NBLK - 2 + k, k)
                        for k in range(2):
                            sp.wait_ge(s_st[k], 16 * (NBLK // 2 + 1))
                            sp.wait_ge(s_w[k], 32 * (NBLK // 2))
                            sp.wait_ge(s_w2[k], 32 * (NBLK // 2))

                    @block.tensor
                    def _(pe):
                        pe.sem_inc(s_xt, 2)
                        pe.sem_inc(s_y, 2)
                        pe.sem_inc(s_h, 2 * FC)

                        def hidden(b, k):
                            pe.wait_ge(s_w[k], b * 16 + (32 - 16 * k))
                            pe.wait_ge(s_xs, b + 1)
                            for c in range(KC):
                                last = nc.tensor.transpose(p_x[k][:, c * 128:(c + 1) * 128],
                                                           xb[k][:, c * 128:(c + 1) * 128], ident[:])
                            last.then_inc(s_xt, 1)
                            pe.wait_ge(s_hs, b * FC + FC)
                            pe.wait_ge(s_xs, b + 3)
                            for j in range(FC):
                                for c in range(KC):
                                    o = c * cf["F"] + j * 128
                                    last = mm(p_h[k][:, j, :], pack[k][:, o:o + 128], xt[k][:, c, :],
                                              start=c == 0, stop=c == KC - 1)
                                last.then_inc(s_h, 1)

                        def output(b, k):
                            pe.wait_ge(s_w2[k], b * 16 + (32 - 16 * k))
                            pe.wait_ge(s_ys, b + 1)
                            mm(p_y[k][:, 0:D], ones[0:1, :], b2[k][:], start=True, stop=False)
                            for j in range(FC):
                                pe.wait_ge(s_hs, b * FC + (j + 1 + 2 * FC))
                                last = mm(p_y[k][:, 0:D], ht[k][:, j, :], w2[k][:, j * D:(j + 1) * D],
                                          start=False, stop=j == FC - 1)
                            last.then_inc(s_y, 1)

                        hidden(0, 0)
                        with pe.Fori(0, NBLK // 2 - 1) as i:
                            for k in range(2):
                                hidden(i * 2 + k + 1, 1 - k)
                                output(i * 2 + k, k)
                        hidden(NBLK - 1, 1)
                        output(NBLK - 2, 0)
                        output(NBLK - 1, 1)

                    @block.scalar
                    def _(act):
                        act.sem_inc(s_hs, 2 * FC)
                        with act.Fori(0, NBLK // 2) as i:
                            for k in range(2):
                                act.wait_ge(s_y, i * 2 + k + 1)
                                for j in range(FC):
                                    if j % 4 == 0:
                                        act.wait_ge(s_h, (i * 2 + k) * FC + (j + 4 + 2 * FC))
                                    a.activation(ht[k][:, j, :], p_h[k][:, j, :], ACT.Relu if f == 0 else ACT.Gelu,
                                                 bias=pack[k][:, cf["ob"] + j:cf["ob"] + j + 1]).then_inc(s_hs, 1)

                    @block.vector
                    def _(dve):
                        dve.sem_inc(s_xs, 2)
                        dve.sem_inc(s_ys, 2)

                        def features(b, k):
                            dve.wait_ge(s_xt, b + 3)
                            if f == 0:
                                v.tensor_copy(xt[k][:].rearrange("p c m -> p (c m)"), p_x[k][:, 0:D]).then_inc(s_xs, 1)
                            else:
                                for c in range(KC):
                                    last = v.tensor_scalar(xt[k][:, c, :], p_x[k][:, c * 128:(c + 1) * 128],
                                                           pack[k][:, cf["og"] + c:cf["og"] + c + 1],
                                                           pack[k][:, cf["og"] + KC + c:cf["og"] + KC + c + 1],
                                                           ALU.mult, ALU.add)
                                last.then_inc(s_xs, 1)

                        def result(b, k):
                            dve.wait_ge(s_st[k], b * 8 + (16 - 8 * k))
                            dve.wait_ge(s_y, b + 3)
                            v.tensor_copy(yb[k][:], p_y[k][:, 0:D]).then_inc(s_ys, 1)

                        features(0, 0)
                        with dve.Fori(0, NBLK // 2 - 1) as i:
                            for k in range(2):
                                features(i * 2 + k + 1, 1 - k)
                                result(i * 2 + k, k)
                        features(NBLK - 1, 1)
                        result(NBLK - 2, 0)
                        result(NBLK - 1, 1)
                with phase() as ph:
                    R = 5
                    got = [[sb(f"{name}got{r}_{k}", [W, D], F32, ph) for k in range(2)] for r in range(R)]
                    gb2 = sb(name + "gamma", [W, 2, D], F32, ph)
                    wide = sb(name + "wide", [W, NW, D], F32, ph) if f == 0 else None
                    s_got = [gather_sem(f"{name}got{r}") for r in range(R)]
                    s_used, s_g, s_var, s_std, s_out, s_c = [sem(name + n) for n in ("used", "gam", "var2", "std2", "out", "c")]
                    block = ph.enter_context(nc.Block())

                    @block.gpsimd
                    def _(pool):
                        for w in range(NW):
                            if w >= R:
                                pool.wait_ge(s_used, w - R + 1)
                            for k in range(2):
                                g.indirect_dma_start(out=got[w % R][k][:], out_offset=None, in_=ys_tab,
                                                     in_offset=bass.IndirectOffsetOnAxis(ap=pos[k][:, w:w + 1], axis=0)
                                                     ).then_inc(s_got[w % R], 16)

                    @block.scalar
                    def _(act):
                        if f == 0:
                            norm_sqrt(act, s_var, s_std)

                    @block.vector
                    def _(dve):
                        into = z if f == 0 else xcur
                        c = 0
                        for w in range(NW):
                            dve.wait_ge(s_got[w % R], 32 * (w // R + 1))
                            v.scalar_tensor_tensor(out=into[:, w, :], in0=got[w % R][0][:], scalar=wt2[0][:, w:w + 1],
                                                   in1=into[:, w, :], op0=ALU.mult, op1=ALU.add).then_inc(s_c, 1)
                            dve.wait_ge(s_c, w + 1)
                            v.scalar_tensor_tensor(out=into[:, w, :], in0=got[w % R][1][:], scalar=wt2[1][:, w:w + 1],
                                                   in1=into[:, w, :], op0=ALU.mult, op1=ALU.add).then_inc(s_used, 1)
                        if f == 0:
                            dve.wait_ge(s_g, 32)
                            v.drain()
                            norm_stats(dve, z, s_var, s_std)
                            norm_apply(dve, z, z)
                            vd(v.tensor_tensor(wide[:], z[:, 0:NW, :],
                                               gb2[:, 0:1, :].to_broadcast([W, NW, D]), ALU.mult))
                            v.tensor_tensor(xcur[:, 0:NW, :], xcur[:, 0:NW, :],
                                            gb2[:, 1:2, :].to_broadcast([W, NW, D]), ALU.add)
                            v.drain()
                            v.tensor_tensor(xcur[:, 0:NW, :], xcur[:, 0:NW, :], wide[:], ALU.add)

                    @block.sync
                    def _(sp):
                        if f == 0:
                            for k, n in enumerate(("gamma", "beta")):
                                sp.dma_start(gb2[:, k, :], t[n].to_broadcast([W, D])).then_inc(s_g, 16)
                            sp.wait_ge(s_g, 32)
                        else:
                            sp.wait_ge(s_used, NW)
                            sp.dma_start(t["out"].rearrange("(w p) d -> p w d", p=W), xcur[:, 0:NW, :]).then_inc(s_out, 16)
                            sp.wait_ge(s_out, 16)

        with ExitStack() as gat:
            for l in range(2):
                H, RW = ATT[l]["H"], D + 2 * ATT[l]["H"]
                src = z if l == 0 else None
                with phase() as ph:
                    wnat = sb(f"wnat{l}", [128, KC, D], F32, ph)
                    wts = sb(f"wts{l}", [128, KC, RW], F32, ph)
                    amat = sb(f"amat{l}", [128, KC, 2 * H], F32, ph)
                    rows = [sb(f"grow{l}_{k}", [W, D + H], F32, ph) for k in range(2)]
                    p_a = ph.enter_context(nc.psum_tensor(f"p_a{l}", [128, 512], F32))
                    s_pa, s_am, s_ld2 = sem(f"s_pa{l}"), sem(f"s_am{l}"), sem(f"s_al{l}")

                    def dve_first(dve, s_load, s_wts, _):
                        dve.wait_ge(s_pa, 1)
                        v.tensor_copy(wts[:, :, D:RW], p_a[:, 0:KC * 2 * H].rearrange("p (c h) -> p c h", c=KC))
                        v.drain().then_inc(s_wts, 1)

                    def pe_first(pe, _):
                        for ci in range(KC):
                            for co in range(KC):
                                last = mm(p_a[:, ci * 2 * H:(ci + 1) * 2 * H], wnat[:, co, ci * 128:(ci + 1) * 128],
                                          amat[:, co, :], start=co == 0, stop=co == KC - 1)
                        last.then_inc(s_pa, 1)

                    with nc.Block() as pre:
                        @pre.vector
                        def _(dve):
                            v.memset(amat[:], 0.0)
                            v.drain().then_inc(s_am, 1)

                        @pre.sync
                        def _(sp):
                            sp.wait_ge(s_am, 1)
                            n = 0
                            for k, nm in enumerate(("src", "dst")):
                                for h in range(H):
                                    for o in range(h * (D // H), (h + 1) * (D // H), min(128, D // H)):
                                        m = min(128, D // H)
                                        sp.dma_start(amat[o % 128:o % 128 + m, o // 128, k * H + h:k * H + h + 1],
                                                     t[f"a{l}_{nm}"][o:o + m, :]).then_inc(s_ld2, 16)
                                        n += 1
                            sp.wait_ge(s_ld2, 16 * n)

                    def emit(j, k, p):
                        v.tensor_copy(rows[k][:], p[0:W, 0:D + H])
                        return v.tensor_copy(dwin[:, bass.ds(j, 1), 0:H].rearrange("p a b -> p (a b)"),
                                             p[0:W, D + H:RW])

                    project(f"p{l}_", z, RW,
                            [(wnat[:], t[f"W{l}"].rearrange("(c p) i -> p c i", p=128)),
                             (wts[:, :, 0:D], t[f"WT{l}"].rearrange("(c p) o -> p c o", p=128))], wts, emit,
                            norm=l == 0, dve_first=dve_first, pe_first=pe_first, rows=rows, row_dram=row_tab[l])
                with phase() as ph:
                    acc = sb(f"acc{l}", [W + 1, NV, RW], F32, ph)
                    edges(l, acc, 1.0)

                    def finish(c, part, l=l):
                        if l == 0:
                            vd(v.tensor_tensor(part[0][:], part[0][:], part[1][:], ALU.add))
                            v.tensor_scalar(z[:, c:c + 5, :], part[0][:], 0.0, None, ALU.max)
                        else:
                            vd(v.tensor_tensor(part[0][:], part[0][:], part[1][:], ALU.add))
                            v.tensor_tensor(xcur[:, c:c + 5, :], xcur[:, c:c + 5, :], part[0][:], ALU.add)

                    merge(l, acc, 1.0, finish)

        experts(0, False)

        DH = D // ATT[2]["H"]
        with phase() as ph:
            wq = sb("wq", [128, KC, 3 * D], F32, ph)
            bq = sb("bq", [W, 3 * D], F32, ph)
            rows = [sb(f"kv{k}", [W, 2 * D], F32, ph) for k in range(2)]

            def emit(j, k, p):
                v.tensor_tensor(z[:, bass.ds(j, 1), :].rearrange("p a b -> p (a b)"), p[0:W, 0:D], bq[:, 0:D], ALU.add)
                return v.tensor_tensor(rows[k][:], p[0:W, D:3 * D], bq[:, D:3 * D], ALU.add)

            project("pq_", z, 3 * D,
                    [(wq[:], t["Wqkv"].rearrange("(c p) o -> p c o", p=128)),
                     (bq[:], t["bqkv"].to_broadcast([W, 3 * D]))], wq, emit,
                    norm=True, rows=rows, row_dram=row_tab[2])
        with phase() as ph:
            RW = D + 2 * ATT[2]["H"]
            acc = sb("acc2x", [W + 1, NV, RW], F32, ph)
            edges(2, acc, float(DH) ** -0.5)

            def finish(c, part):
                for w in range(c, c + 5):
                    v.tensor_scalar(z[:, w, :], xcur[:, w, :], mean[:, w:w + 1], rstd[:, w:w + 1],
                                    ALU.subtract, ALU.mult)
                vd(v.tensor_tensor(part[0][:], part[0][:], part[1][:], ALU.add))
                for w in range(5):
                    zz = z[:, c + w, :].rearrange("p (d h) -> p h d", d=DH)
                    v.tensor_tensor(zz, zz, part[0][:, w, :].rearrange("p (h d) -> p h d", d=DH), ALU.add)

            merge(2, acc, float(DH) ** -0.5, finish)
        with phase() as ph:
            wo = sb("wo", [128, KC, D], F32, ph)
            bo = sb("bo", [W, D], F32, ph)

            def add_bias(dve, s_load, s_wts, _):
                dve.wait_ge(s_load, 32)
                v.tensor_tensor(xcur[:], xcur[:], bo[:].unsqueeze(1).to_broadcast([W, NV, D]), ALU.add)
                v.drain().then_inc(s_wts, 1)

            def emit(j, k, p):
                xw = xcur[:, bass.ds(j, 1), :].rearrange("p a b -> p (a b)")
                return v.tensor_tensor(xw, xw, p[0:W, 0:D], ALU.add)

            project("po_", z, D, [(wo[:], t["Wout"].rearrange("(c p) o -> p c o", p=128)),
                                  (bo[:], t["bout"].to_broadcast([W, D]))], wo, emit, dve_first=add_bias)
        experts(1, True)


def kernel(**inputs):
    import concourse.bacc as bacc
    from concourse.bass_utils import run_bass_kernel_spmd

    x = {k: np.asarray(val) for k, val in inputs.items()}
    src, dst = x["src"], x["dst"]
    edges = np.full((NT, 256), -1, dst.dtype)
    edges[:, 1:W + 1] = dst.reshape(NT, W)
    edges[1:, 0] = dst[W - 1:-1:W]
    edges[:-1, W + 1] = dst[W::W]
    edges[:, W + 2:2 * W + 2] = src.reshape(NT, W)

    def expert_pack(f, w1, b1, gain, offset):
        ne = FFN[f]["E"]
        parts = [w1.reshape(ne, KC, 128, -1).transpose(0, 2, 1, 3).reshape(ne, 128, -1),
                 b1.reshape(ne, -1, 128).transpose(0, 2, 1)]
        for col in (gain, offset):
            parts.append(np.zeros((ne, 128, KC), w1.dtype) if col is None
                         else col.reshape(ne, KC, 128).transpose(0, 2, 1))
        return np.ascontiguousarray(np.concatenate(parts, axis=2))

    def rows_of(w2):
        return w2.reshape(len(w2), -1, 128, D).transpose(0, 2, 1, 3).reshape(len(w2), 128, -1)

    arrays = {
        "x": x["x"], "edges": edges, "ends": np.stack([dst[0::W], dst[W - 1::W]]),
        "W0": x["L0_gnn_W1"], "WT0": x["L0_gnn_W1"].T, "W1": x["L0_gnn_W2"], "WT1": x["L0_gnn_W2"].T,
        "a0_src": x["L0_gnn_a1_src"].reshape(-1, 1), "a0_dst": x["L0_gnn_a1_dst"].reshape(-1, 1),
        "a1_src": x["L0_gnn_a2_src"].reshape(-1, 1), "a1_dst": x["L0_gnn_a2_dst"].reshape(-1, 1),
        "gate_w0": x["L0_ffn_gate_w"], "gate_b0": x["L0_ffn_gate_b"].reshape(1, -1),
        "gate_w1": x["L1_ffn_Wr"], "gate_b1": x["L1_ffn_br"].reshape(1, -1),
        "pack0": expert_pack(0, x["L0_ffn_w1"], x["L0_ffn_b1"], None, None),
        "pack1": expert_pack(1, x["L1_ffn_W1"], x["L1_ffn_b1"], x["L1_ffn_ln_g"], x["L1_ffn_ln_b"]),
        "w2_0": rows_of(x["L0_ffn_w2"]), "w2_1": rows_of(x["L1_ffn_W2"]),
        "b2_0": x["L0_ffn_b2"], "b2_1": x["L1_ffn_b2"],
        "gamma": x["L0_ffn_gamma"].reshape(1, -1), "beta": x["L0_ffn_beta"].reshape(1, -1),
        "Wqkv": x["L1_gnn_W_qkv"], "bqkv": x["L1_gnn_b_qkv"].reshape(1, -1),
        "Wout": x["L1_gnn_W_out"], "bout": x["L1_gnn_b_out"].reshape(1, -1),
    }
    nc = bacc.Bacc("TRN2", target_bir_lowering=False, num_devices=1)
    arrays = {k: np.ascontiguousarray(val) for k, val in arrays.items()}
    t = {k: nc.dram_tensor("in_" + k, val.shape, mybir.dt.from_np(val.dtype), kind="ExternalInput").ap()
         for k, val in arrays.items()}
    t["out"] = nc.dram_tensor("out_0", (N, D), F32, kind="ExternalOutput").ap()
    build(nc, t)
    r = run_bass_kernel_spmd(nc, [{"in_" + k: val for k, val in arrays.items()}], core_ids=[0])
    return r.results[0]["out_0"]
```

```python
from contextlib import ExitStack, contextmanager

import numpy as np

import concourse.bass as bass
from concourse import mybir

F32 = mybir.dt.float32
I32 = mybir.dt.int32
ALU = mybir.AluOpType
ACT = mybir.ActivationFunctionType
AX = mybir.AxisListType.X

N, D, E = 3125, 256, 53125
W = 125
NW = N // W
NV = NW + 1
NT = E // W
G = 10
NB = 46
NP = NB * G
PC = 4
PQ = NP // PC
HEAD = W
FAR = -3.0e38
MAGIC = 12582912.0
EPS = 1e-5
KC = D // 128
assert NP >= NT + NW - 1 and NB % 2 == 0 and NP % PC == 0 and NV % 2 == 0

FFN = [dict(E=16, F=512), dict(E=8, F=1024)]
for _f in FFN:
    _f["NBLK"] = (2 * N - _f["E"]) // 128 + _f["E"]
    _f["FC"] = _f["F"] // 128
    _f["ob"] = KC * _f["F"]
    _f["og"] = _f["ob"] + _f["FC"]
    _f["PK"] = _f["og"] + 2 * KC
SLOTS = 128 * max(f["NBLK"] for f in FFN)
ATT = [dict(H=4, ROW=260), dict(H=1, ROW=257), dict(H=8, ROW=512)]


def build(nc, t):
    with ExitStack() as top:
        def sb(name, shape, dt=F32, stack=top):
            return stack.enter_context(nc.sbuf_tensor(name, shape, dt))

        sems = [[]]

        def sem(name):
            sems[-1].append(nc.alloc_semaphore(name=name))
            return sems[-1][-1]

        def gather_sem(name):
            return top.enter_context(nc.semaphore(name))

        @contextmanager
        def phase():
            sems.append([])
            with ExitStack() as ph:
                yield ph
            mine = sems.pop()
            if mine:
                with nc.Block() as clear:
                    @clear.gpsimd
                    def _(pool):
                        for s in mine:
                            pool.sem_clear(s)
            for s in mine:
                nc.release_semaphore(s)

        v, a, g = nc.vector, nc.scalar, nc.gpsimd

        gate_tab = nc.dram_tensor("gate_tab", (NP, W + 1), F32).ap()
        code_tab = nc.dram_tensor("code_tab", (NP, W), F32).ap()
        srcs_tab = nc.dram_tensor("srcs_tab", (NB, W, G), I32).ap()
        row_tab = [nc.dram_tensor(f"row_tab{l}", (NV * W, ATT[l]["ROW"]), F32).ap() for l in range(3)]
        head_tab = [nc.dram_tensor(f"head_tab{l}", (NP, D + 2 * ATT[l]["H"]), F32).ap() for l in range(3)]
        xs_tab = nc.dram_tensor("xs_tab", (SLOTS, D), F32).ap()
        ys_tab = nc.dram_tensor("ys_tab", (SLOTS, D), F32).ap()

        xcur = sb("xcur", [W, NV, D])
        z = sb("z", [W, NV, D])
        ident = sb("ident", [128, 128])
        ones = sb("ones", [128, 128])
        iota_row = sb("iota_row", [128, 128])
        iota_col = sb("iota_col", [128, 1])
        iota_neg = sb("iota_neg", [128, 1])
        mcode = sb("mcode", [W, NP])
        first = sb("first", [W, NP])
        wtab = sb("wtab", [1, NP], I32)
        hdst = sb("hdst", [PQ, PC])
        hfirst = sb("hfirst", [PQ, PC])
        hgate = sb("hgate", [8, NP + 1])
        stats = sb("stats", [W, NV, 6])
        mean = sb("mean", [W, NV])
        rstd = sb("rstd", [W, NV])
        lt = [sb(f"lt{k}", [W, NV]) for k in range(3)]
        dwin = sb("dwin", [W, NV, 4])

        def vd(_):
            v.drain()

        def mm(*args, **kw):
            return nc.tensor.matmul(*args, **kw)

        with phase() as ph:
            def ps(name, shape):
                return ph.enter_context(nc.psum_tensor(name, shape, F32))

            ends_i = sb("ends_i", [1, 2, NT], I32, ph)
            ends = sb("ends", [1, 2, NT], F32, ph)
            low = sb("low", [1, 2, NT], F32, ph)
            span = sb("span", [1, NT], F32, ph)
            zrow = sb("zrow", [1, NT], F32, ph)
            stair = sb("stair", [1, 2, NT], F32, ph)
            tnum = sb("tnum", [1, NT], F32, ph)
            bnum = sb("bnum", [PQ, PC], F32, ph)
            mask = sb("mask", [PQ, NT], F32, ph)
            tmpn = sb("tmpn", [PQ, NT], F32, ph)
            cnt = sb("cnt", [PQ, PC], F32, ph)
            bfirst = sb("bfirst", [PQ, PC], F32, ph)
            wlow = sb("wlow", [PQ, PC], F32, ph)
            wb = sb("wb", [PQ, PC], F32, ph)
            w125 = sb("w125", [PQ, PC], F32, ph)
            tb_i = sb("tb_i", [PQ, PC], I32, ph)
            er_i = sb("er_i", [PQ, PC, 256], I32, ph)
            er = sb("er", [PQ, PC, 256], F32, ph)
            gate = sb("gate", [PQ, PC, W + 1], F32, ph)
            st = sb("st", [PQ, PC, W], F32, ph)
            hd = sb("hd", [PQ, PC, W], F32, ph)
            dl = sb("dl", [PQ, PC, W], F32, ph)
            inw = sb("inw", [PQ, PC, W], F32, ph)
            dco = sb("dco", [PQ, PC, W], F32, ph)
            mco = sb("mco", [PQ, PC, W], F32, ph)
            u = sb("u", [PQ, PC, W], F32, ph)
            hv = sb("hv", [PQ, PC], F32, ph)
            hrow = sb("hrow", [8, NP + 1], F32, ph)
            hr2 = sb("hr2", [8, NP + 1], F32, ph)
            srcp = sb("srcp", [W, NP], I32, ph)
            zero = sb("zero", [128, 4096], F32, ph)
            p_b = ps("p_b", [PQ, 2, 512])
            p_t = [ps(f"p_t{k}", [W, 512]) for k in range(3)]
            p_w = ps("p_w", [1, 512])
            p_h = ps("p_h", [8, 512])
            s_in = sem("a_in")
            s_const = sem("a_const")
            s_stair = sem("a_stair")
            s_bc = sem("a_bc")
            s_tb = sem("a_tb")
            s_er = gather_sem("a_er")
            s_rows = sem("a_rows")
            s_tr = sem("a_tr")
            s_trd = sem("a_trd")
            s_cols = sem("a_cols")
            s_out = sem("a_out")
            s_hf = sem("a_hf")
            s_zero = sem("a_zero")
            block = ph.enter_context(nc.Block())

            @block.sync
            def _(sp):
                for k in range(2):
                    sp.dma_start(ends_i[0:1, k, :], t["ends"][k:k + 1, :]).then_inc(s_in, 16)
                sp.dma_start(xcur[:, 0:NW, :], t["x"].rearrange("(w p) d -> p w d", p=W)).then_inc(s_in, 16)
                sp.wait_ge(s_zero, 1)
                for k in range(SLOTS * D // (128 * 4096)):
                    sp.dma_start(xs_tab.rearrange("(k p r) d -> k p (r d)", p=128, r=4096 // D)[k],
                                 zero[:]).then_inc(s_out, 16)
                sp.wait_ge(s_rows, 1)
                sp.dma_start(gate_tab.rearrange("(c p) e -> p c e", p=PQ), gate[:]).then_inc(s_out, 16)
                sp.dma_start(code_tab.rearrange("(c p) e -> p c e", p=PQ), dco[:]).then_inc(s_out, 16)
                sp.wait_ge(s_cols, 1)
                sp.dma_start(srcs_tab.rearrange("n p g -> p n g"),
                             srcp[:].rearrange("p (n g) -> p n g", g=G)).then_inc(s_out, 16)
                sp.wait_ge(s_out, 16 * (3 + SLOTS * D // (128 * 4096)))

            @block.gpsimd
            def _(pool):
                g.memset(ones[:], 1.0).then_inc(s_const, 1)
                pool.wait_ge(s_const, 1)
                g.affine_select(out=ident[:], in_=ones[:], compare_op=ALU.is_equal, fill=0.0, base=0,
                                pattern=[[-1, 128]], channel_multiplier=1).then_inc(s_const, 1)
                g.iota(iota_row[:], pattern=[[1, 128]], base=0, channel_multiplier=0,
                       allow_small_or_imprecise_dtypes=True).then_inc(s_const, 1)
                g.iota(iota_col[:], pattern=[[1, 1]], base=0, channel_multiplier=1,
                       allow_small_or_imprecise_dtypes=True).then_inc(s_const, 1)
                g.iota(tnum[:], pattern=[[1, NT]], base=0, channel_multiplier=0,
                       allow_small_or_imprecise_dtypes=True).then_inc(s_const, 1)
                g.iota(bnum[:], pattern=[[PQ, PC]], base=0, channel_multiplier=1,
                       allow_small_or_imprecise_dtypes=True).then_inc(s_const, 1)
                pool.wait_ge(s_tb, 1)
                for c in range(PC):
                    g.indirect_dma_start(out=er_i[:, c, :], out_offset=None, in_=t["edges"],
                                         in_offset=bass.IndirectOffsetOnAxis(ap=tb_i[:, c:c + 1], axis=0)
                                         ).then_inc(s_er, 16)
                pool.wait_ge(s_er, 16 * PC)

            @block.tensor
            def _(pe):
                pe.wait_ge(s_const, 6)
                pe.wait_ge(s_stair, 1)
                for k in range(2):
                    last = mm(p_b[:, k, 0:NT], ones[0:1, 0:PQ], stair[0:1, k, :], start=True, stop=True)
                last.then_inc(s_bc, 1)
                pe.wait_ge(s_rows, 1)
                for c in range(PC):
                    for k, (out, src) in enumerate(((p_t[0], mco[:, c, :]), (p_t[1], st[:, c, :]),
                                                    (p_t[2], er[:, c, W + 2:2 * W + 2]))):
                        nc.tensor.transpose(out[:, c * PQ:(c + 1) * PQ], src, ident[0:PQ, 0:PQ])
                    nc.tensor.transpose(p_w[:, c * PQ:(c + 1) * PQ], wb[:, c:c + 1], ident[0:PQ, 0:PQ])
                    last = mm(p_h[:, c * PQ:(c + 1) * PQ], hdst[:, c:c + 1].to_broadcast([PQ, 8]),
                              ident[0:PQ, 0:PQ], start=True, stop=True)
                last.then_inc(s_tr, 1)
                pe.wait_ge(s_hf, 1)
                for c in range(PC):
                    last = nc.tensor.transpose(p_b[:, 0, c:c + 1], hr2[0:1, c * PQ:(c + 1) * PQ],
                                               ident[0:1, 0:1])
                last.then_inc(s_trd, 1)

            @block.vector
            def _(dve):
                v.memset(zero[:], 0.0)
                v.drain().then_inc(s_zero, 1)
                v.memset(xcur[:, NW, :], 0.0)
                vd(v.memset(zrow[:], 0.0))
                dve.wait_ge(s_in, 48)
                dve.wait_ge(s_const, 6)
                v.tensor_scalar(iota_neg[:], iota_col[:], -1.0, None, ALU.mult)
                vd(v.tensor_copy(ends[:], ends_i[:]))
                vd(v.tensor_scalar(low[:], ends[:], -(W // 2) * 1.0, 1.0 / W, ALU.add, ALU.mult))
                vd(v.tensor_scalar(ends[:], low[:], MAGIC, None, ALU.add))
                vd(v.tensor_scalar(low[:], ends[:], MAGIC, None, ALU.subtract))
                vd(v.tensor_tensor(span[:], low[0:1, 1, :], low[0:1, 0, :], ALU.subtract))
                vd(v.tensor_tensor_scan(out=stair[0:1, 0, :], data0=span[:], data1=zrow[:], initial=0.0,
                                        op0=ALU.add, op1=ALU.add))
                vd(v.tensor_tensor(stair[0:1, 0, :], stair[0:1, 0, :], span[:], ALU.subtract))
                vd(v.tensor_tensor(stair[0:1, 0, :], stair[0:1, 0, :], tnum[:], ALU.add))
                v.tensor_copy(stair[0:1, 1, :], low[0:1, 0, :])
                v.drain().then_inc(s_stair, 1)
                dve.wait_ge(s_bc, 1)
                for c in range(PC):
                    vd(v.tensor_scalar(mask[:], p_b[:, 0, 0:NT], bnum[:, c:c + 1], None, ALU.is_le))
                    v.tensor_reduce(cnt[:, c:c + 1], mask[:], AX, ALU.add)
                    vd(v.tensor_tensor(tmpn[:], mask[:], p_b[:, 0, 0:NT], ALU.mult))
                    vd(v.tensor_reduce(bfirst[:, c:c + 1], tmpn[:], AX, ALU.max))
                    vd(v.tensor_tensor(tmpn[:], mask[:], p_b[:, 1, 0:NT], ALU.mult))
                    vd(v.tensor_reduce(wlow[:, c:c + 1], tmpn[:], AX, ALU.max))
                v.tensor_scalar(tb_i[:], cnt[:], -1.0, None, ALU.add)
                v.drain().then_inc(s_tb, 1)
                vd(v.tensor_tensor(wb[:], wlow[:], bnum[:], ALU.add))
                vd(v.tensor_tensor(wb[:], wb[:], bfirst[:], ALU.subtract))
                vd(v.tensor_scalar(wb[:], wb[:], float(NW), None, ALU.min))
                vd(v.tensor_scalar(w125[:], wb[:], float(W), None, ALU.mult))
                dve.wait_ge(s_er, 16 * PC)
                vd(v.tensor_copy(er[:], er_i[:]))
                v.memset(gate[:], FAR)
                dst = er[:, :, 1:W + 1]
                vd(v.tensor_tensor(st[:], dst, er[:, :, 0:W], ALU.not_equal))
                vd(v.tensor_scalar(gate[:, :, 0:W], st[:], FAR, None, ALU.mult))
                v.memset(st[:, :, 0:1], 1.0)
                vd(v.tensor_tensor(hd[:], dst, er[:, :, 0:1].to_broadcast([PQ, PC, W]), ALU.is_equal))
                vd(v.tensor_tensor(dl[:], dst, w125[:].unsqueeze(2).to_broadcast([PQ, PC, W]), ALU.subtract))
                vd(v.tensor_scalar(u[:], dl[:], 0.0, None, ALU.is_ge))
                vd(v.tensor_scalar(inw[:], dl[:], W - 1.0, None, ALU.is_le))
                vd(v.tensor_tensor(inw[:], inw[:], u[:], ALU.mult))
                vd(v.tensor_scalar(dco[:], dl[:], 1.0, None, ALU.add))
                vd(v.tensor_tensor(dco[:], dco[:], inw[:], ALU.mult))
                vd(v.tensor_scalar(dco[:], dco[:], -1.0, None, ALU.add))
                vd(v.tensor_scalar(u[:], dl[:], -1.0, float(HEAD), ALU.mult, ALU.add))
                vd(v.tensor_tensor(u[:], u[:], hd[:], ALU.mult))
                vd(v.tensor_tensor(u[:], u[:], inw[:], ALU.mult))
                vd(v.tensor_tensor(mco[:], dco[:], u[:], ALU.add))
                vd(v.tensor_tensor(hv[:], hd[:, :, 0], inw[:, :, 0], ALU.mult))
                vd(v.tensor_scalar(hdst[:], er[:, :, 0], 1.0, None, ALU.add))
                vd(v.tensor_tensor(hdst[:], hdst[:], hv[:], ALU.mult))
                v.tensor_scalar(hdst[:], hdst[:], -1.0, None, ALU.add)
                v.drain().then_inc(s_rows, 1)
                v.memset(hrow[:], -2.0)
                vd(v.memset(hr2[:], 1.0))
                dve.wait_ge(s_tr, 1)
                v.tensor_copy(mcode[:], p_t[0][:, 0:NP])
                v.tensor_copy(first[:], p_t[1][:, 0:NP])
                v.tensor_copy(srcp[:], p_t[2][:, 0:NP])
                v.tensor_copy(wtab[:], p_w[:, 0:NP])
                v.tensor_copy(hrow[:, 1:NP + 1], p_h[:, 0:NP])
                v.drain().then_inc(s_cols, 1)
                vd(v.tensor_tensor(hr2[:, 0:NP], hrow[:, 1:NP + 1], hrow[:, 0:NP], ALU.not_equal))
                v.tensor_scalar(hgate[:], hr2[:], FAR, None, ALU.mult)
                v.drain().then_inc(s_hf, 1)
                dve.wait_ge(s_trd, 1)
                v.tensor_copy(hfirst[:], p_b[:, 0, 0:PC])

        def norm_stats(dve, src, s_var, s_std):
            with dve.Fori(0, NV) as w:
                v.bn_stats(stats[:, bass.ds(w, 1), :].rearrange("p a b -> p (a b)"),
                           src[:, bass.ds(w, 1), :].rearrange("p a b -> p (a b)"))
            v.drain()
            v.tensor_tensor(mean[:], stats[:, :, 1], stats[:, :, 4], ALU.add)
            v.tensor_tensor(lt[0][:], stats[:, :, 1], stats[:, :, 4], ALU.subtract)
            vd(v.tensor_tensor(lt[1][:], stats[:, :, 2], stats[:, :, 5], ALU.add))
            v.tensor_scalar(mean[:], mean[:], 0.5, None, ALU.mult)
            vd(v.tensor_scalar(lt[2][:], lt[0][:], 0.25, None, ALU.mult))
            vd(v.tensor_tensor(lt[0][:], lt[0][:], lt[2][:], ALU.mult))
            vd(v.tensor_scalar(lt[1][:], lt[1][:], 1.0 / D, EPS, ALU.mult, ALU.add))
            v.tensor_tensor(lt[0][:], lt[0][:], lt[1][:], ALU.add)
            v.drain().then_inc(s_var, 1)
            dve.wait_ge(s_std, 1)
            vd(v.reciprocal(rstd[:], lt[2][:]))

        def norm_apply(dve, src, dst):
            with dve.Fori(0, NV) as w:
                v.tensor_scalar(dst[:, bass.ds(w, 1), :].rearrange("p a b -> p (a b)"),
                                src[:, bass.ds(w, 1), :].rearrange("p a b -> p (a b)"),
                                mean[:, bass.ds(w, 1)], rstd[:, bass.ds(w, 1)],
                                ALU.subtract, ALU.mult)
            v.drain()

        def norm_sqrt(act, s_var, s_std):
            act.wait_ge(s_var, 1)
            a.activation(lt[2][:], lt[0][:], ACT.Sqrt).then_inc(s_std, 1)

        def sem2(name):
            return [sem(f"{name}{k}") for k in range(2)]

        def project(name, src, cols, loads, wt, emit, norm=False, dve_first=None, pe_first=None,
                    rows=None, row_dram=None, frees=None):
            nb = (cols + 511) // 512
            with phase() as ph:
                slot = sb(name + "slot", [W, 2, D], F32, ph)
                tr = sb(name + "tr", [128, 2, KC, 128], F32, ph)
                p_tr = [ph.enter_context(nc.psum_tensor(f"{name}p_tr{k}", [128, 512], F32)) for k in range(2)]
                p_o = [ph.enter_context(nc.psum_tensor(f"{name}p_o{k}", [128, 512 * nb], F32)) for k in range(2)]
                s_load, s_wts, s_var, s_std = sem(name + "load"), sem(name + "wts"), sem(name + "var"), sem(name + "std")
                s_slot = sem(name + "slot")
                s_turn = sem(name + "turn")
                s_feat = sem(name + "feat")
                s_prod = sem(name + "prod")
                s_emit = sem(name + "emit")
                s_row = sem2(name + "row")
                block = ph.enter_context(nc.Block())

                @block.sync
                def _(sp):
                    for dst, dram in loads:
                        sp.dma_start(dst, dram, allow_slow_non_contiguous=True).then_inc(s_load, 16)
                    if rows is not None:
                        for k in range(2):
                            sp.sem_inc(s_row[k], 16)
                        with sp.Fori(0, NV // 2) as i:
                            for k in range(2):
                                sp.wait_ge(s_emit, i * 2 + k + 3)
                                sp.dma_start(row_dram[bass.ds(i * (2 * W) + k * W, W), :],
                                             rows[k][:]).then_inc(s_row[k], 16)
                        for k in range(2):
                            sp.wait_ge(s_row[k], 16 * (NV // 2 + 1))
                    sp.wait_ge(s_load, 16 * len(loads))

                @block.scalar
                def _(act):
                    act.sem_inc(s_feat, 2)
                    if norm:
                        norm_sqrt(act, s_var, s_std)
                    with act.Fori(0, NV // 2) as i:
                        for k in range(2):
                            act.wait_ge(s_turn, i * 2 + k + 3)
                            act.wait_ge(s_prod, i * 2 + k + 1)
                            a.activation(tr[:, k, :, 0:W],
                                         p_tr[k][:, 0:256].rearrange("p (c w) -> p c w", c=KC)[:, :, 0:W],
                                         ACT.Copy).then_inc(s_feat, 1)

                @block.vector
                def _(dve):
                    dve.sem_inc(s_emit, 2)
                    if dve_first is not None:
                        dve_first(dve, s_load, s_wts, frees)
                    if norm:
                        norm_stats(dve, xcur, s_var, s_std)
                        norm_apply(dve, xcur, z)

                    def fill(j, k):
                        dve.wait_ge(s_turn, j + 1)
                        v.tensor_copy(slot[:, k, :], src[:, bass.ds(j, 1), :].rearrange("p a b -> p (a b)")
                                      ).then_inc(s_slot, 1)

                    def take(j, k):
                        if rows is not None:
                            dve.wait_ge(s_row[k], j * 8 + (16 - 8 * k))
                        dve.wait_ge(s_prod, j + 3)
                        emit(j, k, p_o[k]).then_inc(s_emit, 1)

                    fill(0, 0)
                    fill(1, 1)
                    with dve.Fori(0, NV // 2 - 1) as i:
                        for k in range(2):
                            fill(i * 2 + k + 2, k)
                            take(i * 2 + k, k)
                    take(NV - 2, 0)
                    take(NV - 1, 1)

                @block.tensor
                def _(pe):
                    pe.sem_inc(s_turn, 2)
                    pe.sem_inc(s_prod, 2)
                    pe.wait_ge(s_load, 16 * len(loads))
                    if pe_first is not None:
                        pe_first(pe, frees)
                        pe.wait_ge(s_wts, 1)

                    def turn(j, k):
                        pe.wait_ge(s_slot, j + 1)
                        pe.wait_ge(s_feat, j + 1)
                        for c in range(KC):
                            last = nc.tensor.transpose(p_tr[k][:, c * 128:c * 128 + W],
                                                       slot[:, k, c * 128:(c + 1) * 128], ident[0:W, 0:W])
                        last.then_inc(s_turn, 1)

                    def product(j, k):
                        pe.wait_ge(s_feat, j + 3)
                        pe.wait_ge(s_emit, j + 1)
                        for b in range(nb):
                            c0, c1 = b * 512, min(cols, b * 512 + 512)
                            for c in range(KC):
                                last = mm(p_o[k][0:W, c0:c1], tr[:, k, c, 0:W], wt[:, c, c0:c1],
                                          start=c == 0, stop=c == KC - 1)
                        last.then_inc(s_prod, 1)

                    turn(0, 0)
                    with pe.Fori(0, NV // 2 - 1) as i:
                        for k in range(2):
                            turn(i * 2 + k + 1, 1 - k)
                            product(i * 2 + k, k)
                    turn(NV - 1, 1)
                    product(NV - 2, 0)
                    product(NV - 1, 1)

        def edges(l, acc, scale):
            H, RW, dots = ATT[l]["H"], D + 2 * ATT[l]["H"], l == 2
            V0 = D if dots else 0
            GW = V0 + RW
            GH = G * H
            K = 2 if dots else 3
            NG = G // 2 if dots else 1
            NZ = 2 if dots else 5
            DONE = (3, 5, 6, 8, 8) if dots else (0, 2, 3, 6, 7)
            TURNS = (G, G) if dots else (4, 8)
            name = f"e{l}_"
            with phase() as ph:
                rowbuf = [sb(f"{name}rowbuf{k}", [W, G, GW], F32, ph) for k in range(K)]
                idx = [sb(f"{name}idx{k}", [W, G], I32, ph) for k in range(K)]
                codet = [sb(f"{name}codet{k}", [W, G * W], F32, ph) for k in range(K)]
                gates = [sb(f"{name}gates{k}", [GH, W + 1], F32, ph) for k in range(K)]
                hot = [sb(f"{name}hot{k}", [W, G, W + 1], F32, ph) for k in range(K)]
                zb = [sb(f"{name}zb{k}", [W + 1, G, RW], F32, ph) for k in range(K)]
                prod = sb(f"{name}prod", [W, 3, 2 * D], F32, ph) if dots else sb(f"{name}prod", [W, GH], F32, ph)
                sc = sb(f"{name}sc", [W, GH], F32, ph)
                df = sb(f"{name}df", [W, GH], F32, ph)
                fw = sb(f"{name}fw", [GH, W], F32, ph)
                mx = sb(f"{name}mx", [GH, W], F32, ph)
                p_q = [ph.enter_context(nc.psum_tensor(f"{name}p_q{k}", [W, 512], F32)) for k in range(NG)]
                p_z = [ph.enter_context(nc.psum_tensor(f"{name}p_z{k}", [W + 1, 512], F32)) for k in range(NZ)]
                p_turn = ph.enter_context(nc.psum_tensor(f"{name}p_turn", [128, 512], F32))
                p_sc, p_m = p_turn[0:GH, 0:W], p_turn[0:W, W:W + GH]
                s_ld = [sem(f"{name}ld{k}") for k in range(K)]
                s_codes = [sem(f"{name}codes{k}") for k in range(K)]
                s_go = sem(name + "go")
                s_seen = sem(name + "seen")
                s_rows = [gather_sem(f"{name}rows{k}") for k in range(K)]
                s_far = sem(name + "far")
                s_codet = sem(name + "codet")
                s_hot = sem(name + "hot")
                s_q = sem(name + "q")
                s_mul = sem(name + "mul")
                s_red = sem(name + "red")
                s_sc = sem(name + "sc")
                s_tsc = sem(name + "tsc")
                s_fw = sem(name + "fw")
                s_mx = sem(name + "mx")
                s_tm = sem(name + "tm")
                s_df = sem(name + "df")
                s_w = sem(name + "w")
                s_wv = sem(name + "wv")
                s_z = sem(name + "z")
                s_zb = sem(name + "zb")
                s_acc = sem(name + "acc")
                s_hs = [sem(f"{name}hs{k}") for k in range(K)]
                block = ph.enter_context(nc.Block())

                def windows_of(engine, n, count=1):
                    return nc.values_load_multi_w_load_instructions(
                        wtab[0:1, bass.ds(n * G, count * G)], engines=[engine], min_val=0, max_val=NW,
                        skip_runtime_bounds_check_because="the table was made with min(., NW) of values >= 0")[1]

                def slot(k, r, more):
                    return (k + more) % K, r + (k + more) // K

                def over(engine, lo, hi, step):
                    turns = (hi - lo) // K
                    with engine.Fori(0, turns) as i:
                        for k in range(K):
                            step(i * K + (lo + k), *slot(lo % K, i + lo // K, k))
                    for n in range(lo + turns * K, hi):
                        step(n, n % K, n // K)

                @block.sync
                def _(sp):
                    def load(n, k, r):
                        sp.wait_ge(s_q, n * NG + NG)
                        sp.dma_start(codet[k][:],
                                     code_tab[bass.ds(n * G, G), :].rearrange("(o g) e -> o (g e)", o=1)
                                     .to_broadcast([W, G * W])).then_inc(s_codes[k], 16)
                        sp.wait_ge(s_mx, n + 1)
                        sp.dma_start(idx[k][:], srcs_tab[bass.ds(n, 1)].rearrange("a p g -> (a p) g")
                                     ).then_inc(s_ld[k], 16)
                        sp.dma_start(gates[k][:],
                                     gate_tab[bass.ds(n * G, G), :].unsqueeze(1)
                                     .to_broadcast([G, H, W + 1])).then_inc(s_ld[k], 16)
                    over(sp, 0, NB, load)

                @block.gpsimd
                def _(pool):
                    def gather(n, k, r):
                        pool.wait_ge(s_ld[k], r * 32 + 32)
                        for q in range(G):
                            pool.wait_ge(s_z, n * G + (q + 1))
                            pool.sem_inc(s_go, 1)
                            g.indirect_dma_start(
                                out=rowbuf[k][:, q, 0:ATT[l]["ROW"]], out_offset=None, in_=row_tab[l],
                                in_offset=bass.IndirectOffsetOnAxis(ap=idx[k][:, q:q + 1], axis=0)
                            ).then_inc(s_rows[k], 16)
                    over(pool, 0, NB, gather)

                @block.scalar
                def _(act):
                    act.sem_inc(s_zb, NZ)
                    for k in range(K):
                        act.sem_inc(s_hs[k], 16)

                    def code_t(n, k, r):
                        act.wait_ge(s_codes[k], r * 16 + 16)
                        a.activation(codet[k][:], codet[k][:], ACT.Abs, bias=iota_neg[0:W, :]).then_inc(s_far, 1)
                        act.wait_ge(s_far, n + 1)
                        a.activation(codet[k][:], codet[k][:], ACT.Relu, scale=-1.0, bias=ones[0:W, 0:1]
                                     ).then_inc(s_codet, 1)

                    def weigh(n, k):
                        act.wait_ge(s_df, n + 1)
                        a.activation(rowbuf[k][:, :, V0 + D:V0 + D + H],
                                     df[:].rearrange("p (g h) -> p g h", h=H),
                                     ACT.Exp, scale=scale).then_inc(s_w, 1)

                    def batch(n, k, r, codes=True, ahead=True):
                        if codes:
                            code_t(n + 2, *slot(k, r, 2))
                        act.wait_ge(s_hs[k], r * 16 + 16)
                        for q in range(G):
                            if ahead and q == DONE[3]:
                                weigh(n + 1, (k + 1) % K)
                            act.wait_ge(s_z, n * G + (q + 1 + K * G))
                            act.wait_ge(s_acc, n * G + (q + 1))
                            a.activation(zb[k][:, q, :], p_z[q % NZ][:, 0:RW], ACT.Copy).then_inc(s_zb, 1)
                        act.wait_ge(s_zb, n * G + (G + NZ))
                        act.dma_start(head_tab[l][bass.ds(n * G, G), :].rearrange("(o g) r -> o g r", o=1),
                                      zb[k][HEAD:HEAD + 1, :, :]).then_inc(s_hs[k], 16)

                    code_t(0, 0, 0)
                    code_t(1, 1, 0)
                    weigh(0, 0)
                    over(act, 0, NB - 2, batch)
                    batch(NB - 2, (NB - 2) % K, (NB - 2) // K, codes=False)
                    batch(NB - 1, (NB - 1) % K, (NB - 1) // K, codes=False, ahead=False)
                    for k in range(K):
                        act.wait_ge(s_hs[k], 16 * (1 + len(range(k, NB, K))))

                @block.tensor
                def _(pe):
                    pe.sem_inc(s_z, K * G)
                    pe.sem_inc(s_q, K * NG)

                    def spread(n, k):
                        wins = windows_of(mybir.EngineType.PE, n)
                        pe.wait_ge(s_codet, n + 1)
                        if dots:
                            for q in range(NG):
                                pe.wait_ge(s_mul, n * NG + (q + 1))
                                for r in range(2):
                                    last = mm(p_q[q][:, r * D:(r + 1) * D],
                                              codet[k][:, (2 * q + r) * W:(2 * q + r + 1) * W],
                                              z[:, bass.ds(wins[2 * q + r], 1), :].rearrange("p a b -> p (a b)"),
                                              start=True, stop=True)
                                last.then_inc(s_q, 1)
                        else:
                            pe.wait_ge(s_sc, n + 1)
                            for q in range(G):
                                last = mm(p_q[0][:, q * H:(q + 1) * H], codet[k][:, q * W:(q + 1) * W],
                                          dwin[:, bass.ds(wins[q], 1), 0:H].rearrange("p a b -> p (a b)"),
                                          start=True, stop=True)
                            last.then_inc(s_q, 1)

                    def turn_scores(n):
                        pe.wait_ge(s_sc, n + 2)
                        pe.sem_inc(s_seen, 1)
                        nc.tensor.transpose(p_sc, sc[:], ident[0:W, 0:W]).then_inc(s_tsc, 1)

                    def turn_maxima(n):
                        pe.wait_ge(s_mx, n + (1 + K))
                        pe.sem_inc(s_seen, 1)
                        nc.tensor.transpose(p_m, mx[:], ident[0:GH, 0:GH]).then_inc(s_tm, 1)

                    def batch(n, k, r, ahead=True):
                        if ahead:
                            spread(n + 1, (k + 1) % K)
                        pe.wait_ge(s_hot, n * G + G)
                        for q in range(G + 1):
                            if ahead and q == TURNS[0]:
                                turn_scores(n + 1)
                            if ahead and q == TURNS[1]:
                                turn_maxima(n + 1)
                            if q in (0, G // 2):
                                pe.wait_ge(s_wv, n * 2 + (1 + q * 2 // G))
                            if q < G:
                                pe.wait_ge(s_zb, n * G + (q + 1))
                                mm(p_z[q % NZ][:, 0:RW], hot[k][:, q, :], rowbuf[k][:, q, V0:V0 + RW],
                                   start=True, stop=True).then_inc(s_z, 1)

                    spread(0, 0)
                    turn_scores(0)
                    turn_maxima(0)
                    over(pe, 0, NB - 1, batch)
                    batch(NB - 1, (NB - 1) % K, (NB - 1) // K, ahead=False)

                @block.vector
                def _(dve):
                    v.memset(acc[:], 0.0).then_inc(s_acc, K * G)
                    dve.sem_inc(s_mul, NG)
                    dve.sem_inc(s_sc, 1)
                    dve.sem_inc(s_mx, K)

                    def one_hot(n, k, q):
                        v.tensor_scalar(hot[k][:, q, :], iota_row[0:W, 0:W + 1], mcode[:, bass.ds(n * G + q, 1)],
                                        None, ALU.is_equal).then_inc(s_hot, 1)

                    def add_up(n, k, q, wins, ahead):
                        into = acc[:, bass.ds(wins[q], 1), :].rearrange("p a b -> p (a b)")
                        dve.wait_ge(s_zb, n * G + (q + 1 + NZ))
                        dve.wait_ge(s_acc, n * G + (q + K * G))
                        v.tensor_tensor(into, into, zb[k][:, q, :], ALU.add).then_inc(s_acc, 1)
                        if ahead:
                            one_hot(n + K, k, q)

                    def multiply(n, k, q):
                        if q >= 3:
                            dve.wait_ge(s_red, n * NG + (q - 2))
                        dve.wait_ge(s_q, n * NG + (q + 1 + K * NG))
                        v.tensor_tensor(prod[:, q % 3, :].rearrange("p (r d) -> p r d", r=2),
                                        rowbuf[k][:, 2 * q:2 * q + 2, 0:D],
                                        p_q[q][:].rearrange("p (r d) -> p r d", r=2),
                                        ALU.mult).then_inc(s_mul, 1)

                    def batch(n, k, r, wins=None, ahead=True):
                        def add_before(lo, hi):
                            if wins is not None:
                                for q in range(lo, hi):
                                    add_up(n - 1, (k - 1) % K, q, wins, ahead)

                        dve.wait_ge(s_rows[k], r * (16 * G) + 16 * G)
                        if dots:
                            multiply(n, k, 0)
                            for q in range(NG):
                                if q + 1 < NG:
                                    multiply(n, k, q + 1)
                                dve.wait_ge(s_mul, n * NG + (q + 1 + NG))
                                v.tensor_reduce(sc[:, 2 * H * q:2 * H * (q + 1)],
                                                prod[:, q % 3, :].rearrange("p (h d) -> p h d", d=D // H),
                                                AX, ALU.add).then_inc(s_red, 1)
                                if q >= 2:
                                    add_before(q - 2, q - 1)
                            dve.wait_ge(s_red, n * NG + NG)
                            dve.sem_inc(s_sc, 1)
                        else:
                            dve.wait_ge(s_q, n + (1 + K))
                            v.tensor_tensor(prod[:].rearrange("p (g h) -> p g h", h=H),
                                            rowbuf[k][:, :, D:D + H],
                                            p_q[0][:, 0:GH].rearrange("p (g h) -> p g h", h=H),
                                            ALU.add).then_inc(s_mul, 1)
                            dve.wait_ge(s_mul, n + 2)
                            v.scalar_tensor_tensor(out=sc[:], in0=prod[:], scalar=0.2, in1=prod[:],
                                                   op0=ALU.mult, op1=ALU.max).then_inc(s_sc, 1)
                        add_before(DONE[0], DONE[1])
                        dve.wait_ge(s_tsc, n + 1)
                        dve.wait_ge(s_ld[k], r * 32 + 32)
                        v.tensor_tensor_scan(out=fw[:], data0=gates[k][:, 0:W], data1=p_sc, initial=FAR,
                                             op0=ALU.add, op1=ALU.max).then_inc(s_fw, 1)
                        add_before(DONE[1], DONE[2])
                        dve.wait_ge(s_fw, n + 1)
                        v.tensor_tensor_scan(out=mx[:, ::-1], data0=gates[k][:, 1:W + 1][:, ::-1],
                                             data1=fw[:, ::-1], initial=FAR,
                                             op0=ALU.add, op1=ALU.max).then_inc(s_mx, 1)
                        add_before(DONE[2], DONE[3])
                        dve.wait_ge(s_tm, n + 1)
                        v.tensor_tensor(df[:], sc[:], p_m, ALU.subtract).then_inc(s_df, 1)
                        v.tensor_tensor(rowbuf[k][:, :, V0 + D + H:V0 + RW],
                                        p_m.rearrange("p (g h) -> p g h", h=H),
                                        first[:, bass.ds(n * G, G)].unsqueeze(2).to_broadcast([W, G, H]), ALU.mult)
                        add_before(DONE[3], DONE[4])
                        dve.wait_ge(s_w, n + 1)
                        for half in (slice(0, G // 2), slice(G // 2, G)):
                            rows = rowbuf[k][:, half, V0:V0 + D].rearrange("p g (h d) -> p g h d", h=H)
                            v.tensor_tensor(rows, rows, rowbuf[k][:, half, V0 + D:V0 + D + H].unsqueeze(3)
                                            .to_broadcast([W, G // 2, H, D // H]), ALU.mult).then_inc(s_wv, 1)
                        add_before(DONE[4], G)

                    for k in range(K):
                        for q in range(G):
                            one_hot(k, k, q)
                    batch(0, 0, 0)
                    turns = (NB - K) // K
                    with dve.Fori(0, turns) as i:
                        wins = windows_of(mybir.EngineType.DVE, i * K, K)
                        for k in range(K):
                            batch(i * K + (k + 1), *slot(0, i, k + 1), wins[k * G:(k + 1) * G])
                    for n in range(turns * K + 1, NB):
                        batch(n, n % K, n // K, windows_of(mybir.EngineType.DVE, n - 1), ahead=n - 1 + K < NB)
                    wins = windows_of(mybir.EngineType.DVE, NB - 1)
                    for q in range(G):
                        add_up(NB - 1, (NB - 1) % K, q, wins, False)

        def merge(l, acc, scale, finish):
            H, RW = ATT[l]["H"], D + 2 * ATT[l]["H"]
            name = f"m{l}_"
            with phase() as ph:
                hrows = sb(name + "hrows", [PQ, PC, RW], F32, ph)
                hm = sb(name + "hm", [8, NP], F32, ph)
                hf = sb(name + "hf", [8, NP], F32, ph)
                hr = sb(name + "hr", [PQ, PC, H], F32, ph)
                hx = sb(name + "hx", [PQ, PC, H], F32, ph)
                winof = sb(name + "winof", [PQ, NV], F32, ph)
                oh = sb(name + "oh", [PQ, 2, PC, W], F32, ph)
                acc2 = sb(name + "acc2", [W, NV, RW], F32, ph)
                sm = [sb(f"{name}sm{k}", [W, NW, H], F32, ph) for k in range(5)]
                part = [sb(f"{name}part{k}", [W, 5, D], F32, ph) for k in range(2)]
                p_r = ph.enter_context(nc.psum_tensor(name + "p_r", [8, 512], F32))
                p_c = ph.enter_context(nc.psum_tensor(name + "p_c", [PQ, 512], F32))
                p_w = [ph.enter_context(nc.psum_tensor(f"{name}p_w{k}", [W, 512], F32)) for k in range(2)]
                s_in, s_iota, s_r, s_hm, s_c, s_hx, s_hr, s_hv = [
                    sem(name + n) for n in ("in", "iota", "r", "hm", "c", "hx", "hr", "hv")]
                s_oh = sem(name + "oh")
                s_p = sem(name + "p")
                s_ev = sem(name + "ev")
                s_sh, s_ex = sem(name + "sh"), sem(name + "ex")
                block = ph.enter_context(nc.Block())

                @block.sync
                def _(sp):
                    sp.dma_start(hrows[:], head_tab[l].rearrange("(c p) r -> p c r", p=PQ)).then_inc(s_in, 16)
                    sp.wait_ge(s_in, 16)

                @block.gpsimd
                def _(pool):
                    g.iota(winof[:], pattern=[[W, NV]], base=0, channel_multiplier=0,
                           allow_small_or_imprecise_dtypes=True).then_inc(s_iota, 1)

                @block.tensor
                def _(pe):
                    pe.sem_inc(s_p, 2)
                    pe.wait_ge(s_in, 16)
                    for c in range(PC):
                        last = nc.tensor.transpose(p_r[0:H, c * PQ:(c + 1) * PQ], hrows[:, c, D + H:RW],
                                                   ident[0:PQ, 0:PQ])
                    last.then_inc(s_r, 1)
                    pe.wait_ge(s_hm, 1)
                    for c in range(PC):
                        last = nc.tensor.transpose(p_c[:, c * H:(c + 1) * H], hm[0:H, c * PQ:(c + 1) * PQ],
                                                   ident[0:H, 0:H])
                    last.then_inc(s_c, 1)
                    pe.wait_ge(s_hv, 1)
                    with pe.Fori(0, NV // 2) as i:
                        for k in range(2):
                            pe.wait_ge(s_oh, i * 2 + k + 1)
                            pe.wait_ge(s_ev, i * 2 + k + 1)
                            for c in range(PC):
                                last = mm(p_w[k][:, 0:RW], oh[:, k, c, :], hrows[:, c, :],
                                          start=c == 0, stop=c == PC - 1)
                            last.then_inc(s_p, 1)

                @block.scalar
                def _(act):
                    act.sem_inc(s_ev, 2)
                    act.wait_ge(s_hx, 1)
                    a.activation(hr[:], hx[:], ACT.Exp, scale=scale).then_inc(s_hr, 1)
                    with act.Fori(0, NV // 2) as i:
                        for k in range(2):
                            act.wait_ge(s_p, i * 2 + k + 3)
                            a.activation(acc2[:, bass.ds(i * 2 + k, 1), :].rearrange("p a b -> p (a b)"),
                                         p_w[k][:, 0:RW], ACT.Copy).then_inc(s_ev, 1)
                    act.wait_ge(s_sh, 1)
                    a.activation(sm[0][:], sm[0][:], ACT.Exp, scale=scale)
                    a.activation(sm[1][:], sm[1][:], ACT.Exp, scale=scale).then_inc(s_ex, 1)

                @block.vector
                def _(dve):
                    dve.wait_ge(s_r, 1)
                    vd(v.tensor_copy(hm[0:H, :], p_r[0:H, 0:NP]))
                    vd(v.tensor_tensor_scan(out=hf[0:H, :], data0=hgate[0:H, 0:NP], data1=hm[0:H, :], initial=FAR,
                                            op0=ALU.add, op1=ALU.max))
                    v.tensor_tensor_scan(out=hm[0:H, ::-1], data0=hgate[0:H, 1:NP + 1][:, ::-1],
                                         data1=hf[0:H, ::-1], initial=FAR,
                                         op0=ALU.add, op1=ALU.max).then_inc(s_hm, 1)
                    dve.wait_ge(s_c, 1)
                    dve.wait_ge(s_in, 16)
                    top_m = p_c[:, 0:PC * H].rearrange("p (c h) -> p c h", h=H)
                    v.tensor_tensor(hx[:], hrows[:, :, D + H:RW], top_m, ALU.subtract).then_inc(s_hx, 1)
                    dve.wait_ge(s_hr, 1)
                    v.tensor_tensor(hrows[:, :, D + H:RW], top_m, hfirst[:].unsqueeze(2).to_broadcast([PQ, PC, H]),
                                    ALU.mult)
                    v.tensor_tensor(hrows[:, :, D:D + H], hrows[:, :, D:D + H], hr[:], ALU.mult)
                    body = hrows[:, :, 0:D].rearrange("p c (h d) -> p c h d", h=H)
                    v.tensor_tensor(body, body, hr[:].unsqueeze(3).to_broadcast([PQ, PC, H, D // H]),
                                    ALU.mult).then_inc(s_hv, 1)
                    dve.wait_ge(s_iota, 1)
                    with dve.Fori(0, NV // 2) as i:
                        for k in range(2):
                            dve.wait_ge(s_p, i * 2 + k + 1)
                            for c in range(PC):
                                last = v.tensor_scalar(oh[:, k, c, :], iota_row[0:PQ, 0:W],
                                                       winof[:, bass.ds(i * 2 + k, 1)], hdst[:, c:c + 1],
                                                       ALU.add, ALU.is_equal)
                            last.then_inc(s_oh, 1)
                    dve.wait_ge(s_ev, NV + 2)
                    acc1, ac2 = acc[0:W, 0:NW, :], acc2[:, 0:NW, :]
                    den1, max1 = acc1[:, :, D:D + H], acc1[:, :, D + H:RW]
                    den2, max2 = ac2[:, :, D:D + H], ac2[:, :, D + H:RW]
                    v.tensor_scalar(sm[0][:], den1, 0.0, FAR, ALU.is_equal, ALU.mult)
                    vd(v.tensor_scalar(sm[1][:], den2, 0.0, FAR, ALU.is_equal, ALU.mult))
                    v.tensor_tensor(sm[0][:], sm[0][:], max1, ALU.add)
                    vd(v.tensor_tensor(sm[1][:], sm[1][:], max2, ALU.add))
                    vd(v.tensor_tensor(sm[2][:], sm[0][:], sm[1][:], ALU.max))
                    v.tensor_tensor(sm[0][:], sm[0][:], sm[2][:], ALU.subtract)
                    v.tensor_tensor(sm[1][:], sm[1][:], sm[2][:], ALU.subtract)
                    v.drain().then_inc(s_sh, 1)
                    dve.wait_ge(s_ex, 1)
                    v.tensor_tensor(sm[2][:], sm[0][:], den1, ALU.mult)
                    vd(v.tensor_tensor(sm[3][:], sm[1][:], den2, ALU.mult))
                    vd(v.tensor_tensor(sm[2][:], sm[2][:], sm[3][:], ALU.add))
                    if l < 2:
                        vd(v.tensor_scalar(sm[2][:], sm[2][:], 1e-16, None, ALU.add))
                    else:
                        vd(v.tensor_scalar(sm[2][:], sm[2][:], 1e-30, None, ALU.max))
                    vd(v.reciprocal(sm[4][:], sm[2][:]))
                    v.tensor_tensor(sm[0][:], sm[0][:], sm[4][:], ALU.mult)
                    vd(v.tensor_tensor(sm[1][:], sm[1][:], sm[4][:], ALU.mult))
                    for c in range(0, NW, 5):
                        for k, ac in enumerate((acc1, ac2)):
                            v.tensor_tensor(part[k][:].rearrange("p w (h d) -> p w h d", h=H),
                                            ac[:, c:c + 5, 0:D].rearrange("p w (h d) -> p w h d", h=H),
                                            sm[k][:, c:c + 5, :].unsqueeze(3).to_broadcast([W, 5, H, D // H]),
                                            ALU.mult)
                        v.drain()
                        finish(c, part)
                        v.drain()

        def experts(f, last_layer):
            cf = FFN[f]
            NE, FC, NBLK = cf["E"], cf["FC"], cf["NBLK"]
            name = f"x{f}_"
            with ExitStack() as keep:
                logit = sb(name + "logit", [W, NV, NE], F32, keep)
                wt2 = [sb(f"{name}wt{k}", [W, NW], F32, keep) for k in range(2)]
                pos = [sb(f"{name}pos{k}", [W, NW], I32, keep) for k in range(2)]
                bexp = sb(name + "bexp", [1, NBLK], I32, keep)
                with phase() as ph:
                    gw = sb(name + "gw", [128, KC, NE], F32, ph)
                    gb = sb(name + "gb", [W, NE], F32, ph)
                    project(name + "g_", z, NE,
                            [(gw[:], t[f"gate_w{f}"].rearrange("(c p) e -> p c e", p=128)),
                             (gb[:], t[f"gate_b{f}"].to_broadcast([W, NE]))], gw,
                            lambda j, k, p: v.tensor_tensor(logit[:, bass.ds(j, 1), :].rearrange("p a b -> p (a b)"),
                                                            p[0:W, 0:NE], gb[:], ALU.add), norm=True)
                with phase() as ph:
                    def arr(n, shape=(W, NW, NE)):
                        return sb(name + n, list(shape), F32, ph)
                    lg = logit[:, 0:NW, :]
                    order = arr("order", (W, NE))
                    eq, key, lg2, both, base, rank = [arr(n) for n in ("eq", "key", "lg2", "both", "base", "rank")]
                    oh = [arr("oh0"), arr("oh1")]
                    top1, top2, kmax, dd, ee = [arr(n, (W, NW)) for n in ("top1", "top2", "kmax", "dd", "ee")]
                    colt, reset, run = [arr(n, (W, NE, NW)) for n in ("colt", "reset", "run")]
                    steps = arr("steps", (W, NW))
                    nblk, cend, zer = [arr(n, (W, NE)) for n in ("nblk", "cend", "zer")]
                    lower = arr("lower", (W, W))
                    bnum = arr("bnum", (1, NBLK))
                    bcmp = arr("bcmp", (1, NBLK, NE))
                    bsum = arr("bsum", (1, NBLK))
                    p_rank = ph.enter_context(nc.psum_tensor(name + "p_rank", [W, 512], F32))
                    p_col = ph.enter_context(nc.psum_tensor(name + "p_col", [W, 512], F32))
                    s_const, s_both, s_ranks, s_dd, s_ee, s_pos, s_var, s_std = [
                        sem(name + n) for n in ("const", "both", "ranks", "dd", "ee", "pos", "var", "std")]
                    s_sent = gather_sem(name + "sent")
                    block = ph.enter_context(nc.Block())

                    @block.gpsimd
                    def _(pool):
                        g.iota(order[:], pattern=[[-1, NE]], base=NE, channel_multiplier=0,
                               allow_small_or_imprecise_dtypes=True).then_inc(s_const, 1)
                        g.iota(steps[:], pattern=[[128, NW]], base=0, channel_multiplier=0,
                               allow_small_or_imprecise_dtypes=True).then_inc(s_const, 1)
                        g.iota(bnum[:], pattern=[[1, NBLK]], base=0, channel_multiplier=0,
                               allow_small_or_imprecise_dtypes=True).then_inc(s_const, 1)
                        g.affine_select(out=lower[:], in_=ones[0:W, 0:W], compare_op=ALU.is_ge, fill=0.0, base=-1,
                                        pattern=[[1, W]], channel_multiplier=-1).then_inc(s_const, 1)
                        pool.wait_ge(s_pos, 1)
                        for w in range(NW):
                            for k in range(2):
                                g.indirect_dma_start(out=xs_tab, in_=z[:, w, :], in_offset=None,
                                                     out_offset=bass.IndirectOffsetOnAxis(ap=pos[k][:, w:w + 1], axis=0)
                                                     ).then_inc(s_sent, 16)
                        pool.wait_ge(s_sent, 16 * 2 * NW)

                    @block.tensor
                    def _(pe):
                        pe.wait_ge(s_both, 1)
                        flat = both[:].rearrange("p w e -> p (w e)")
                        mm(p_rank[:, 0:NW * NE], lower[:], flat, start=True, stop=True)
                        mm(p_col[:, 0:NW * NE], ones[0:W, 0:W], flat, start=True, stop=True).then_inc(s_ranks, 1)

                    @block.scalar
                    def _(act):
                        act.wait_ge(s_dd, 1)
                        a.activation(ee[:], dd[:], ACT.Exp).then_inc(s_ee, 1)
                        if f == 1:
                            norm_sqrt(act, s_var, s_std)

                    @block.vector
                    def _(dve):
                        def wide(ap):
                            return ap.unsqueeze(2).to_broadcast([W, NW, NE])

                        def each(ap):
                            return ap.unsqueeze(1).to_broadcast([W, NW, NE])

                        dve.wait_ge(s_const, 4)

                        def pick(src, best, hot):
                            vd(v.tensor_reduce(best[:], src, AX, ALU.max))
                            vd(v.tensor_tensor(eq[:], src, wide(best[:]), ALU.is_equal))
                            vd(v.tensor_tensor(key[:], eq[:], each(order[:]), ALU.mult))
                            vd(v.tensor_reduce(kmax[:], key[:], AX, ALU.max))
                            vd(v.tensor_tensor(hot[:], key[:], wide(kmax[:]), ALU.is_equal))

                        pick(lg, top1, oh[0])
                        vd(v.tensor_scalar(lg2[:], oh[0][:], FAR, None, ALU.mult))
                        vd(v.tensor_tensor(lg2[:], lg2[:], lg, ALU.add))
                        pick(lg2[:], top2, oh[1])
                        vd(v.tensor_tensor(both[:], oh[0][:], oh[1][:], ALU.add))
                        v.tensor_tensor(dd[:], top2[:], top1[:], ALU.subtract)
                        v.drain().then_inc(s_both, 1)
                        dve.sem_inc(s_dd, 1)
                        dve.wait_ge(s_ee, 1)
                        vd(v.tensor_scalar(dd[:], ee[:], 1.0, None, ALU.add))
                        vd(v.reciprocal(wt2[0][:], dd[:]))
                        v.tensor_tensor(wt2[1][:], ee[:], wt2[0][:], ALU.mult)
                        v.memset(reset[:], 1.0)
                        dve.wait_ge(s_ranks, 1)
                        v.tensor_copy(colt[:], p_col[:, 0:NW * NE].rearrange("p (w e) -> p e w", e=NE))
                        v.memset(zer[:], 0.0)
                        v.drain()
                        vd(v.memset(reset[:, :, 0:1], 0.0))
                        vd(v.tensor_tensor_scan(out=run[:].rearrange("p e w -> p (e w)"),
                                                data0=reset[:].rearrange("p e w -> p (e w)"),
                                                data1=colt[:].rearrange("p e w -> p (e w)"), initial=0.0,
                                                op0=ALU.mult, op1=ALU.add))
                        cmp3 = reset[:]
                        vd(v.tensor_tensor(cmp3, run[:, :, NW - 1:NW].to_broadcast([W, NE, NW]),
                                           steps[:].unsqueeze(1).to_broadcast([W, NE, NW]), ALU.is_gt))
                        vd(v.tensor_reduce(nblk[:], cmp3, AX, ALU.add))
                        vd(v.tensor_tensor_scan(out=cend[:], data0=nblk[:], data1=zer[:], initial=0.0,
                                                op0=ALU.add, op1=ALU.add))
                        vd(v.tensor_tensor(zer[:], cend[:], nblk[:], ALU.subtract))
                        vd(v.tensor_scalar(zer[:], zer[:], 128.0, None, ALU.mult))
                        v.tensor_tensor(run[:], run[:], colt[:], ALU.subtract)
                        v.drain()
                        vd(v.tensor_tensor(base[:], run[:].rearrange("p e w -> p w e"), each(zer[:]), ALU.add))
                        vd(v.tensor_tensor(rank[:], base[:],
                                           p_rank[:, 0:NW * NE].rearrange("p (w e) -> p w e", e=NE), ALU.add))
                        for k in range(2):
                            vd(v.tensor_tensor(key[:], rank[:], oh[k][:], ALU.mult))
                            vd(v.tensor_reduce(top1[:], key[:], AX, ALU.add))
                            vd(v.tensor_copy(pos[k][:], top1[:]))
                        vd(v.tensor_tensor(bcmp[:], cend[0:1, :].unsqueeze(1).to_broadcast([1, NBLK, NE]),
                                           bnum[:].unsqueeze(2).to_broadcast([1, NBLK, NE]), ALU.is_le))
                        vd(v.tensor_reduce(bsum[:], bcmp[:], AX, ALU.add))
                        vd(v.tensor_scalar(bexp[:], bsum[:], NE - 1.0, None, ALU.min))
                        if f == 1:
                            norm_stats(dve, z, s_var, s_std)
                            norm_apply(dve, z, z)
                        v.drain().then_inc(s_pos, 1)
                with phase() as ph:
                    pack = [sb(f"{name}pack{k}", [128, cf["PK"]], F32, ph) for k in range(2)]
                    w2 = [sb(f"{name}w2{k}", [128, FC * D], F32, ph) for k in range(2)]
                    b2 = [sb(f"{name}b2{k}", [1, D], F32, ph) for k in range(2)]
                    xb = [sb(f"{name}xb{k}", [128, D], F32, ph) for k in range(2)]
                    xt = [sb(f"{name}xt{k}", [128, KC, 128], F32, ph) for k in range(2)]
                    ht = [sb(f"{name}ht{k}", [128, FC, 128], F32, ph) for k in range(2)]
                    yb = [sb(f"{name}yb{k}", [128, D], F32, ph) for k in range(2)]
                    p_x = [ph.enter_context(nc.psum_tensor(f"{name}p_x{k}", [128, 512], F32)) for k in range(2)]
                    p_h = [ph.enter_context(nc.psum_tensor(f"{name}p_h{k}", [128, max(4, FC), 128], F32)) for k in range(2)]
                    p_y = [ph.enter_context(nc.psum_tensor(f"{name}p_y{k}", [128, 512], F32))
                           for k in range(2)] if FC == 4 else None
                    if p_y is None:
                        p_y = [ph.enter_context(nc.psum_tensor(f"{name}p_y{k}", [128, 512], F32)) for k in range(2)]
                    s_w = sem2(name + "w")
                    s_w2 = sem2(name + "w2")
                    s_xt = sem(name + "xtp")
                    s_xs = sem(name + "xs")
                    s_h = sem(name + "h")
                    s_hs = sem(name + "hs")
                    s_y = sem(name + "y")
                    s_ys = sem(name + "ys")
                    s_st = sem2(name + "st")
                    block = ph.enter_context(nc.Block())

                    @block.sync
                    def _(sp):
                        for k in range(2):
                            sp.sem_inc(s_st[k], 16)

                        def load(b, k):
                            e = sp.value_load(bexp[0:1, bass.ds(b, 1)], min_val=0, max_val=NE - 1)
                            sp.wait_ge(s_h, b * FC + FC)
                            sp.wait_ge(s_hs, b * FC + FC)
                            sp.dma_start(xb[k][:], xs_tab[bass.ds(b * 128, 128), :]).then_inc(s_w[k], 16)
                            sp.dma_start(pack[k][:], t[f"pack{f}"][bass.ds(e, 1)].rearrange("a p c -> (a p) c")
                                         ).then_inc(s_w[k], 16)
                            return e

                        def load2(b, k):
                            e = sp.value_load(bexp[0:1, bass.ds(b, 1)], min_val=0, max_val=NE - 1)
                            sp.wait_ge(s_y, b + 1)
                            sp.dma_start(w2[k][:], t[f"w2_{f}"][bass.ds(e, 1)].rearrange("a p c -> (a p) c")
                                         ).then_inc(s_w2[k], 16)
                            sp.dma_start(b2[k][:], t[f"b2_{f}"][bass.ds(e, 1), :]).then_inc(s_w2[k], 16)

                        def store(b, k):
                            sp.wait_ge(s_ys, b + 3)
                            sp.dma_start(ys_tab[bass.ds(b * 128, 128), :], yb[k][:]).then_inc(s_st[k], 16)

                        for k in range(2):
                            load(k, k)
                            load2(k, k)
                        with sp.Fori(0, NBLK // 2 - 1) as i:
                            for k in range(2):
                                load(i * 2 + k + 2, k)
                                load2(i * 2 + k + 2, k)
                                store(i * 2 + k, k)
                        for k in range(2):
                            store(NBLK - 2 + k, k)
                        for k in range(2):
                            sp.wait_ge(s_st[k], 16 * (NBLK // 2 + 1))
                            sp.wait_ge(s_w[k], 32 * (NBLK // 2))
                            sp.wait_ge(s_w2[k], 32 * (NBLK // 2))

                    @block.tensor
                    def _(pe):
                        pe.sem_inc(s_xt, 2)
                        pe.sem_inc(s_y, 2)
                        pe.sem_inc(s_h, 2 * FC)

                        def hidden(b, k):
                            pe.wait_ge(s_w[k], b * 16 + (32 - 16 * k))
                            pe.wait_ge(s_xs, b + 1)
                            for c in range(KC):
                                last = nc.tensor.transpose(p_x[k][:, c * 128:(c + 1) * 128],
                                                           xb[k][:, c * 128:(c + 1) * 128], ident[:])
                            last.then_inc(s_xt, 1)
                            pe.wait_ge(s_hs, b * FC + FC)
                            pe.wait_ge(s_xs, b + 3)
                            for j in range(FC):
                                for c in range(KC):
                                    o = c * cf["F"] + j * 128
                                    last = mm(p_h[k][:, j, :], pack[k][:, o:o + 128], xt[k][:, c, :],
                                              start=c == 0, stop=c == KC - 1)
                                last.then_inc(s_h, 1)

                        def output(b, k):
                            pe.wait_ge(s_w2[k], b * 16 + (32 - 16 * k))
                            pe.wait_ge(s_ys, b + 1)
                            mm(p_y[k][:, 0:D], ones[0:1, :], b2[k][:], start=True, stop=False)
                            for j in range(FC):
                                pe.wait_ge(s_hs, b * FC + (j + 1 + 2 * FC))
                                last = mm(p_y[k][:, 0:D], ht[k][:, j, :], w2[k][:, j * D:(j + 1) * D],
                                          start=False, stop=j == FC - 1)
                            last.then_inc(s_y, 1)

                        hidden(0, 0)
                        with pe.Fori(0, NBLK // 2 - 1) as i:
                            for k in range(2):
                                hidden(i * 2 + k + 1, 1 - k)
                                output(i * 2 + k, k)
                        hidden(NBLK - 1, 1)
                        output(NBLK - 2, 0)
                        output(NBLK - 1, 1)

                    @block.scalar
                    def _(act):
                        act.sem_inc(s_hs, 2 * FC)
                        with act.Fori(0, NBLK // 2) as i:
                            for k in range(2):
                                act.wait_ge(s_y, i * 2 + k + 1)
                                for j in range(FC):
                                    if j % 4 == 0:
                                        act.wait_ge(s_h, (i * 2 + k) * FC + (j + 4 + 2 * FC))
                                    a.activation(ht[k][:, j, :], p_h[k][:, j, :], ACT.Relu if f == 0 else ACT.Gelu,
                                                 bias=pack[k][:, cf["ob"] + j:cf["ob"] + j + 1]).then_inc(s_hs, 1)

                    @block.vector
                    def _(dve):
                        dve.sem_inc(s_xs, 2)
                        dve.sem_inc(s_ys, 2)

                        def features(b, k):
                            dve.wait_ge(s_xt, b + 3)
                            if f == 0:
                                v.tensor_copy(xt[k][:].rearrange("p c m -> p (c m)"), p_x[k][:, 0:D]).then_inc(s_xs, 1)
                            else:
                                for c in range(KC):
                                    last = v.tensor_scalar(xt[k][:, c, :], p_x[k][:, c * 128:(c + 1) * 128],
                                                           pack[k][:, cf["og"] + c:cf["og"] + c + 1],
                                                           pack[k][:, cf["og"] + KC + c:cf["og"] + KC + c + 1],
                                                           ALU.mult, ALU.add)
                                last.then_inc(s_xs, 1)

                        def result(b, k):
                            dve.wait_ge(s_st[k], b * 8 + (16 - 8 * k))
                            dve.wait_ge(s_y, b + 3)
                            v.tensor_copy(yb[k][:], p_y[k][:, 0:D]).then_inc(s_ys, 1)

                        features(0, 0)
                        with dve.Fori(0, NBLK // 2 - 1) as i:
                            for k in range(2):
                                features(i * 2 + k + 1, 1 - k)
                                result(i * 2 + k, k)
                        features(NBLK - 1, 1)
                        result(NBLK - 2, 0)
                        result(NBLK - 1, 1)
                with phase() as ph:
                    R = 5
                    got = [[sb(f"{name}got{r}_{k}", [W, D], F32, ph) for k in range(2)] for r in range(R)]
                    gb2 = sb(name + "gamma", [W, 2, D], F32, ph)
                    wide = sb(name + "wide", [W, NW, D], F32, ph) if f == 0 else None
                    s_got = [gather_sem(f"{name}got{r}") for r in range(R)]
                    s_used, s_g, s_var, s_std, s_out, s_c = [sem(name + n) for n in ("used", "gam", "var2", "std2", "out", "c")]
                    block = ph.enter_context(nc.Block())

                    @block.gpsimd
                    def _(pool):
                        for w in range(NW):
                            if w >= R:
                                pool.wait_ge(s_used, w - R + 1)
                            for k in range(2):
                                g.indirect_dma_start(out=got[w % R][k][:], out_offset=None, in_=ys_tab,
                                                     in_offset=bass.IndirectOffsetOnAxis(ap=pos[k][:, w:w + 1], axis=0)
                                                     ).then_inc(s_got[w % R], 16)

                    @block.scalar
                    def _(act):
                        if f == 0:
                            norm_sqrt(act, s_var, s_std)

                    @block.vector
                    def _(dve):
                        into = z if f == 0 else xcur
                        c = 0
                        for w in range(NW):
                            dve.wait_ge(s_got[w % R], 32 * (w // R + 1))
                            v.scalar_tensor_tensor(out=into[:, w, :], in0=got[w % R][0][:], scalar=wt2[0][:, w:w + 1],
                                                   in1=into[:, w, :], op0=ALU.mult, op1=ALU.add).then_inc(s_c, 1)
                            dve.wait_ge(s_c, w + 1)
                            v.scalar_tensor_tensor(out=into[:, w, :], in0=got[w % R][1][:], scalar=wt2[1][:, w:w + 1],
                                                   in1=into[:, w, :], op0=ALU.mult, op1=ALU.add).then_inc(s_used, 1)
                        if f == 0:
                            dve.wait_ge(s_g, 32)
                            v.drain()
                            norm_stats(dve, z, s_var, s_std)
                            norm_apply(dve, z, z)
                            vd(v.tensor_tensor(wide[:], z[:, 0:NW, :],
                                               gb2[:, 0:1, :].to_broadcast([W, NW, D]), ALU.mult))
                            v.tensor_tensor(xcur[:, 0:NW, :], xcur[:, 0:NW, :],
                                            gb2[:, 1:2, :].to_broadcast([W, NW, D]), ALU.add)
                            v.drain()
                            v.tensor_tensor(xcur[:, 0:NW, :], xcur[:, 0:NW, :], wide[:], ALU.add)

                    @block.sync
                    def _(sp):
                        if f == 0:
                            for k, n in enumerate(("gamma", "beta")):
                                sp.dma_start(gb2[:, k, :], t[n].to_broadcast([W, D])).then_inc(s_g, 16)
                            sp.wait_ge(s_g, 32)
                        else:
                            sp.wait_ge(s_used, NW)
                            sp.dma_start(t["out"].rearrange("(w p) d -> p w d", p=W), xcur[:, 0:NW, :]).then_inc(s_out, 16)
                            sp.wait_ge(s_out, 16)

        with ExitStack() as gat:
            for l in range(2):
                H, RW = ATT[l]["H"], D + 2 * ATT[l]["H"]
                src = z if l == 0 else None
                with phase() as ph:
                    wnat = sb(f"wnat{l}", [128, KC, D], F32, ph)
                    wts = sb(f"wts{l}", [128, KC, RW], F32, ph)
                    amat = sb(f"amat{l}", [128, KC, 2 * H], F32, ph)
                    rows = [sb(f"grow{l}_{k}", [W, D + H], F32, ph) for k in range(2)]
                    p_a = ph.enter_context(nc.psum_tensor(f"p_a{l}", [128, 512], F32))
                    s_pa, s_am, s_ld2 = sem(f"s_pa{l}"), sem(f"s_am{l}"), sem(f"s_al{l}")

                    def dve_first(dve, s_load, s_wts, _):
                        dve.wait_ge(s_pa, 1)
                        v.tensor_copy(wts[:, :, D:RW], p_a[:, 0:KC * 2 * H].rearrange("p (c h) -> p c h", c=KC))
                        v.drain().then_inc(s_wts, 1)

                    def pe_first(pe, _):
                        for ci in range(KC):
                            for co in range(KC):
                                last = mm(p_a[:, ci * 2 * H:(ci + 1) * 2 * H], wnat[:, co, ci * 128:(ci + 1) * 128],
                                          amat[:, co, :], start=co == 0, stop=co == KC - 1)
                        last.then_inc(s_pa, 1)

                    with nc.Block() as pre:
                        @pre.vector
                        def _(dve):
                            v.memset(amat[:], 0.0)
                            v.drain().then_inc(s_am, 1)

                        @pre.sync
                        def _(sp):
                            sp.wait_ge(s_am, 1)
                            n = 0
                            for k, nm in enumerate(("src", "dst")):
                                for h in range(H):
                                    for o in range(h * (D // H), (h + 1) * (D // H), min(128, D // H)):
                                        m = min(128, D // H)
                                        sp.dma_start(amat[o % 128:o % 128 + m, o // 128, k * H + h:k * H + h + 1],
                                                     t[f"a{l}_{nm}"][o:o + m, :]).then_inc(s_ld2, 16)
                                        n += 1
                            sp.wait_ge(s_ld2, 16 * n)

                    def emit(j, k, p):
                        v.tensor_copy(rows[k][:], p[0:W, 0:D + H])
                        return v.tensor_copy(dwin[:, bass.ds(j, 1), 0:H].rearrange("p a b -> p (a b)"),
                                             p[0:W, D + H:RW])

                    project(f"p{l}_", z, RW,
                            [(wnat[:], t[f"W{l}"].rearrange("(c p) i -> p c i", p=128)),
                             (wts[:, :, 0:D], t[f"WT{l}"].rearrange("(c p) o -> p c o", p=128))], wts, emit,
                            norm=l == 0, dve_first=dve_first, pe_first=pe_first, rows=rows, row_dram=row_tab[l])
                with phase() as ph:
                    acc = sb(f"acc{l}", [W + 1, NV, RW], F32, ph)
                    edges(l, acc, 1.0)

                    def finish(c, part, l=l):
                        if l == 0:
                            vd(v.tensor_tensor(part[0][:], part[0][:], part[1][:], ALU.add))
                            v.tensor_scalar(z[:, c:c + 5, :], part[0][:], 0.0, None, ALU.max)
                        else:
                            vd(v.tensor_tensor(part[0][:], part[0][:], part[1][:], ALU.add))
                            v.tensor_tensor(xcur[:, c:c + 5, :], xcur[:, c:c + 5, :], part[0][:], ALU.add)

                    merge(l, acc, 1.0, finish)

        experts(0, False)

        DH = D // ATT[2]["H"]
        with phase() as ph:
            wq = sb("wq", [128, KC, 3 * D], F32, ph)
            bq = sb("bq", [W, 3 * D], F32, ph)
            rows = [sb(f"kv{k}", [W, 2 * D], F32, ph) for k in range(2)]

            def emit(j, k, p):
                v.tensor_tensor(z[:, bass.ds(j, 1), :].rearrange("p a b -> p (a b)"), p[0:W, 0:D], bq[:, 0:D], ALU.add)
                return v.tensor_tensor(rows[k][:], p[0:W, D:3 * D], bq[:, D:3 * D], ALU.add)

            project("pq_", z, 3 * D,
                    [(wq[:], t["Wqkv"].rearrange("(c p) o -> p c o", p=128)),
                     (bq[:], t["bqkv"].to_broadcast([W, 3 * D]))], wq, emit,
                    norm=True, rows=rows, row_dram=row_tab[2])
        with phase() as ph:
            RW = D + 2 * ATT[2]["H"]
            acc = sb("acc2x", [W + 1, NV, RW], F32, ph)
            edges(2, acc, float(DH) ** -0.5)

            def finish(c, part):
                for w in range(c, c + 5):
                    v.tensor_scalar(z[:, w, :], xcur[:, w, :], mean[:, w:w + 1], rstd[:, w:w + 1],
                                    ALU.subtract, ALU.mult)
                vd(v.tensor_tensor(part[0][:], part[0][:], part[1][:], ALU.add))
                for w in range(5):
                    zz = z[:, c + w, :].rearrange("p (d h) -> p h d", d=DH)
                    v.tensor_tensor(zz, zz, part[0][:, w, :].rearrange("p (h d) -> p h d", d=DH), ALU.add)

            merge(2, acc, float(DH) ** -0.5, finish)
        with phase() as ph:
            wo = sb("wo", [128, KC, D], F32, ph)
            bo = sb("bo", [W, D], F32, ph)

            def add_bias(dve, s_load, s_wts, _):
                dve.wait_ge(s_load, 32)
                v.tensor_tensor(xcur[:], xcur[:], bo[:].unsqueeze(1).to_broadcast([W, NV, D]), ALU.add)
                v.drain().then_inc(s_wts, 1)

            def emit(j, k, p):
                xw = xcur[:, bass.ds(j, 1), :].rearrange("p a b -> p (a b)")
                return v.tensor_tensor(xw, xw, p[0:W, 0:D], ALU.add)

            project("po_", z, D, [(wo[:], t["Wout"].rearrange("(c p) o -> p c o", p=128)),
                                  (bo[:], t["bout"].to_broadcast([W, D]))], wo, emit, dve_first=add_bias)
        experts(1, True)


def kernel(**inputs):
    import concourse.bacc as bacc
    from concourse.bass_utils import run_bass_kernel_spmd

    x = {k: np.asarray(val) for k, val in inputs.items()}
    src, dst = x["src"], x["dst"]
    edges = np.full((NT, 256), -1, dst.dtype)
    edges[:, 1:W + 1] = dst.reshape(NT, W)
    edges[1:, 0] = dst[W - 1:-1:W]
    edges[:-1, W + 1] = dst[W::W]
    edges[:, W + 2:2 * W + 2] = src.reshape(NT, W)

    def expert_pack(f, w1, b1, gain, offset):
        ne = FFN[f]["E"]
        parts = [w1.reshape(ne, KC, 128, -1).transpose(0, 2, 1, 3).reshape(ne, 128, -1),
                 b1.reshape(ne, -1, 128).transpose(0, 2, 1)]
        for col in (gain, offset):
            parts.append(np.zeros((ne, 128, KC), w1.dtype) if col is None
                         else col.reshape(ne, KC, 128).transpose(0, 2, 1))
        return np.ascontiguousarray(np.concatenate(parts, axis=2))

    def rows_of(w2):
        return w2.reshape(len(w2), -1, 128, D).transpose(0, 2, 1, 3).reshape(len(w2), 128, -1)

    arrays = {
        "x": x["x"], "edges": edges, "ends": np.stack([dst[0::W], dst[W - 1::W]]),
        "W0": x["L0_gnn_W1"], "WT0": x["L0_gnn_W1"].T, "W1": x["L0_gnn_W2"], "WT1": x["L0_gnn_W2"].T,
        "a0_src": x["L0_gnn_a1_src"].reshape(-1, 1), "a0_dst": x["L0_gnn_a1_dst"].reshape(-1, 1),
        "a1_src": x["L0_gnn_a2_src"].reshape(-1, 1), "a1_dst": x["L0_gnn_a2_dst"].reshape(-1, 1),
        "gate_w0": x["L0_ffn_gate_w"], "gate_b0": x["L0_ffn_gate_b"].reshape(1, -1),
        "gate_w1": x["L1_ffn_Wr"], "gate_b1": x["L1_ffn_br"].reshape(1, -1),
        "pack0": expert_pack(0, x["L0_ffn_w1"], x["L0_ffn_b1"], None, None),
        "pack1": expert_pack(1, x["L1_ffn_W1"], x["L1_ffn_b1"], x["L1_ffn_ln_g"], x["L1_ffn_ln_b"]),
        "w2_0": rows_of(x["L0_ffn_w2"]), "w2_1": rows_of(x["L1_ffn_W2"]),
        "b2_0": x["L0_ffn_b2"], "b2_1": x["L1_ffn_b2"],
        "gamma": x["L0_ffn_gamma"].reshape(1, -1), "beta": x["L0_ffn_beta"].reshape(1, -1),
        "Wqkv": x["L1_gnn_W_qkv"], "bqkv": x["L1_gnn_b_qkv"].reshape(1, -1),
        "Wout": x["L1_gnn_W_out"], "bout": x["L1_gnn_b_out"].reshape(1, -1),
    }
    nc = bacc.Bacc("TRN2", target_bir_lowering=False, num_devices=1)
    arrays = {k: np.ascontiguousarray(val) for k, val in arrays.items()}
    t = {k: nc.dram_tensor("in_" + k, val.shape, mybir.dt.from_np(val.dtype), kind="ExternalInput").ap()
         for k, val in arrays.items()}
    t["out"] = nc.dram_tensor("out_0", (N, D), F32, kind="ExternalOutput").ap()
    build(nc, t)
    r = run_bass_kernel_spmd(nc, [{"in_" + k: val for k, val in arrays.items()}], core_ids=[0])
    return r.results[0]["out_0"]
```

```python
from contextlib import ExitStack, contextmanager

import numpy as np

import concourse.bass as bass
from concourse import mybir

F32 = mybir.dt.float32
I32 = mybir.dt.int32
ALU = mybir.AluOpType
ACT = mybir.ActivationFunctionType
AX = mybir.AxisListType.X

N, D, E = 3125, 256, 53125
W = 125
NW = N // W
NV = NW + 1
NT = E // W
G = 10
NB = 46
NP = NB * G
PC = 4
PQ = NP // PC
HEAD = W
FAR = -3.0e38
MAGIC = 12582912.0
EPS = 1e-5
KC = D // 128
assert NP >= NT + NW - 1 and NP % PC == 0 and NV % 2 == 0 and NW % 5 == 0

FFN = [dict(E=16, F=512), dict(E=8, F=1024)]
for _f in FFN:
    _f["NBLK"] = (2 * N - _f["E"]) // 128 + _f["E"]
    _f["FC"] = _f["F"] // 128
    _f["ob"] = KC * _f["F"]
    _f["og"] = _f["ob"] + _f["FC"]
    _f["PK"] = _f["og"] + 2 * KC
assert all(_f["NBLK"] % 4 == 0 for _f in FFN)
SLOTS = 128 * max(f["NBLK"] for f in FFN)
ATT = [dict(H=4, ROW=260), dict(H=1, ROW=257), dict(H=8, ROW=512)]


def build(nc, t):
    with ExitStack() as top:
        def sb(name, shape, dt=F32, stack=top):
            return stack.enter_context(nc.sbuf_tensor(name, shape, dt))

        sems = [[]]

        def sem(name):
            sems[-1].append(nc.alloc_semaphore(name=name))
            return sems[-1][-1]

        def gather_sem(name):
            return top.enter_context(nc.semaphore(name))

        @contextmanager
        def phase():
            sems.append([])
            with ExitStack() as ph:
                yield ph
            mine = sems.pop()
            if mine:
                with nc.Block() as clear:
                    @clear.gpsimd
                    def _(pool):
                        for s in mine:
                            pool.sem_clear(s)
            for s in mine:
                nc.release_semaphore(s)

        v, a, g = nc.vector, nc.scalar, nc.gpsimd

        gate_tab = nc.dram_tensor("gate_tab", (NP, W + 1), F32).ap()
        code_tab = nc.dram_tensor("code_tab", (NP, W), F32).ap()
        srcs_tab = nc.dram_tensor("srcs_tab", (NB, W, G), I32).ap()
        row_tab = [nc.dram_tensor(f"row_tab{l}", (NV * W, ATT[l]["ROW"]), F32).ap() for l in range(3)]
        head_tab = [nc.dram_tensor(f"head_tab{l}", (NP, D + 2 * ATT[l]["H"]), F32).ap() for l in range(3)]
        xs_tab = nc.dram_tensor("xs_tab", (SLOTS, D), F32).ap()
        ys_tab = nc.dram_tensor("ys_tab", (SLOTS, D), F32).ap()

        xcur = sb("xcur", [W, NV, D])
        z = sb("z", [W, NV, D])
        ident = sb("ident", [128, 128])
        ones = sb("ones", [128, 128])
        iota_row = sb("iota_row", [128, 128])
        iota_col = sb("iota_col", [128, 1])
        iota_neg = sb("iota_neg", [128, 1])
        mcode = sb("mcode", [W, NP])
        first = sb("first", [W, NP])
        wtab = sb("wtab", [1, NP], I32)
        hdst = sb("hdst", [PQ, PC])
        hfirst = sb("hfirst", [PQ, PC])
        hgate = sb("hgate", [8, NP + 1])
        stats = sb("stats", [W, NV, 6])
        mean = sb("mean", [W, NV])
        rstd = sb("rstd", [W, NV])
        lt = [sb(f"lt{k}", [W, NV]) for k in range(3)]
        dwin = sb("dwin", [W, NV, 4])

        def vd(_):
            v.drain()

        def mm(*args, **kw):
            return nc.tensor.matmul(*args, **kw)

        def slot(k, r, more, K):
            return (k + more) % K, r + (k + more) // K

        def over(engine, lo, hi, K, step):
            turns = (hi - lo) // K
            with engine.Fori(0, turns) as i:
                for k in range(K):
                    step(i * K + (lo + k), *slot(lo % K, i + lo // K, k, K))
            for n in range(lo + turns * K, hi):
                step(n, n % K, n // K)

        with phase() as ph:
            def ps(name, shape):
                return ph.enter_context(nc.psum_tensor(name, shape, F32))

            ends_i = sb("ends_i", [1, 2, NT], I32, ph)
            ends = sb("ends", [1, 2, NT], F32, ph)
            low = sb("low", [1, 2, NT], F32, ph)
            span = sb("span", [1, NT], F32, ph)
            zrow = sb("zrow", [1, NT], F32, ph)
            stair = sb("stair", [1, 2, NT], F32, ph)
            tnum = sb("tnum", [1, NT], F32, ph)
            bnum = sb("bnum", [PQ, PC], F32, ph)
            mask = sb("mask", [PQ, NT], F32, ph)
            tmpn = sb("tmpn", [PQ, NT], F32, ph)
            cnt = sb("cnt", [PQ, PC], F32, ph)
            bfirst = sb("bfirst", [PQ, PC], F32, ph)
            wlow = sb("wlow", [PQ, PC], F32, ph)
            wb = sb("wb", [PQ, PC], F32, ph)
            w125 = sb("w125", [PQ, PC], F32, ph)
            tb_i = sb("tb_i", [PQ, PC], I32, ph)
            er_i = sb("er_i", [PQ, PC, 256], I32, ph)
            er = sb("er", [PQ, PC, 256], F32, ph)
            gate = sb("gate", [PQ, PC, W + 1], F32, ph)
            st = sb("st", [PQ, PC, W], F32, ph)
            hd = sb("hd", [PQ, PC, W], F32, ph)
            dl = sb("dl", [PQ, PC, W], F32, ph)
            inw = sb("inw", [PQ, PC, W], F32, ph)
            dco = sb("dco", [PQ, PC, W], F32, ph)
            mco = sb("mco", [PQ, PC, W], F32, ph)
            u = sb("u", [PQ, PC, W], F32, ph)
            hv = sb("hv", [PQ, PC], F32, ph)
            hrow = sb("hrow", [8, NP + 1], F32, ph)
            hr2 = sb("hr2", [8, NP + 1], F32, ph)
            srcp = sb("srcp", [W, NP], I32, ph)
            zero = sb("zero", [128, 4096], F32, ph)
            p_b = ps("p_b", [PQ, 2, 512])
            p_t = [ps(f"p_t{k}", [W, 512]) for k in range(3)]
            p_w = ps("p_w", [1, 512])
            p_h = ps("p_h", [8, 512])
            s_in = sem("a_in")
            s_const = sem("a_const")
            s_stair = sem("a_stair")
            s_bc = sem("a_bc")
            s_tb = sem("a_tb")
            s_er = gather_sem("a_er")
            s_rows = sem("a_rows")
            s_tr = sem("a_tr")
            s_trd = sem("a_trd")
            s_cols = sem("a_cols")
            s_out = sem("a_out")
            s_hf = sem("a_hf")
            s_zero = sem("a_zero")
            block = ph.enter_context(nc.Block())

            @block.sync
            def _(sp):
                for k in range(2):
                    sp.dma_start(ends_i[0:1, k, :], t["ends"][k:k + 1, :]).then_inc(s_in, 16)
                sp.dma_start(xcur[:, 0:NW, :], t["x"].rearrange("(w p) d -> p w d", p=W)).then_inc(s_in, 16)
                sp.wait_ge(s_zero, 1)
                for k in range(SLOTS * D // (128 * 4096)):
                    sp.dma_start(xs_tab.rearrange("(k p r) d -> k p (r d)", p=128, r=4096 // D)[k],
                                 zero[:]).then_inc(s_out, 16)
                sp.wait_ge(s_rows, 1)
                sp.dma_start(gate_tab.rearrange("(c p) e -> p c e", p=PQ), gate[:]).then_inc(s_out, 16)
                sp.dma_start(code_tab.rearrange("(c p) e -> p c e", p=PQ), dco[:]).then_inc(s_out, 16)
                sp.wait_ge(s_cols, 1)
                sp.dma_start(srcs_tab.rearrange("n p g -> p n g"),
                             srcp[:].rearrange("p (n g) -> p n g", g=G)).then_inc(s_out, 16)
                sp.wait_ge(s_out, 16 * (3 + SLOTS * D // (128 * 4096)))

            @block.gpsimd
            def _(pool):
                g.memset(ones[:], 1.0).then_inc(s_const, 1)
                pool.wait_ge(s_const, 1)
                g.affine_select(out=ident[:], in_=ones[:], compare_op=ALU.is_equal, fill=0.0, base=0,
                                pattern=[[-1, 128]], channel_multiplier=1).then_inc(s_const, 1)
                g.iota(iota_row[:], pattern=[[1, 128]], base=0, channel_multiplier=0,
                       allow_small_or_imprecise_dtypes=True).then_inc(s_const, 1)
                g.iota(iota_col[:], pattern=[[1, 1]], base=0, channel_multiplier=1,
                       allow_small_or_imprecise_dtypes=True).then_inc(s_const, 1)
                g.iota(tnum[:], pattern=[[1, NT]], base=0, channel_multiplier=0,
                       allow_small_or_imprecise_dtypes=True).then_inc(s_const, 1)
                g.iota(bnum[:], pattern=[[PQ, PC]], base=0, channel_multiplier=1,
                       allow_small_or_imprecise_dtypes=True).then_inc(s_const, 1)
                pool.wait_ge(s_tb, 1)
                for c in range(PC):
                    g.indirect_dma_start(out=er_i[:, c, :], out_offset=None, in_=t["edges"],
                                         in_offset=bass.IndirectOffsetOnAxis(ap=tb_i[:, c:c + 1], axis=0)
                                         ).then_inc(s_er, 16)
                pool.wait_ge(s_er, 16 * PC)

            @block.tensor
            def _(pe):
                pe.wait_ge(s_const, 6)
                pe.wait_ge(s_stair, 1)
                for k in range(2):
                    last = mm(p_b[:, k, 0:NT], ones[0:1, 0:PQ], stair[0:1, k, :], start=True, stop=True)
                last.then_inc(s_bc, 1)
                pe.wait_ge(s_rows, 1)
                for c in range(PC):
                    for k, (out, src) in enumerate(((p_t[0], mco[:, c, :]), (p_t[1], st[:, c, :]),
                                                    (p_t[2], er[:, c, W + 2:2 * W + 2]))):
                        nc.tensor.transpose(out[:, c * PQ:(c + 1) * PQ], src, ident[0:PQ, 0:PQ])
                    nc.tensor.transpose(p_w[:, c * PQ:(c + 1) * PQ], wb[:, c:c + 1], ident[0:PQ, 0:PQ])
                    last = mm(p_h[:, c * PQ:(c + 1) * PQ], hdst[:, c:c + 1].to_broadcast([PQ, 8]),
                              ident[0:PQ, 0:PQ], start=True, stop=True)
                last.then_inc(s_tr, 1)
                pe.wait_ge(s_hf, 1)
                for c in range(PC):
                    last = nc.tensor.transpose(p_b[:, 0, c:c + 1], hr2[0:1, c * PQ:(c + 1) * PQ],
                                               ident[0:1, 0:1])
                last.then_inc(s_trd, 1)

            @block.vector
            def _(dve):
                v.memset(zero[:], 0.0)
                v.drain().then_inc(s_zero, 1)
                v.memset(xcur[:, NW, :], 0.0)
                vd(v.memset(zrow[:], 0.0))
                dve.wait_ge(s_in, 48)
                dve.wait_ge(s_const, 6)
                v.tensor_scalar(iota_neg[:], iota_col[:], -1.0, None, ALU.mult)
                vd(v.tensor_copy(ends[:], ends_i[:]))
                vd(v.tensor_scalar(low[:], ends[:], -(W // 2) * 1.0, 1.0 / W, ALU.add, ALU.mult))
                vd(v.tensor_scalar(ends[:], low[:], MAGIC, None, ALU.add))
                vd(v.tensor_scalar(low[:], ends[:], MAGIC, None, ALU.subtract))
                vd(v.tensor_tensor(span[:], low[0:1, 1, :], low[0:1, 0, :], ALU.subtract))
                vd(v.tensor_tensor_scan(out=stair[0:1, 0, :], data0=span[:], data1=zrow[:], initial=0.0,
                                        op0=ALU.add, op1=ALU.add))
                vd(v.tensor_tensor(stair[0:1, 0, :], stair[0:1, 0, :], span[:], ALU.subtract))
                vd(v.tensor_tensor(stair[0:1, 0, :], stair[0:1, 0, :], tnum[:], ALU.add))
                v.tensor_copy(stair[0:1, 1, :], low[0:1, 0, :])
                v.drain().then_inc(s_stair, 1)
                dve.wait_ge(s_bc, 1)
                for c in range(PC):
                    vd(v.tensor_scalar(mask[:], p_b[:, 0, 0:NT], bnum[:, c:c + 1], None, ALU.is_le))
                    v.tensor_reduce(cnt[:, c:c + 1], mask[:], AX, ALU.add)
                    vd(v.tensor_tensor(tmpn[:], mask[:], p_b[:, 0, 0:NT], ALU.mult))
                    vd(v.tensor_reduce(bfirst[:, c:c + 1], tmpn[:], AX, ALU.max))
                    vd(v.tensor_tensor(tmpn[:], mask[:], p_b[:, 1, 0:NT], ALU.mult))
                    vd(v.tensor_reduce(wlow[:, c:c + 1], tmpn[:], AX, ALU.max))
                v.tensor_scalar(tb_i[:], cnt[:], -1.0, None, ALU.add)
                v.drain().then_inc(s_tb, 1)
                vd(v.tensor_tensor(wb[:], wlow[:], bnum[:], ALU.add))
                vd(v.tensor_tensor(wb[:], wb[:], bfirst[:], ALU.subtract))
                vd(v.tensor_scalar(wb[:], wb[:], float(NW), None, ALU.min))
                vd(v.tensor_scalar(w125[:], wb[:], float(W), None, ALU.mult))
                dve.wait_ge(s_er, 16 * PC)
                vd(v.tensor_copy(er[:], er_i[:]))
                v.memset(gate[:], FAR)
                dst = er[:, :, 1:W + 1]
                vd(v.tensor_tensor(st[:], dst, er[:, :, 0:W], ALU.not_equal))
                vd(v.tensor_scalar(gate[:, :, 0:W], st[:], FAR, None, ALU.mult))
                v.memset(st[:, :, 0:1], 1.0)
                vd(v.tensor_tensor(hd[:], dst, er[:, :, 0:1].to_broadcast([PQ, PC, W]), ALU.is_equal))
                vd(v.tensor_tensor(dl[:], dst, w125[:].unsqueeze(2).to_broadcast([PQ, PC, W]), ALU.subtract))
                vd(v.tensor_scalar(u[:], dl[:], 0.0, None, ALU.is_ge))
                vd(v.tensor_scalar(inw[:], dl[:], W - 1.0, None, ALU.is_le))
                vd(v.tensor_tensor(inw[:], inw[:], u[:], ALU.mult))
                vd(v.tensor_scalar(dco[:], dl[:], 1.0, None, ALU.add))
                vd(v.tensor_tensor(dco[:], dco[:], inw[:], ALU.mult))
                vd(v.tensor_scalar(dco[:], dco[:], -1.0, None, ALU.add))
                vd(v.tensor_scalar(u[:], dl[:], -1.0, float(HEAD), ALU.mult, ALU.add))
                vd(v.tensor_tensor(u[:], u[:], hd[:], ALU.mult))
                vd(v.tensor_tensor(u[:], u[:], inw[:], ALU.mult))
                vd(v.tensor_tensor(mco[:], dco[:], u[:], ALU.add))
                vd(v.tensor_tensor(hv[:], hd[:, :, 0], inw[:, :, 0], ALU.mult))
                vd(v.tensor_scalar(hdst[:], er[:, :, 0], 1.0, None, ALU.add))
                vd(v.tensor_tensor(hdst[:], hdst[:], hv[:], ALU.mult))
                v.tensor_scalar(hdst[:], hdst[:], -1.0, None, ALU.add)
                v.drain().then_inc(s_rows, 1)
                v.memset(hrow[:], -2.0)
                vd(v.memset(hr2[:], 1.0))
                dve.wait_ge(s_tr, 1)
                v.tensor_copy(mcode[:], p_t[0][:, 0:NP])
                v.tensor_copy(first[:], p_t[1][:, 0:NP])
                v.tensor_copy(srcp[:], p_t[2][:, 0:NP])
                v.tensor_copy(wtab[:], p_w[:, 0:NP])
                v.tensor_copy(hrow[:, 1:NP + 1], p_h[:, 0:NP])
                v.drain().then_inc(s_cols, 1)
                vd(v.tensor_tensor(hr2[:, 0:NP], hrow[:, 1:NP + 1], hrow[:, 0:NP], ALU.not_equal))
                v.tensor_scalar(hgate[:], hr2[:], FAR, None, ALU.mult)
                v.drain().then_inc(s_hf, 1)
                dve.wait_ge(s_trd, 1)
                v.tensor_copy(hfirst[:], p_b[:, 0, 0:PC])

        def norm_stats(dve, src, s_var, s_std):
            with dve.Fori(0, 2) as i:
                for w in range(NV // 2):
                    window_stats(src, i * (NV // 2) + w)
            norm_moments(dve, s_var, s_std)

        def window_stats(src, w):
            v.bn_stats(stats[:, bass.ds(w, 1), :].rearrange("p a b -> p (a b)"),
                       src[:, bass.ds(w, 1), :].rearrange("p a b -> p (a b)"))

        def norm_moments(dve, s_var, s_std):
            v.drain()
            v.tensor_tensor(mean[:], stats[:, :, 1], stats[:, :, 4], ALU.add)
            v.tensor_tensor(lt[0][:], stats[:, :, 1], stats[:, :, 4], ALU.subtract)
            vd(v.tensor_tensor(lt[1][:], stats[:, :, 2], stats[:, :, 5], ALU.add))
            v.tensor_scalar(mean[:], mean[:], 0.5, None, ALU.mult)
            vd(v.tensor_scalar(lt[2][:], lt[0][:], 0.25, None, ALU.mult))
            vd(v.tensor_tensor(lt[0][:], lt[0][:], lt[2][:], ALU.mult))
            vd(v.tensor_scalar(lt[1][:], lt[1][:], 1.0 / D, EPS, ALU.mult, ALU.add))
            v.tensor_tensor(lt[0][:], lt[0][:], lt[1][:], ALU.add)
            v.drain().then_inc(s_var, 1)
            dve.wait_ge(s_std, 1)
            vd(v.reciprocal(rstd[:], lt[2][:]))

        def norm_apply(dve, src, dst):
            with dve.Fori(0, 2) as i:
                for k in range(NV // 2):
                    w = i * (NV // 2) + k
                    v.tensor_scalar(dst[:, bass.ds(w, 1), :].rearrange("p a b -> p (a b)"),
                                    src[:, bass.ds(w, 1), :].rearrange("p a b -> p (a b)"),
                                    mean[:, bass.ds(w, 1)], rstd[:, bass.ds(w, 1)],
                                    ALU.subtract, ALU.mult)
            v.drain()

        def norm_sqrt(act, s_var, s_std):
            act.wait_ge(s_var, 1)
            a.activation(lt[2][:], lt[0][:], ACT.Sqrt).then_inc(s_std, 1)

        def sem2(name):
            return [sem(f"{name}{k}") for k in range(2)]

        def project(name, src, cols, loads, wt, emit, norm=False, dve_first=None, pe_first=None,
                    rows=None, row_dram=None, frees=None):
            nb = (cols + 511) // 512
            with phase() as ph:
                KP = 4
                win = sb(name + "win", [W, KP, D], F32, ph)
                tr = sb(name + "tr", [128, KP, KC, 128], F32, ph)
                p_tr = [ph.enter_context(nc.psum_tensor(f"{name}p_tr{k}", [128, 512], F32)) for k in range(2)]
                p_o = [ph.enter_context(nc.psum_tensor(f"{name}p_o{k}", [128, 512 * nb], F32)) for k in range(2)]
                s_load, s_wts, s_var, s_std = sem(name + "load"), sem(name + "wts"), sem(name + "var"), sem(name + "std")
                s_slot = sem(name + "slot")
                s_turn = sem(name + "turn")
                s_feat = sem(name + "feat")
                s_prod = sem(name + "prod")
                s_emit = sem(name + "emit")
                s_row = sem2(name + "row")
                block = ph.enter_context(nc.Block())

                @block.sync
                def _(sp):
                    for dst, dram in loads:
                        sp.dma_start(dst, dram, allow_slow_non_contiguous=True).then_inc(s_load, 16)
                    if rows is not None:
                        for k in range(2):
                            sp.sem_inc(s_row[k], 16)
                        with sp.Fori(0, NV // 2) as i:
                            for k in range(2):
                                sp.wait_ge(s_emit, i * 2 + k + 3)
                                sp.dma_start(row_dram[bass.ds(i * (2 * W) + k * W, W), :],
                                             rows[k][:]).then_inc(s_row[k], 16)
                        for k in range(2):
                            sp.wait_ge(s_row[k], 16 * (NV // 2 + 1))
                    sp.wait_ge(s_load, 16 * len(loads))

                @block.scalar
                def _(act):
                    act.sem_inc(s_feat, 2)
                    if norm:
                        norm_sqrt(act, s_var, s_std)

                    def features(j, k, r):
                        act.wait_ge(s_turn, j + 3)
                        act.wait_ge(s_prod, j + 1)
                        a.activation(tr[:, k, :, 0:W],
                                     p_tr[k % 2][:, 0:256].rearrange("p (c w) -> p c w", c=KC)[:, :, 0:W],
                                     ACT.Copy).then_inc(s_feat, 1)
                    over(act, 0, NV, KP, features)

                @block.vector
                def _(dve):
                    dve.sem_inc(s_emit, 2)
                    if dve_first is not None:
                        dve_first(dve, s_load, s_wts, frees)
                    if norm:
                        norm_stats(dve, xcur, s_var, s_std)
                        norm_apply(dve, xcur, z)

                    def fill(j, k):
                        if k == 3 or not isinstance(j, int):
                            dve.wait_ge(s_turn, j - 1)
                        v.tensor_copy(win[:, k, :], src[:, bass.ds(j, 1), :].rearrange("p a b -> p (a b)")
                                      ).then_inc(s_slot, 1)

                    def take(j, k):
                        if rows is not None:
                            dve.wait_ge(s_row[k % 2], j * 8 + (16 - 8 * (k % 2)))
                        dve.wait_ge(s_prod, j + 3)
                        emit(j, k % 2, p_o[k % 2]).then_inc(s_emit, 1)

                    def step(j, k, r):
                        fill(j + 3, (k + 3) % KP)
                        take(j, k)

                    for j in range(3):
                        fill(j, j)
                    over(dve, 0, NV - 3, KP, step)
                    for j in range(NV - 3, NV):
                        take(j, j % KP)

                @block.tensor
                def _(pe):
                    pe.sem_inc(s_turn, 2)
                    pe.sem_inc(s_prod, 2)
                    pe.wait_ge(s_load, 16 * len(loads))
                    if pe_first is not None:
                        pe_first(pe, frees)
                        pe.wait_ge(s_wts, 1)

                    def turn(j, k):
                        pe.wait_ge(s_slot, j + 1)
                        pe.wait_ge(s_feat, j + 1)
                        for c in range(KC):
                            last = nc.tensor.transpose(p_tr[k % 2][:, c * 128:c * 128 + W],
                                                       win[:, k, c * 128:(c + 1) * 128], ident[0:W, 0:W])
                        last.then_inc(s_turn, 1)

                    def product(j, k):
                        pe.wait_ge(s_feat, j + 3)
                        pe.wait_ge(s_emit, j + 1)
                        for b in range(nb):
                            c0, c1 = b * 512, min(cols, b * 512 + 512)
                            for c in range(KC):
                                last = mm(p_o[k % 2][0:W, c0:c1], tr[:, k, c, 0:W], wt[:, c, c0:c1],
                                          start=c == 0, stop=c == KC - 1)
                        last.then_inc(s_prod, 1)

                    def step(j, k, r):
                        turn(j + 2, (k + 2) % KP)
                        product(j, k)

                    turn(0, 0)
                    turn(1, 1)
                    over(pe, 0, NV - 2, KP, step)
                    for j in (NV - 2, NV - 1):
                        product(j, j % KP)

        def edges(l, acc, scale):
            H, RW, dots = ATT[l]["H"], D + 2 * ATT[l]["H"], l == 2
            V0 = D if dots else 0
            GW = V0 + RW
            GH = G * H
            K = 2 if dots else 3
            NG = G // 2 if dots else 1
            NZ = 2 if dots else 5
            DONE = (3, 5, 6, 8, 8) if dots else (0, 2, 3, 6, 7)
            TURNS = (G, None) if dots else (4, 8)
            name = f"e{l}_"
            with phase() as ph:
                rowbuf = [sb(f"{name}rowbuf{k}", [W, G, GW], F32, ph) for k in range(K)]
                idx = [sb(f"{name}idx{k}", [W, G], I32, ph) for k in range(K)]
                codet = [sb(f"{name}codet{k}", [W, G * W], F32, ph) for k in range(K)]
                gates = [sb(f"{name}gates{k}", [GH, W + 1], F32, ph) for k in range(K)]
                hot = [sb(f"{name}hot{k}", [W, G, W + 1], F32, ph) for k in range(K)]
                zb = [sb(f"{name}zb{k}", [W + 1, G, RW], F32, ph) for k in range(K)]
                prod = sb(f"{name}prod", [W, 3, 2 * D], F32, ph) if dots else sb(f"{name}prod", [W, GH], F32, ph)
                sc = sb(f"{name}sc", [W, GH], F32, ph)
                df = sb(f"{name}df", [W, GH], F32, ph)
                fw = sb(f"{name}fw", [GH, W], F32, ph)
                mx = sb(f"{name}mx", [GH, W], F32, ph)
                p_q = [ph.enter_context(nc.psum_tensor(f"{name}p_q{k}", [W, 512], F32)) for k in range(NG)]
                p_z = [ph.enter_context(nc.psum_tensor(f"{name}p_z{k}", [W + 1, 512], F32)) for k in range(NZ)]
                p_turn = ph.enter_context(nc.psum_tensor(f"{name}p_turn", [128, 512], F32))
                p_sc, p_m = p_turn[0:GH, 0:W], p_turn[0:W, W:W + GH]
                s_ld = [sem(f"{name}ld{k}") for k in range(K)]
                s_codes = [sem(f"{name}codes{k}") for k in range(K)]
                s_go = sem(name + "go")
                s_seen = sem(name + "seen")
                s_rows = [gather_sem(f"{name}rows{k}") for k in range(K)]
                s_far = sem(name + "far")
                s_codet = sem(name + "codet")
                s_miss = sem(name + "miss")
                s_hot = sem(name + "hot")
                s_q = sem(name + "q")
                s_mul = sem(name + "mul")
                s_red = sem(name + "red")
                s_sc = sem(name + "sc")
                s_tsc = sem(name + "tsc")
                s_fw = sem(name + "fw")
                s_mx = sem(name + "mx")
                s_tm = sem(name + "tm")
                s_df = sem(name + "df")
                s_w = sem(name + "w")
                s_wv = sem(name + "wv")
                s_z = sem(name + "z")
                s_zb = sem(name + "zb")
                s_acc = sem(name + "acc")
                s_hs = [sem(f"{name}hs{k}") for k in range(K)]
                block = ph.enter_context(nc.Block())

                def windows_of(engine, n, count=1):
                    return nc.values_load_multi_w_load_instructions(
                        wtab[0:1, bass.ds(n * G, count * G)], engines=[engine], min_val=0, max_val=NW,
                        skip_runtime_bounds_check_because="the table was made with min(., NW) of values >= 0")[1]

                @block.sync
                def _(sp):
                    def load(n, k, r):
                        sp.wait_ge(s_q, n * NG + NG)
                        sp.dma_start(codet[k][:],
                                     code_tab[bass.ds(n * G, G), :].rearrange("(o g) e -> o (g e)", o=1)
                                     .to_broadcast([W, G * W])).then_inc(s_codes[k], 16)
                        sp.wait_ge(s_mx, n + 1)
                        sp.dma_start(idx[k][:], srcs_tab[bass.ds(n, 1)].rearrange("a p g -> (a p) g")
                                     ).then_inc(s_ld[k], 16)
                        sp.dma_start(gates[k][:],
                                     gate_tab[bass.ds(n * G, G), :].unsqueeze(1)
                                     .to_broadcast([G, H, W + 1])).then_inc(s_ld[k], 16)
                    over(sp, 0, NB, K, load)

                @block.gpsimd
                def _(pool):
                    def gather(n, k, r):
                        pool.wait_ge(s_ld[k], r * 32 + 32)
                        for q in range(G):
                            pool.wait_ge(s_z, n * G + (q + 1))
                            pool.sem_inc(s_go, 1)
                            g.indirect_dma_start(
                                out=rowbuf[k][:, q, 0:ATT[l]["ROW"]], out_offset=None, in_=row_tab[l],
                                in_offset=bass.IndirectOffsetOnAxis(ap=idx[k][:, q:q + 1], axis=0)
                            ).then_inc(s_rows[k], 16)
                    over(pool, 0, NB, K, gather)

                @block.scalar
                def _(act):
                    act.sem_inc(s_zb, NZ)
                    for k in range(K):
                        act.sem_inc(s_hs[k], 16)

                    def code_t(n, k, r):
                        act.wait_ge(s_codes[k], r * 16 + 16)
                        a.activation(codet[k][:], codet[k][:], ACT.Abs, bias=iota_neg[0:W, :]).then_inc(s_far, 1)
                        act.wait_ge(s_far, n + 1)
                        a.activation(codet[k][:], codet[k][:], ACT.Relu, scale=-1.0, bias=ones[0:W, 0:1]
                                     ).then_inc(s_codet, 1)

                    def distance(n, k, q):
                        a.activation(hot[k][:, q, :], iota_row[0:W, 0:W + 1], ACT.Abs, scale=-1.0,
                                     bias=mcode[:, bass.ds(n * G + q, 1)]).then_inc(s_miss, 1)

                    def one_hots(n, k):
                        act.wait_ge(s_miss, n * G + G)
                        a.activation(hot[k][:], hot[k][:], ACT.Relu, scale=-1.0, bias=ones[0:W, 0:1]
                                     ).then_inc(s_hot, G)

                    def weigh(n, k):
                        act.wait_ge(s_df, n + 1)
                        a.activation(rowbuf[k][:, :, V0 + D:V0 + D + H],
                                     df[:].rearrange("p (g h) -> p g h", h=H),
                                     ACT.Exp, scale=scale).then_inc(s_w, 1)

                    def batch(n, k, r, codes=True, hots=dots, ahead=True):
                        if codes and not dots:
                            code_t(n + 2, *slot(k, r, 2, K))
                        act.wait_ge(s_hs[k], r * 16 + 16)
                        for q in range(G):
                            if ahead and not dots and q == DONE[3]:
                                weigh(n + 1, (k + 1) % K)
                            act.wait_ge(s_z, n * G + (q + 1 + K * G))
                            act.wait_ge(s_acc, n * G + (q + 1))
                            a.activation(zb[k][:, q, :], p_z[q % NZ][:, 0:RW], ACT.Copy).then_inc(s_zb, 1)
                            if hots:
                                distance(n + K, k, q)
                        if dots:
                            if ahead:
                                weigh(n + 1, (k + 1) % K)
                            if codes:
                                code_t(n + 3, *slot(k, r, 3, K))
                            if hots:
                                one_hots(n + K, k)
                        act.wait_ge(s_zb, n * G + (G + NZ))
                        act.dma_start(head_tab[l][bass.ds(n * G, G), :].rearrange("(o g) r -> o g r", o=1),
                                      zb[k][HEAD:HEAD + 1, :, :]).then_inc(s_hs[k], 16)

                    code_t(0, 0, 0)
                    code_t(1, 1, 0)
                    if dots:
                        for k in range(K):
                            for q in range(G):
                                distance(k, k, q)
                            one_hots(k, k)
                    weigh(0, 0)
                    if dots:
                        code_t(2, *slot(0, 0, 2, K))
                    coded = NB - (3 if dots else 2)
                    over(act, 0, coded, K, batch)
                    for n in range(coded, NB):
                        batch(n, n % K, n // K, codes=False, hots=dots and n + K < NB, ahead=n + 1 < NB)
                    for k in range(K):
                        act.wait_ge(s_hs[k], 16 * (1 + len(range(k, NB, K))))

                @block.tensor
                def _(pe):
                    pe.sem_inc(s_z, K * G)
                    pe.sem_inc(s_q, K * NG)

                    def spread(n, k, turn=None):
                        wins = windows_of(mybir.EngineType.PE, n)
                        pe.wait_ge(s_codet, n + 1)
                        if dots:
                            for q in range(NG):
                                if q == 1 and turn is not None:
                                    turn_maxima(turn)
                                pe.wait_ge(s_mul, n * NG + (q + 1))
                                for r in range(2):
                                    last = mm(p_q[q][:, r * D:(r + 1) * D],
                                              codet[k][:, (2 * q + r) * W:(2 * q + r + 1) * W],
                                              z[:, bass.ds(wins[2 * q + r], 1), :].rearrange("p a b -> p (a b)"),
                                              start=True, stop=True)
                                last.then_inc(s_q, 1)
                        else:
                            pe.wait_ge(s_sc, n + 1)
                            for q in range(G):
                                last = mm(p_q[0][:, q * H:(q + 1) * H], codet[k][:, q * W:(q + 1) * W],
                                          dwin[:, bass.ds(wins[q], 1), 0:H].rearrange("p a b -> p (a b)"),
                                          start=True, stop=True)
                            last.then_inc(s_q, 1)

                    def turn_scores(n):
                        pe.wait_ge(s_sc, n + 2)
                        pe.sem_inc(s_seen, 1)
                        nc.tensor.transpose(p_sc, sc[:], ident[0:W, 0:W]).then_inc(s_tsc, 1)

                    def turn_maxima(n):
                        pe.wait_ge(s_mx, n + (1 + K))
                        pe.sem_inc(s_seen, 1)
                        nc.tensor.transpose(p_m, mx[:], ident[0:GH, 0:GH]).then_inc(s_tm, 1)

                    def batch(n, k, r, ahead=True):
                        if ahead:
                            spread(n + 1, (k + 1) % K, turn=n if dots else None)
                        elif dots:
                            turn_maxima(n)
                        pe.wait_ge(s_hot, n * G + G)
                        for q in range(G + 1):
                            if ahead and q == TURNS[0]:
                                turn_scores(n + 1)
                            if ahead and q == TURNS[1]:
                                turn_maxima(n + 1)
                            if q in (0, G // 2):
                                pe.wait_ge(s_wv, n * 2 + (1 + q * 2 // G))
                            if q < G:
                                pe.wait_ge(s_zb, n * G + (q + 1))
                                mm(p_z[q % NZ][:, 0:RW], hot[k][:, q, :], rowbuf[k][:, q, V0:V0 + RW],
                                   start=True, stop=True).then_inc(s_z, 1)

                    spread(0, 0)
                    turn_scores(0)
                    if not dots:
                        turn_maxima(0)
                    over(pe, 0, NB - 1, K, batch)
                    batch(NB - 1, (NB - 1) % K, (NB - 1) // K, ahead=False)

                @block.vector
                def _(dve):
                    v.memset(acc[:], 0.0).then_inc(s_acc, K * G)
                    dve.sem_inc(s_mul, NG)
                    dve.sem_inc(s_sc, 1)
                    dve.sem_inc(s_mx, K)

                    def one_hot(n, k, q):
                        v.tensor_scalar(hot[k][:, q, :], iota_row[0:W, 0:W + 1], mcode[:, bass.ds(n * G + q, 1)],
                                        None, ALU.is_equal).then_inc(s_hot, 1)

                    def add_up(n, k, q, wins, ahead):
                        into = acc[:, bass.ds(wins[q], 1), :].rearrange("p a b -> p (a b)")
                        dve.wait_ge(s_zb, n * G + (q + 1 + NZ))
                        dve.wait_ge(s_acc, n * G + (q + K * G))
                        v.tensor_tensor(into, into, zb[k][:, q, :], ALU.add).then_inc(s_acc, 1)
                        if ahead and not dots:
                            one_hot(n + K, k, q)

                    def multiply(n, k, q):
                        if q >= 3:
                            dve.wait_ge(s_red, n * NG + (q - 2))
                        dve.wait_ge(s_q, n * NG + (q + 1 + K * NG))
                        v.tensor_tensor(prod[:, q % 3, :].rearrange("p (r d) -> p r d", r=2),
                                        rowbuf[k][:, 2 * q:2 * q + 2, 0:D],
                                        p_q[q][:].rearrange("p (r d) -> p r d", r=2),
                                        ALU.mult).then_inc(s_mul, 1)

                    def batch(n, k, r, wins=None, ahead=True):
                        def add_before(lo, hi):
                            if wins is not None:
                                for q in range(lo, hi):
                                    add_up(n - 1, (k - 1) % K, q, wins, ahead)

                        dve.wait_ge(s_rows[k], r * (16 * G) + 16 * G)
                        if dots:
                            multiply(n, k, 0)
                            for q in range(NG):
                                if q + 1 < NG:
                                    multiply(n, k, q + 1)
                                dve.wait_ge(s_mul, n * NG + (q + 1 + NG))
                                v.tensor_reduce(sc[:, 2 * H * q:2 * H * (q + 1)],
                                                prod[:, q % 3, :].rearrange("p (h d) -> p h d", d=D // H),
                                                AX, ALU.add).then_inc(s_red, 1)
                                if q > NG - 1 - DONE[0]:
                                    add_before(q - NG + DONE[0], q - NG + DONE[0] + 1)
                            dve.wait_ge(s_red, n * NG + NG)
                            dve.sem_inc(s_sc, 1)
                        else:
                            dve.wait_ge(s_q, n + (1 + K))
                            v.tensor_tensor(prod[:].rearrange("p (g h) -> p g h", h=H),
                                            rowbuf[k][:, :, D:D + H],
                                            p_q[0][:, 0:GH].rearrange("p (g h) -> p g h", h=H),
                                            ALU.add).then_inc(s_mul, 1)
                            dve.wait_ge(s_mul, n + 2)
                            v.scalar_tensor_tensor(out=sc[:], in0=prod[:], scalar=0.2, in1=prod[:],
                                                   op0=ALU.mult, op1=ALU.max).then_inc(s_sc, 1)
                        add_before(DONE[0], DONE[1])
                        dve.wait_ge(s_tsc, n + 1)
                        dve.wait_ge(s_ld[k], r * 32 + 32)
                        v.tensor_tensor_scan(out=fw[:], data0=gates[k][:, 0:W], data1=p_sc, initial=FAR,
                                             op0=ALU.add, op1=ALU.max).then_inc(s_fw, 1)
                        add_before(DONE[1], DONE[2])
                        dve.wait_ge(s_fw, n + 1)
                        v.tensor_tensor_scan(out=mx[:, ::-1], data0=gates[k][:, 1:W + 1][:, ::-1],
                                             data1=fw[:, ::-1], initial=FAR,
                                             op0=ALU.add, op1=ALU.max).then_inc(s_mx, 1)
                        add_before(DONE[2], DONE[3])
                        dve.wait_ge(s_tm, n + 1)
                        v.tensor_tensor(df[:], sc[:], p_m, ALU.subtract).then_inc(s_df, 1)
                        v.tensor_tensor(rowbuf[k][:, :, V0 + D + H:V0 + RW],
                                        p_m.rearrange("p (g h) -> p g h", h=H),
                                        first[:, bass.ds(n * G, G)].unsqueeze(2).to_broadcast([W, G, H]), ALU.mult)
                        add_before(DONE[3], DONE[4])
                        dve.wait_ge(s_w, n + 1)
                        for half in (slice(0, G // 2), slice(G // 2, G)):
                            rows = rowbuf[k][:, half, V0:V0 + D].rearrange("p g (h d) -> p g h d", h=H)
                            v.tensor_tensor(rows, rows, rowbuf[k][:, half, V0 + D:V0 + D + H].unsqueeze(3)
                                            .to_broadcast([W, G // 2, H, D // H]), ALU.mult).then_inc(s_wv, 1)
                        add_before(DONE[4], G)

                    if not dots:
                        for k in range(K):
                            for q in range(G):
                                one_hot(k, k, q)
                    batch(0, 0, 0)
                    turns = (NB - K) // K
                    with dve.Fori(0, turns) as i:
                        wins = windows_of(mybir.EngineType.DVE, i * K, K)
                        for k in range(K):
                            batch(i * K + (k + 1), *slot(0, i, k + 1, K), wins[k * G:(k + 1) * G])
                    for n in range(turns * K + 1, NB):
                        batch(n, n % K, n // K, windows_of(mybir.EngineType.DVE, n - 1), ahead=n - 1 + K < NB)
                    wins = windows_of(mybir.EngineType.DVE, NB - 1)
                    for q in range(G):
                        add_up(NB - 1, (NB - 1) % K, q, wins, False)

        def merge(l, acc, scale, finish):
            H, RW = ATT[l]["H"], D + 2 * ATT[l]["H"]
            name = f"m{l}_"
            with phase() as ph:
                hrows = sb(name + "hrows", [PQ, PC, RW], F32, ph)
                hm = sb(name + "hm", [8, NP], F32, ph)
                hf = sb(name + "hf", [8, NP], F32, ph)
                hr = sb(name + "hr", [PQ, PC, H], F32, ph)
                hx = sb(name + "hx", [PQ, PC, H], F32, ph)
                winof = sb(name + "winof", [PQ, NV], F32, ph)
                oh = sb(name + "oh", [PQ, 2, PC, W], F32, ph)
                acc2 = sb(name + "acc2", [W, NV, RW], F32, ph)
                sm = [sb(f"{name}sm{k}", [W, NW, H], F32, ph) for k in range(5)]
                part = [sb(f"{name}part{k}", [W, 5, D], F32, ph) for k in range(2)]
                p_r = ph.enter_context(nc.psum_tensor(name + "p_r", [8, 512], F32))
                p_c = ph.enter_context(nc.psum_tensor(name + "p_c", [PQ, 512], F32))
                p_w = [ph.enter_context(nc.psum_tensor(f"{name}p_w{k}", [W, 512], F32)) for k in range(2)]
                s_in, s_iota, s_r, s_hm, s_c, s_hx, s_hr, s_hv = [
                    sem(name + n) for n in ("in", "iota", "r", "hm", "c", "hx", "hr", "hv")]
                s_oh = sem(name + "oh")
                s_p = sem(name + "p")
                s_ev = sem(name + "ev")
                s_sh, s_ex = sem(name + "sh"), sem(name + "ex")
                block = ph.enter_context(nc.Block())

                @block.sync
                def _(sp):
                    sp.dma_start(hrows[:], head_tab[l].rearrange("(c p) r -> p c r", p=PQ)).then_inc(s_in, 16)
                    sp.wait_ge(s_in, 16)

                @block.gpsimd
                def _(pool):
                    g.iota(winof[:], pattern=[[W, NV]], base=0, channel_multiplier=0,
                           allow_small_or_imprecise_dtypes=True).then_inc(s_iota, 1)

                @block.tensor
                def _(pe):
                    pe.sem_inc(s_p, 2)
                    pe.wait_ge(s_in, 16)
                    for c in range(PC):
                        last = nc.tensor.transpose(p_r[0:H, c * PQ:(c + 1) * PQ], hrows[:, c, D + H:RW],
                                                   ident[0:PQ, 0:PQ])
                    last.then_inc(s_r, 1)
                    pe.wait_ge(s_hm, 1)
                    for c in range(PC):
                        last = nc.tensor.transpose(p_c[:, c * H:(c + 1) * H], hm[0:H, c * PQ:(c + 1) * PQ],
                                                   ident[0:H, 0:H])
                    last.then_inc(s_c, 1)
                    pe.wait_ge(s_hv, 1)
                    with pe.Fori(0, NV // 2) as i:
                        for k in range(2):
                            pe.wait_ge(s_oh, i * 2 + k + 1)
                            pe.wait_ge(s_ev, i * 2 + k + 1)
                            for c in range(PC):
                                last = mm(p_w[k][:, 0:RW], oh[:, k, c, :], hrows[:, c, :],
                                          start=c == 0, stop=c == PC - 1)
                            last.then_inc(s_p, 1)

                @block.scalar
                def _(act):
                    act.sem_inc(s_ev, 2)
                    act.wait_ge(s_hx, 1)
                    a.activation(hr[:], hx[:], ACT.Exp, scale=scale).then_inc(s_hr, 1)
                    with act.Fori(0, NV // 2) as i:
                        for k in range(2):
                            act.wait_ge(s_p, i * 2 + k + 3)
                            a.activation(acc2[:, bass.ds(i * 2 + k, 1), :].rearrange("p a b -> p (a b)"),
                                         p_w[k][:, 0:RW], ACT.Copy).then_inc(s_ev, 1)
                    act.wait_ge(s_sh, 1)
                    a.activation(sm[0][:], sm[0][:], ACT.Exp, scale=scale)
                    a.activation(sm[1][:], sm[1][:], ACT.Exp, scale=scale).then_inc(s_ex, 1)

                @block.vector
                def _(dve):
                    dve.wait_ge(s_r, 1)
                    vd(v.tensor_copy(hm[0:H, :], p_r[0:H, 0:NP]))
                    vd(v.tensor_tensor_scan(out=hf[0:H, :], data0=hgate[0:H, 0:NP], data1=hm[0:H, :], initial=FAR,
                                            op0=ALU.add, op1=ALU.max))
                    v.tensor_tensor_scan(out=hm[0:H, ::-1], data0=hgate[0:H, 1:NP + 1][:, ::-1],
                                         data1=hf[0:H, ::-1], initial=FAR,
                                         op0=ALU.add, op1=ALU.max).then_inc(s_hm, 1)
                    dve.wait_ge(s_c, 1)
                    dve.wait_ge(s_in, 16)
                    top_m = p_c[:, 0:PC * H].rearrange("p (c h) -> p c h", h=H)
                    v.tensor_tensor(hx[:], hrows[:, :, D + H:RW], top_m, ALU.subtract).then_inc(s_hx, 1)
                    dve.wait_ge(s_hr, 1)
                    v.tensor_tensor(hrows[:, :, D + H:RW], top_m, hfirst[:].unsqueeze(2).to_broadcast([PQ, PC, H]),
                                    ALU.mult)
                    v.tensor_tensor(hrows[:, :, D:D + H], hrows[:, :, D:D + H], hr[:], ALU.mult)
                    body = hrows[:, :, 0:D].rearrange("p c (h d) -> p c h d", h=H)
                    v.tensor_tensor(body, body, hr[:].unsqueeze(3).to_broadcast([PQ, PC, H, D // H]),
                                    ALU.mult).then_inc(s_hv, 1)
                    dve.wait_ge(s_iota, 1)
                    with dve.Fori(0, NV // 2) as i:
                        for k in range(2):
                            dve.wait_ge(s_p, i * 2 + k + 1)
                            for c in range(PC):
                                last = v.tensor_scalar(oh[:, k, c, :], iota_row[0:PQ, 0:W],
                                                       winof[:, bass.ds(i * 2 + k, 1)], hdst[:, c:c + 1],
                                                       ALU.add, ALU.is_equal)
                            last.then_inc(s_oh, 1)
                    dve.wait_ge(s_ev, NV + 2)
                    acc1, ac2 = acc[0:W, 0:NW, :], acc2[:, 0:NW, :]
                    den1, max1 = acc1[:, :, D:D + H], acc1[:, :, D + H:RW]
                    den2, max2 = ac2[:, :, D:D + H], ac2[:, :, D + H:RW]
                    v.tensor_scalar(sm[0][:], den1, 0.0, FAR, ALU.is_equal, ALU.mult)
                    vd(v.tensor_scalar(sm[1][:], den2, 0.0, FAR, ALU.is_equal, ALU.mult))
                    v.tensor_tensor(sm[0][:], sm[0][:], max1, ALU.add)
                    vd(v.tensor_tensor(sm[1][:], sm[1][:], max2, ALU.add))
                    vd(v.tensor_tensor(sm[2][:], sm[0][:], sm[1][:], ALU.max))
                    v.tensor_tensor(sm[0][:], sm[0][:], sm[2][:], ALU.subtract)
                    v.tensor_tensor(sm[1][:], sm[1][:], sm[2][:], ALU.subtract)
                    v.drain().then_inc(s_sh, 1)
                    dve.wait_ge(s_ex, 1)
                    v.tensor_tensor(sm[2][:], sm[0][:], den1, ALU.mult)
                    vd(v.tensor_tensor(sm[3][:], sm[1][:], den2, ALU.mult))
                    vd(v.tensor_tensor(sm[2][:], sm[2][:], sm[3][:], ALU.add))
                    if l < 2:
                        vd(v.tensor_scalar(sm[2][:], sm[2][:], 1e-16, None, ALU.add))
                    else:
                        vd(v.tensor_scalar(sm[2][:], sm[2][:], 1e-30, None, ALU.max))
                    vd(v.reciprocal(sm[4][:], sm[2][:]))
                    v.tensor_tensor(sm[0][:], sm[0][:], sm[4][:], ALU.mult)
                    vd(v.tensor_tensor(sm[1][:], sm[1][:], sm[4][:], ALU.mult))
                    for c in range(0, NW, 5):
                        for k, ac in enumerate((acc1, ac2)):
                            v.tensor_tensor(part[k][:].rearrange("p w (h d) -> p w h d", h=H),
                                            ac[:, c:c + 5, 0:D].rearrange("p w (h d) -> p w h d", h=H),
                                            sm[k][:, c:c + 5, :].unsqueeze(3).to_broadcast([W, 5, H, D // H]),
                                            ALU.mult)
                        v.drain()
                        finish(c, part)
                        v.drain()

        def experts(f):
            cf = FFN[f]
            NE, FC, NBLK = cf["E"], cf["FC"], cf["NBLK"]
            name = f"x{f}_"
            with ExitStack() as keep:
                logit = sb(name + "logit", [W, NV, NE], F32, keep)
                wt2 = [sb(f"{name}wt{k}", [W, NW], F32, keep) for k in range(2)]
                pos = [sb(f"{name}pos{k}", [W, NW], I32, keep) for k in range(2)]
                bexp = sb(name + "bexp", [1, NBLK], I32, keep)
                with phase() as ph:
                    gw = sb(name + "gw", [128, KC, NE], F32, ph)
                    gb = sb(name + "gb", [W, NE], F32, ph)
                    project(name + "g_", z, NE,
                            [(gw[:], t[f"gate_w{f}"].rearrange("(c p) e -> p c e", p=128)),
                             (gb[:], t[f"gate_b{f}"].to_broadcast([W, NE]))], gw,
                            lambda j, k, p: v.tensor_tensor(logit[:, bass.ds(j, 1), :].rearrange("p a b -> p (a b)"),
                                                            p[0:W, 0:NE], gb[:], ALU.add), norm=True)
                with phase() as ph:
                    def arr(n, shape=(W, NW, NE)):
                        return sb(name + n, list(shape), F32, ph)
                    lg = logit[:, 0:NW, :]
                    order = arr("order", (W, NE))
                    eq, key, lg2, both, base, rank = [arr(n) for n in ("eq", "key", "lg2", "both", "base", "rank")]
                    oh = [arr("oh0"), arr("oh1")]
                    top1, top2, kmax, dd, ee = [arr(n, (W, NW)) for n in ("top1", "top2", "kmax", "dd", "ee")]
                    colt, reset, run = [arr(n, (W, NE, NW)) for n in ("colt", "reset", "run")]
                    steps = arr("steps", (W, NW))
                    nblk, cend, zer = [arr(n, (W, NE)) for n in ("nblk", "cend", "zer")]
                    lower = arr("lower", (W, W))
                    bnum = arr("bnum", (1, NBLK))
                    bcmp = arr("bcmp", (1, NBLK, NE))
                    bsum = arr("bsum", (1, NBLK))
                    p_rank = ph.enter_context(nc.psum_tensor(name + "p_rank", [W, 512], F32))
                    p_col = ph.enter_context(nc.psum_tensor(name + "p_col", [W, 512], F32))
                    s_const, s_both, s_ranks, s_dd, s_ee, s_pos, s_var, s_std = [
                        sem(name + n) for n in ("const", "both", "ranks", "dd", "ee", "pos", "var", "std")]
                    s_sent = gather_sem(name + "sent")
                    block = ph.enter_context(nc.Block())

                    @block.gpsimd
                    def _(pool):
                        g.iota(order[:], pattern=[[-1, NE]], base=NE, channel_multiplier=0,
                               allow_small_or_imprecise_dtypes=True).then_inc(s_const, 1)
                        g.iota(steps[:], pattern=[[128, NW]], base=0, channel_multiplier=0,
                               allow_small_or_imprecise_dtypes=True).then_inc(s_const, 1)
                        g.iota(bnum[:], pattern=[[1, NBLK]], base=0, channel_multiplier=0,
                               allow_small_or_imprecise_dtypes=True).then_inc(s_const, 1)
                        g.affine_select(out=lower[:], in_=ones[0:W, 0:W], compare_op=ALU.is_ge, fill=0.0, base=-1,
                                        pattern=[[1, W]], channel_multiplier=-1).then_inc(s_const, 1)
                        pool.wait_ge(s_pos, 1)
                        for w in range(NW):
                            for k in range(2):
                                g.indirect_dma_start(out=xs_tab, in_=z[:, w, :], in_offset=None,
                                                     out_offset=bass.IndirectOffsetOnAxis(ap=pos[k][:, w:w + 1], axis=0)
                                                     ).then_inc(s_sent, 16)
                        pool.wait_ge(s_sent, 16 * 2 * NW)

                    @block.tensor
                    def _(pe):
                        pe.wait_ge(s_both, 1)
                        flat = both[:].rearrange("p w e -> p (w e)")
                        mm(p_rank[:, 0:NW * NE], lower[:], flat, start=True, stop=True)
                        mm(p_col[:, 0:NW * NE], ones[0:W, 0:W], flat, start=True, stop=True).then_inc(s_ranks, 1)

                    @block.scalar
                    def _(act):
                        act.wait_ge(s_dd, 1)
                        a.activation(ee[:], dd[:], ACT.Exp).then_inc(s_ee, 1)
                        if f == 1:
                            norm_sqrt(act, s_var, s_std)

                    @block.vector
                    def _(dve):
                        def wide(ap):
                            return ap.unsqueeze(2).to_broadcast([W, NW, NE])

                        def each(ap):
                            return ap.unsqueeze(1).to_broadcast([W, NW, NE])

                        dve.wait_ge(s_const, 4)

                        def pick(src, best, hot):
                            vd(v.tensor_reduce(best[:], src, AX, ALU.max))
                            vd(v.tensor_tensor(eq[:], src, wide(best[:]), ALU.is_equal))
                            vd(v.tensor_tensor(key[:], eq[:], each(order[:]), ALU.mult))
                            vd(v.tensor_reduce(kmax[:], key[:], AX, ALU.max))
                            vd(v.tensor_tensor(hot[:], key[:], wide(kmax[:]), ALU.is_equal))

                        pick(lg, top1, oh[0])
                        vd(v.tensor_scalar(lg2[:], oh[0][:], FAR, None, ALU.mult))
                        vd(v.tensor_tensor(lg2[:], lg2[:], lg, ALU.add))
                        pick(lg2[:], top2, oh[1])
                        vd(v.tensor_tensor(both[:], oh[0][:], oh[1][:], ALU.add))
                        v.tensor_tensor(dd[:], top2[:], top1[:], ALU.subtract)
                        v.drain().then_inc(s_both, 1)
                        dve.sem_inc(s_dd, 1)
                        dve.wait_ge(s_ee, 1)
                        vd(v.tensor_scalar(dd[:], ee[:], 1.0, None, ALU.add))
                        vd(v.reciprocal(wt2[0][:], dd[:]))
                        v.tensor_tensor(wt2[1][:], ee[:], wt2[0][:], ALU.mult)
                        v.memset(reset[:], 1.0)
                        dve.wait_ge(s_ranks, 1)
                        v.tensor_copy(colt[:], p_col[:, 0:NW * NE].rearrange("p (w e) -> p e w", e=NE))
                        v.memset(zer[:], 0.0)
                        v.drain()
                        vd(v.memset(reset[:, :, 0:1], 0.0))
                        vd(v.tensor_tensor_scan(out=run[:].rearrange("p e w -> p (e w)"),
                                                data0=reset[:].rearrange("p e w -> p (e w)"),
                                                data1=colt[:].rearrange("p e w -> p (e w)"), initial=0.0,
                                                op0=ALU.mult, op1=ALU.add))
                        cmp3 = reset[:]
                        vd(v.tensor_tensor(cmp3, run[:, :, NW - 1:NW].to_broadcast([W, NE, NW]),
                                           steps[:].unsqueeze(1).to_broadcast([W, NE, NW]), ALU.is_gt))
                        vd(v.tensor_reduce(nblk[:], cmp3, AX, ALU.add))
                        vd(v.tensor_tensor_scan(out=cend[:], data0=nblk[:], data1=zer[:], initial=0.0,
                                                op0=ALU.add, op1=ALU.add))
                        vd(v.tensor_tensor(zer[:], cend[:], nblk[:], ALU.subtract))
                        vd(v.tensor_scalar(zer[:], zer[:], 128.0, None, ALU.mult))
                        v.tensor_tensor(run[:], run[:], colt[:], ALU.subtract)
                        v.drain()
                        vd(v.tensor_tensor(base[:], run[:].rearrange("p e w -> p w e"), each(zer[:]), ALU.add))
                        vd(v.tensor_tensor(rank[:], base[:],
                                           p_rank[:, 0:NW * NE].rearrange("p (w e) -> p w e", e=NE), ALU.add))
                        for k in range(2):
                            vd(v.tensor_tensor(key[:], rank[:], oh[k][:], ALU.mult))
                            vd(v.tensor_reduce(top1[:], key[:], AX, ALU.add))
                            vd(v.tensor_copy(pos[k][:], top1[:]))
                        vd(v.tensor_tensor(bcmp[:], cend[0:1, :].unsqueeze(1).to_broadcast([1, NBLK, NE]),
                                           bnum[:].unsqueeze(2).to_broadcast([1, NBLK, NE]), ALU.is_le))
                        vd(v.tensor_reduce(bsum[:], bcmp[:], AX, ALU.add))
                        vd(v.tensor_scalar(bexp[:], bsum[:], NE - 1.0, None, ALU.min))
                        if f == 1:
                            norm_stats(dve, z, s_var, s_std)
                            norm_apply(dve, z, z)
                        v.drain().then_inc(s_pos, 1)
                with phase() as ph:
                    KS = 4
                    pack = [sb(f"{name}pack{k}", [128, cf["PK"]], F32, ph) for k in range(KS)]
                    w2 = [sb(f"{name}w2{k}", [128, FC * D], F32, ph) for k in range(KS)]
                    b2 = [sb(f"{name}b2{k}", [1, D], F32, ph) for k in range(KS)]
                    xb = [sb(f"{name}xb{k}", [128, D], F32, ph) for k in range(KS)]
                    xt = [sb(f"{name}xt{k}", [128, KC, 128], F32, ph) for k in range(2)]
                    ht = [sb(f"{name}ht{k}", [128, FC, 128], F32, ph) for k in range(2)]
                    yb = [sb(f"{name}yb{k}", [128, D], F32, ph) for k in range(2)]
                    p_x = [ph.enter_context(nc.psum_tensor(f"{name}p_x{k}", [128, 512], F32)) for k in range(2)]
                    p_h = [ph.enter_context(nc.psum_tensor(f"{name}p_h{k}", [128, max(4, FC), 128], F32)) for k in range(2)]
                    p_y = [ph.enter_context(nc.psum_tensor(f"{name}p_y{k}", [128, 512], F32)) for k in range(2)]
                    s_w = [sem(f"{name}w{k}") for k in range(KS)]
                    s_w2 = [sem(f"{name}w2{k}") for k in range(KS)]
                    s_xt = sem(name + "xtp")
                    s_xs = sem(name + "xs")
                    s_h = sem(name + "h")
                    s_hs = sem(name + "hs")
                    s_y = sem(name + "y")
                    s_ys = sem(name + "ys")
                    s_st = sem2(name + "st")
                    block = ph.enter_context(nc.Block())

                    @block.sync
                    def _(sp):
                        for k in range(2):
                            sp.sem_inc(s_st[k], 16)

                        def load(b, k):
                            ex = sp.value_load(bexp[0:1, bass.ds(b, 1)], min_val=0, max_val=NE - 1)
                            sp.dma_start(xb[k][:], xs_tab[bass.ds(b * 128, 128), :]).then_inc(s_w[k], 16)
                            sp.dma_start(pack[k][:], t[f"pack{f}"][bass.ds(ex, 1)].rearrange("a p c -> (a p) c")
                                         ).then_inc(s_w[k], 16)
                            sp.dma_start(w2[k][:], t[f"w2_{f}"][bass.ds(ex, 1)].rearrange("a p c -> (a p) c")
                                         ).then_inc(s_w2[k], 16)
                            sp.dma_start(b2[k][:], t[f"b2_{f}"][bass.ds(ex, 1), :]).then_inc(s_w2[k], 16)

                        def store(b, k):
                            sp.wait_ge(s_ys, b + 3)
                            sp.dma_start(ys_tab[bass.ds(b * 128, 128), :], yb[k % 2][:]).then_inc(s_st[k % 2], 16)

                        def follow(b, k, r):
                            sp.wait_ge(s_y, b - KS + 3)
                            load(b, k)
                            store(b - KS, k)

                        for k in range(KS):
                            load(k, k)
                        over(sp, KS, NBLK, KS, follow)
                        for k in range(KS):
                            store(NBLK - KS + k, k)
                        for k in range(2):
                            sp.wait_ge(s_st[k], 16 * (NBLK // 2 + 1))
                        for k in range(KS):
                            sp.wait_ge(s_w[k], 32 * (NBLK // KS))
                            sp.wait_ge(s_w2[k], 32 * (NBLK // KS))

                    @block.tensor
                    def _(pe):
                        pe.sem_inc(s_xt, 2)
                        pe.sem_inc(s_y, 2)
                        pe.sem_inc(s_h, 2 * FC)

                        def turn(b, k, r):
                            pe.wait_ge(s_w[k], r * 32 + 32)
                            pe.wait_ge(s_xs, b + 1)
                            for c in range(KC):
                                last = nc.tensor.transpose(p_x[k % 2][:, c * 128:(c + 1) * 128],
                                                           xb[k][:, c * 128:(c + 1) * 128], ident[:])
                            last.then_inc(s_xt, 1)

                        def hidden(b, k):
                            pe.wait_ge(s_hs, b * FC + FC)
                            pe.wait_ge(s_xs, b + 3)
                            for j in range(FC):
                                for c in range(KC):
                                    o = c * cf["F"] + j * 128
                                    last = mm(p_h[k % 2][:, j, :], pack[k][:, o:o + 128], xt[k % 2][:, c, :],
                                              start=c == 0, stop=c == KC - 1)
                                last.then_inc(s_h, 1)

                        def output(b, k, r):
                            pe.wait_ge(s_w2[k], r * 32 + 32)
                            pe.wait_ge(s_ys, b + 1)
                            mm(p_y[k % 2][:, 0:D], ones[0:1, :], b2[k][:], start=True, stop=False)
                            for j in range(FC):
                                pe.wait_ge(s_hs, b * FC + (j + 1 + 2 * FC))
                                last = mm(p_y[k % 2][:, 0:D], ht[k % 2][:, j, :], w2[k][:, j * D:(j + 1) * D],
                                          start=False, stop=j == FC - 1)
                            last.then_inc(s_y, 1)

                        def step(b, k, r, ahead=True):
                            hidden(b + 1, (k + 1) % KS)
                            if ahead:
                                turn(b + 2, *slot(k, r, 2, KS))
                            output(b, k, r)

                        turn(0, 0, 0)
                        hidden(0, 0)
                        turn(1, 1, 0)
                        over(pe, 0, NBLK - 2, KS, step)
                        step(NBLK - 2, (NBLK - 2) % KS, (NBLK - 2) // KS, ahead=False)
                        output(NBLK - 1, (NBLK - 1) % KS, (NBLK - 1) // KS)

                    @block.scalar
                    def _(act):
                        act.sem_inc(s_hs, 2 * FC)

                        def activate(b, k, r):
                            act.wait_ge(s_y, b + 1)
                            for j in range(FC):
                                if j % 4 == 0:
                                    act.wait_ge(s_h, b * FC + (j + 4 + 2 * FC))
                                a.activation(ht[k % 2][:, j, :], p_h[k % 2][:, j, :],
                                             ACT.Relu if f == 0 else ACT.Gelu,
                                             bias=pack[k][:, cf["ob"] + j:cf["ob"] + j + 1]).then_inc(s_hs, 1)
                        over(act, 0, NBLK, KS, activate)

                    @block.vector
                    def _(dve):
                        dve.sem_inc(s_xs, 2)
                        dve.sem_inc(s_ys, 2)

                        def features(b, k):
                            dve.wait_ge(s_xt, b + 3)
                            if f == 0:
                                v.tensor_copy(xt[k % 2][:].rearrange("p c m -> p (c m)"), p_x[k % 2][:, 0:D]
                                              ).then_inc(s_xs, 1)
                            else:
                                for c in range(KC):
                                    last = v.tensor_scalar(xt[k % 2][:, c, :], p_x[k % 2][:, c * 128:(c + 1) * 128],
                                                           pack[k][:, cf["og"] + c:cf["og"] + c + 1],
                                                           pack[k][:, cf["og"] + KC + c:cf["og"] + KC + c + 1],
                                                           ALU.mult, ALU.add)
                                last.then_inc(s_xs, 1)

                        def result(b, k):
                            dve.wait_ge(s_st[k % 2], b * 8 + (16 - 8 * (k % 2)))
                            dve.wait_ge(s_y, b + 3)
                            v.tensor_copy(yb[k % 2][:], p_y[k % 2][:, 0:D]).then_inc(s_ys, 1)

                        def step(b, k, r):
                            features(b + 2, (k + 2) % KS)
                            result(b, k)

                        features(0, 0)
                        features(1, 1)
                        over(dve, 0, NBLK - 2, KS, step)
                        for b in (NBLK - 2, NBLK - 1):
                            result(b, b % KS)
                with phase() as ph:
                    R = 5
                    got = [[sb(f"{name}got{r}_{k}", [W, D], F32, ph) for k in range(2)] for r in range(R)]
                    gb2 = sb(name + "gamma", [W, 2, D], F32, ph)
                    s_got = [gather_sem(f"{name}got{r}") for r in range(R)]
                    s_used, s_g, s_var, s_std, s_out, s_c, s_cen = [
                        sem(name + n) for n in ("used", "gam", "var2", "std2", "out", "c", "cen")]
                    block = ph.enter_context(nc.Block())

                    @block.gpsimd
                    def _(pool):
                        for w in range(NW):
                            if w >= R:
                                pool.wait_ge(s_used, w - R + 1)
                            for k in range(2):
                                g.indirect_dma_start(out=got[w % R][k][:], out_offset=None, in_=ys_tab,
                                                     in_offset=bass.IndirectOffsetOnAxis(ap=pos[k][:, w:w + 1], axis=0)
                                                     ).then_inc(s_got[w % R], 16)

                    @block.scalar
                    def _(act):
                        if f == 0:
                            norm_sqrt(act, s_var, s_std)

                    @block.vector
                    def _(dve):
                        into = z if f == 0 else xcur
                        if f == 0:
                            dve.wait_ge(s_g, 32)
                        for w in range(NW):
                            if f == 0:
                                v.tensor_tensor(xcur[:, w, :], xcur[:, w, :], gb2[:, 1, :], ALU.add)
                                if w >= 1:
                                    dve.wait_ge(s_used, w)
                                    window_stats(z, w - 1)
                            dve.wait_ge(s_got[w % R], 32 * (w // R + 1))
                            v.scalar_tensor_tensor(out=into[:, w, :], in0=got[w % R][0][:], scalar=wt2[0][:, w:w + 1],
                                                   in1=into[:, w, :], op0=ALU.mult, op1=ALU.add).then_inc(s_c, 1)
                            dve.wait_ge(s_c, w + 1)
                            v.scalar_tensor_tensor(out=into[:, w, :], in0=got[w % R][1][:], scalar=wt2[1][:, w:w + 1],
                                                   in1=into[:, w, :], op0=ALU.mult, op1=ALU.add).then_inc(s_used, 1)
                        if f == 0:
                            dve.wait_ge(s_used, NW)
                            window_stats(z, NW - 1)
                            norm_moments(dve, s_var, s_std)

                            def centre(w):
                                v.scalar_tensor_tensor(out=z[:, w, :], in0=z[:, w, :], scalar=mean[:, w:w + 1],
                                                       in1=gb2[:, 0, :], op0=ALU.subtract, op1=ALU.mult
                                                       ).then_inc(s_cen, 1)
                            centre(0)
                            for w in range(NW):
                                if w + 1 < NW:
                                    centre(w + 1)
                                dve.wait_ge(s_cen, w + 1)
                                v.scalar_tensor_tensor(out=xcur[:, w, :], in0=z[:, w, :], scalar=rstd[:, w:w + 1],
                                                       in1=xcur[:, w, :], op0=ALU.mult, op1=ALU.add)

                    @block.sync
                    def _(sp):
                        if f == 0:
                            for k, n in enumerate(("gamma", "beta")):
                                sp.dma_start(gb2[:, k, :], t[n].to_broadcast([W, D])).then_inc(s_g, 16)
                            sp.wait_ge(s_g, 32)
                        else:
                            for w in range(0, NW, 5):
                                sp.wait_ge(s_used, w + 5)
                                sp.dma_start(t["out"].rearrange("(w p) d -> p w d", p=W)[:, w:w + 5, :],
                                             xcur[:, w:w + 5, :]).then_inc(s_out, 16)
                            sp.wait_ge(s_out, 16 * (NW // 5))

        with ExitStack() as gat:
            for l in range(2):
                H, RW = ATT[l]["H"], D + 2 * ATT[l]["H"]
                src = z if l == 0 else None
                with phase() as ph:
                    wnat = sb(f"wnat{l}", [128, KC, D], F32, ph)
                    wts = sb(f"wts{l}", [128, KC, RW], F32, ph)
                    amat = sb(f"amat{l}", [128, KC, 2 * H], F32, ph)
                    rows = [sb(f"grow{l}_{k}", [W, D + H], F32, ph) for k in range(2)]
                    p_a = ph.enter_context(nc.psum_tensor(f"p_a{l}", [128, 512], F32))
                    s_pa, s_am, s_ld2 = sem(f"s_pa{l}"), sem(f"s_am{l}"), sem(f"s_al{l}")

                    def dve_first(dve, s_load, s_wts, _):
                        dve.wait_ge(s_pa, 1)
                        v.tensor_copy(wts[:, :, D:RW], p_a[:, 0:KC * 2 * H].rearrange("p (c h) -> p c h", c=KC))
                        v.drain().then_inc(s_wts, 1)

                    def pe_first(pe, _):
                        for ci in range(KC):
                            for co in range(KC):
                                last = mm(p_a[:, ci * 2 * H:(ci + 1) * 2 * H], wnat[:, co, ci * 128:(ci + 1) * 128],
                                          amat[:, co, :], start=co == 0, stop=co == KC - 1)
                        last.then_inc(s_pa, 1)

                    with nc.Block() as pre:
                        @pre.vector
                        def _(dve):
                            v.memset(amat[:], 0.0)
                            v.drain().then_inc(s_am, 1)

                        @pre.sync
                        def _(sp):
                            sp.wait_ge(s_am, 1)
                            n = 0
                            for k, nm in enumerate(("src", "dst")):
                                for h in range(H):
                                    for o in range(h * (D // H), (h + 1) * (D // H), min(128, D // H)):
                                        m = min(128, D // H)
                                        sp.dma_start(amat[o % 128:o % 128 + m, o // 128, k * H + h:k * H + h + 1],
                                                     t[f"a{l}_{nm}"][o:o + m, :]).then_inc(s_ld2, 16)
                                        n += 1
                            sp.wait_ge(s_ld2, 16 * n)

                    def emit(j, k, p):
                        v.tensor_copy(rows[k][:], p[0:W, 0:D + H])
                        return v.tensor_copy(dwin[:, bass.ds(j, 1), 0:H].rearrange("p a b -> p (a b)"),
                                             p[0:W, D + H:RW])

                    project(f"p{l}_", z, RW,
                            [(wnat[:], t[f"W{l}"].rearrange("(c p) i -> p c i", p=128)),
                             (wts[:, :, 0:D], t[f"WT{l}"].rearrange("(c p) o -> p c o", p=128))], wts, emit,
                            norm=l == 0, dve_first=dve_first, pe_first=pe_first, rows=rows, row_dram=row_tab[l])
                with phase() as ph:
                    acc = sb(f"acc{l}", [W + 1, NV, RW], F32, ph)
                    edges(l, acc, 1.0)

                    def finish(c, part, l=l):
                        if l == 0:
                            vd(v.tensor_tensor(part[0][:], part[0][:], part[1][:], ALU.add))
                            v.tensor_scalar(z[:, c:c + 5, :], part[0][:], 0.0, None, ALU.max)
                        else:
                            vd(v.tensor_tensor(part[0][:], part[0][:], part[1][:], ALU.add))
                            v.tensor_tensor(xcur[:, c:c + 5, :], xcur[:, c:c + 5, :], part[0][:], ALU.add)

                    merge(l, acc, 1.0, finish)

        experts(0)

        DH = D // ATT[2]["H"]
        with phase() as ph:
            wq = sb("wq", [128, KC, 3 * D], F32, ph)
            bq = sb("bq", [W, 3 * D], F32, ph)
            rows = [sb(f"kv{k}", [W, 2 * D], F32, ph) for k in range(2)]

            def emit(j, k, p):
                v.tensor_tensor(z[:, bass.ds(j, 1), :].rearrange("p a b -> p (a b)"), p[0:W, 0:D], bq[:, 0:D], ALU.add)
                return v.tensor_tensor(rows[k][:], p[0:W, D:3 * D], bq[:, D:3 * D], ALU.add)

            project("pq_", z, 3 * D,
                    [(wq[:], t["Wqkv"].rearrange("(c p) o -> p c o", p=128)),
                     (bq[:], t["bqkv"].to_broadcast([W, 3 * D]))], wq, emit,
                    norm=True, rows=rows, row_dram=row_tab[2])
        with phase() as ph:
            RW = D + 2 * ATT[2]["H"]
            acc = sb("acc2x", [W + 1, NV, RW], F32, ph)
            edges(2, acc, float(DH) ** -0.5)

            def finish(c, part):
                for w in range(c, c + 5):
                    v.tensor_scalar(z[:, w, :], xcur[:, w, :], mean[:, w:w + 1], rstd[:, w:w + 1],
                                    ALU.subtract, ALU.mult)
                vd(v.tensor_tensor(part[0][:], part[0][:], part[1][:], ALU.add))
                for w in range(5):
                    zz = z[:, c + w, :].rearrange("p (d h) -> p h d", d=DH)
                    v.tensor_tensor(zz, zz, part[0][:, w, :].rearrange("p (h d) -> p h d", d=DH), ALU.add)

            merge(2, acc, float(DH) ** -0.5, finish)
        with phase() as ph:
            wo = sb("wo", [128, KC, D], F32, ph)
            bo = sb("bo", [W, D], F32, ph)

            def add_bias(dve, s_load, s_wts, _):
                dve.wait_ge(s_load, 32)
                v.tensor_tensor(xcur[:], xcur[:], bo[:].unsqueeze(1).to_broadcast([W, NV, D]), ALU.add)
                v.drain().then_inc(s_wts, 1)

            def emit(j, k, p):
                xw = xcur[:, bass.ds(j, 1), :].rearrange("p a b -> p (a b)")
                return v.tensor_tensor(xw, xw, p[0:W, 0:D], ALU.add)

            project("po_", z, D, [(wo[:], t["Wout"].rearrange("(c p) o -> p c o", p=128)),
                                  (bo[:], t["bout"].to_broadcast([W, D]))], wo, emit, dve_first=add_bias)
        experts(1)


def kernel(**inputs):
    import concourse.bacc as bacc
    from concourse.bass_utils import run_bass_kernel_spmd

    x = {k: np.asarray(val) for k, val in inputs.items()}
    src, dst = x["src"], x["dst"]
    edges = np.full((NT, 256), -1, dst.dtype)
    edges[:, 1:W + 1] = dst.reshape(NT, W)
    edges[1:, 0] = dst[W - 1:-1:W]
    edges[:-1, W + 1] = dst[W::W]
    edges[:, W + 2:2 * W + 2] = src.reshape(NT, W)

    def expert_pack(f, w1, b1, gain, offset):
        ne = FFN[f]["E"]
        parts = [w1.reshape(ne, KC, 128, -1).transpose(0, 2, 1, 3).reshape(ne, 128, -1),
                 b1.reshape(ne, -1, 128).transpose(0, 2, 1)]
        for col in (gain, offset):
            parts.append(np.zeros((ne, 128, KC), w1.dtype) if col is None
                         else col.reshape(ne, KC, 128).transpose(0, 2, 1))
        return np.ascontiguousarray(np.concatenate(parts, axis=2))

    def rows_of(w2):
        return w2.reshape(len(w2), -1, 128, D).transpose(0, 2, 1, 3).reshape(len(w2), 128, -1)

    arrays = {
        "x": x["x"], "edges": edges, "ends": np.stack([dst[0::W], dst[W - 1::W]]),
        "W0": x["L0_gnn_W1"], "WT0": x["L0_gnn_W1"].T, "W1": x["L0_gnn_W2"], "WT1": x["L0_gnn_W2"].T,
        "a0_src": x["L0_gnn_a1_src"].reshape(-1, 1), "a0_dst": x["L0_gnn_a1_dst"].reshape(-1, 1),
        "a1_src": x["L0_gnn_a2_src"].reshape(-1, 1), "a1_dst": x["L0_gnn_a2_dst"].reshape(-1, 1),
        "gate_w0": x["L0_ffn_gate_w"], "gate_b0": x["L0_ffn_gate_b"].reshape(1, -1),
        "gate_w1": x["L1_ffn_Wr"], "gate_b1": x["L1_ffn_br"].reshape(1, -1),
        "pack0": expert_pack(0, x["L0_ffn_w1"], x["L0_ffn_b1"], None, None),
        "pack1": expert_pack(1, x["L1_ffn_W1"], x["L1_ffn_b1"], x["L1_ffn_ln_g"], x["L1_ffn_ln_b"]),
        "w2_0": rows_of(x["L0_ffn_w2"]), "w2_1": rows_of(x["L1_ffn_W2"]),
        "b2_0": x["L0_ffn_b2"], "b2_1": x["L1_ffn_b2"],
        "gamma": x["L0_ffn_gamma"].reshape(1, -1), "beta": x["L0_ffn_beta"].reshape(1, -1),
        "Wqkv": x["L1_gnn_W_qkv"], "bqkv": x["L1_gnn_b_qkv"].reshape(1, -1),
        "Wout": x["L1_gnn_W_out"], "bout": x["L1_gnn_b_out"].reshape(1, -1),
    }
    nc = bacc.Bacc("TRN2", target_bir_lowering=False, num_devices=1)
    arrays = {k: np.ascontiguousarray(val) for k, val in arrays.items()}
    t = {k: nc.dram_tensor("in_" + k, val.shape, mybir.dt.from_np(val.dtype), kind="ExternalInput").ap()
         for k, val in arrays.items()}
    t["out"] = nc.dram_tensor("out_0", (N, D), F32, kind="ExternalOutput").ap()
    build(nc, t)
    r = run_bass_kernel_spmd(nc, [{"in_" + k: val for k, val in arrays.items()}], core_ids=[0])
    return r.results[0]["out_0"]
```
